# Optimizing a Trainium2 kernel written in Bass

```python
import numpy as np
import jax
import jax.numpy as jnp

def _softmax(x, axis=-1):
    return jax.nn.softmax(x, axis=axis)

def _gelu(x):
    return jax.nn.gelu(x, approximate=True)

def _silu(x):
    return jax.nn.silu(x)

def _sigmoid(x):
    return jax.nn.sigmoid(x)

def _layernorm(x, axis=-1, eps=1e-05):
    m = jnp.mean(x, axis=axis, keepdims=True)
    v = jnp.var(x, axis=axis, keepdims=True)
    return (x - m) / jnp.sqrt(v + eps)

def _scatter_add(tgt, idx, src, axis=0):
    return tgt.at[idx].add(src)

def _segment_sum(src, seg, n):
    return jax.ops.segment_sum(src, seg, n)
kernel_name = 'mk_flamingo_gated_d1_seqx_r8_94e512'

def setup_inputs(seed: int=0):
    np.random.seed(seed)
    _w = jnp.asarray

    def _rec_inputs():
        import jax
        import jax.numpy as jnp
        _rk = jax.random.key(seed)
        x = -0.0003929 + 0.9999 * jax.random.normal(jax.random.fold_in(_rk, 1), (16, 128, 128), jnp.float32)
        _lenS = 128 - jax.random.randint(jax.random.fold_in(_rk, 7), (16,), 0, max(1, 128 // 4) + 1, jnp.int32)
        _lenS2 = 120 - jax.random.randint(jax.random.fold_in(_rk, 8), (16,), 0, max(1, 120 // 4) + 1, jnp.int32)
        _ctx_768P = jax.random.normal(jax.random.fold_in(_rk, 11), (16, 16, 96), jnp.float32)
        _ctx_768c = jax.random.dirichlet(jax.random.fold_in(_rk, 511), 0.3 * jnp.ones((16,), jnp.float32), (16, 120))
        _ctx_768t = jnp.einsum('bsk,bkd->bsd', _ctx_768c, _ctx_768P)
        _ctx_768t = _ctx_768t * jax.lax.rsqrt(jnp.mean(jnp.square(_ctx_768t)) + 1e-12) * 0.953939
        ctx_768 = -7.36909e-05 + 0.999899 * (_ctx_768t + 0.3 * jax.random.normal(jax.random.fold_in(_rk, 611), (16, 120, 96), jnp.float32))
        _g = jax.random.normal(jax.random.fold_in(_rk, 9001), (2, 1), jnp.float32)
        _g = jnp.sign(_g) * jnp.maximum(jnp.abs(_g), 1.0) + (_g == 0) * 1.0
        g_xattn = _g[0]
        g_ffn = _g[1]
        return (x, ctx_768, g_xattn, g_ffn)
    x, ctx_768, g_xattn, g_ffn = _rec_inputs()

    def _L0_xattn_setup():
        import jax, jax.numpy as jnp
        import numpy as np
        EPS = 1e-05

        def layernorm(x, g, b):
            mu = jnp.mean(x, axis=-1, keepdims=True)
            var = jnp.mean(jnp.square(x - mu), axis=-1, keepdims=True)
            return (x - mu) * jax.lax.rsqrt(var + EPS) * g + b
        key = jax.random.key(seed)
        ks = jax.random.split(key, 12)
        B, L1, L2 = (8, 256, 256)
        D1, D2, E = (128, 96, 128)
        s1, s2, se = (D1 ** (-0.5), D2 ** (-0.5), E ** (-0.5))
        return {'modality1': jax.random.normal(ks[0], (B, L1, D1), jnp.float32), 'modality2': jax.random.normal(ks[1], (B, L2, D2), jnp.float32), 'ln1_g': jnp.ones((D1,), jnp.float32), 'ln1_b': jnp.zeros((D1,), jnp.float32), 'ln2_g': jnp.ones((D2,), jnp.float32), 'ln2_b': jnp.zeros((D2,), jnp.float32), 'Wq': jax.random.normal(ks[2], (D1, E), jnp.float32) * s1, 'bq': jax.random.normal(ks[3], (E,), jnp.float32) * 0.01, 'Wk': jax.random.normal(ks[4], (D2, E), jnp.float32) * s2, 'bk': jax.random.normal(ks[5], (E,), jnp.float32) * 0.01, 'Wv': jax.random.normal(ks[6], (D2, E), jnp.float32) * s2, 'bv': jax.random.normal(ks[7], (E,), jnp.float32) * 0.01, 'Wo': jax.random.normal(ks[8], (E, D1), jnp.float32) * se, 'bo': jax.random.normal(ks[9], (D1,), jnp.float32) * 0.01}
    _L0_xattn_all = _L0_xattn_setup()
    _L0_xattn_in = {k: v for k, v in _L0_xattn_all.items() if k in ('ln1_g', 'ln1_b', 'ln2_g', 'ln2_b', 'Wq', 'bq', 'Wk', 'bk', 'Wv', 'bv', 'Wo', 'bo')}
    del _L0_xattn_all

    def _L0_ffn_setup():
        import jax, jax.numpy as jnp
        import numpy as np
        DIM = 128
        DEPTH = 2
        HEADS = 8
        DIM_HEAD = 64
        WINDOW = 64
        INNER = HEADS * DIM_HEAD
        HID = int(DIM * 4 * 2 / 3)
        B, N = (2, 1024)
        QK_SCALE = 8.0

        def shift_token(t):
            t1, t2 = jnp.split(t, 2, axis=-1)
            t2 = jnp.pad(t2, ((0, 0), (1, 0), (0, 0)))[:, :-1]
            return jnp.concatenate([t1, t2], axis=-1)

        def l2norm(t):
            return t / jnp.clip(jnp.linalg.norm(t, axis=-1, keepdims=True), 1e-12)

        def rotate_half(x):
            x1, x2 = jnp.split(x, 2, axis=-1)
            return jnp.concatenate([-x2, x1], axis=-1)

        def rotary_xpos(q, k):
            n = q.shape[-2]
            half_idx = jnp.arange(0, DIM_HEAD, 2, dtype=jnp.float32)
            inv_freq = 1.0 / 10000.0 ** (half_idx / DIM_HEAD)
            t = jnp.arange(n, dtype=jnp.float32)
            freqs = t[:, None] * inv_freq[None, :]
            freqs = jnp.concatenate([freqs, freqs], axis=-1)
            base = (half_idx + 0.4 * DIM_HEAD) / (1.4 * DIM_HEAD)
            power = (t - n // 2) / float(WINDOW // 2)
            scale = base[None, :] ** power[:, None]
            scale = jnp.concatenate([scale, scale], axis=-1)
            cos, sin = (jnp.cos(freqs), jnp.sin(freqs))
            q = q * cos * scale + rotate_half(q) * sin * scale
            k = k * cos / scale + rotate_half(k) * sin / scale
            return (q, k)

        def local_attention(q, k, v):
            b, h, n, d = q.shape
            w = n // WINDOW
            bq = q.reshape(b, h, w, WINDOW, d) * QK_SCALE
            bk = k.reshape(b, h, w, WINDOW, d)
            bv = v.reshape(b, h, w, WINDOW, d)

            def look_around(t):
                p = jnp.pad(t, ((0, 0), (0, 0), (1, 0), (0, 0), (0, 0)))
                return jnp.concatenate([p[:, :, :w], p[:, :, 1:]], axis=3)
            bk, bv = (look_around(bk), look_around(bv))
            bt = jnp.arange(n).reshape(w, WINDOW)
            btp = jnp.pad(bt, ((1, 0), (0, 0)), constant_values=-1)
            btk = jnp.concatenate([btp[:w], btp[1:]], axis=1)
            sim = jnp.einsum('bhwid,bhwjd->bhwij', bq, bk)
            i = bt[:, :, None]
            j = btk[:, None, :]
            mask = (i < j) | (i > j + WINDOW) | (j == -1)
            sim = jnp.where(mask, -jnp.finfo(sim.dtype).max, sim)
            attn = jax.nn.softmax(sim, axis=-1)
            out = jnp.einsum('bhwij,bhwjd->bhwid', attn, bv)
            return out.reshape(b, h, n, d)

        def _layer(x, wqkv, qs, ksc, wo, lg, lb, w1, b1, w2, b2):
            b, n, _ = x.shape
            h = shift_token(x)
            qkv = h @ wqkv
            q, k, v = jnp.split(qkv, 3, axis=-1)
            to_heads = lambda t: t.reshape(b, n, HEADS, DIM_HEAD).transpose(0, 2, 1, 3)
            q, k, v = (to_heads(q), to_heads(k), to_heads(v))
            q = l2norm(q) * qs
            k = l2norm(k) * ksc
            q, k = rotary_xpos(q, k)
            o = local_attention(q, k, v)
            o = o.transpose(0, 2, 1, 3).reshape(b, n, INNER)
            x = x + o @ wo
            h = shift_token(x)
            mu = h.mean(-1, keepdims=True)
            var = h.var(-1, keepdims=True)
            h = (h - mu) / jnp.sqrt(var + 1e-05) * lg + lb
            h = h @ w1 + b1
            a, g = jnp.split(h, 2, axis=-1)
            h = a * jax.nn.gelu(g, approximate=False)
            x = x + h @ w2 + b2
            return x
        key = jax.random.key(seed)
        ks = jax.random.split(key, 6)
        return {'x': jax.random.normal(ks[0], (B, N, DIM), jnp.float32), 'wqkv': jax.random.normal(ks[1], (DEPTH, DIM, 3 * INNER), jnp.float32) * 0.02, 'q_scale': jnp.ones((DEPTH, DIM_HEAD), jnp.float32), 'k_scale': jnp.ones((DEPTH, DIM_HEAD), jnp.float32), 'wo': jax.random.normal(ks[2], (DEPTH, INNER, DIM), jnp.float32) * 0.02, 'ln_g': jnp.ones((DEPTH, DIM), jnp.float32), 'ln_b': jnp.zeros((DEPTH, DIM), jnp.float32), 'w1': jax.random.normal(ks[3], (DEPTH, DIM, 2 * HID), jnp.float32) * 0.02, 'b1': jnp.zeros((DEPTH, 2 * HID), jnp.float32), 'w2': jax.random.normal(ks[4], (DEPTH, HID, DIM), jnp.float32) * 0.02, 'b2': jnp.zeros((DEPTH, DIM), jnp.float32)}
    _L0_ffn_all = _L0_ffn_setup()
    _L0_ffn_in = {k: v for k, v in _L0_ffn_all.items() if k in ('wqkv', 'q_scale', 'k_scale', 'wo', 'ln_g', 'ln_b', 'w1', 'b1', 'w2', 'b2')}
    del _L0_ffn_all
    return {'x': x, 'ctx_768': ctx_768, 'g_xattn': g_xattn, 'g_ffn': g_ffn, 'L0_xattn_ln1_g': _L0_xattn_in['ln1_g'], 'L0_xattn_ln1_b': _L0_xattn_in['ln1_b'], 'L0_xattn_ln2_g': _L0_xattn_in['ln2_g'], 'L0_xattn_ln2_b': _L0_xattn_in['ln2_b'], 'L0_xattn_Wq': _L0_xattn_in['Wq'], 'L0_xattn_bq': _L0_xattn_in['bq'], 'L0_xattn_Wk': _L0_xattn_in['Wk'], 'L0_xattn_bk': _L0_xattn_in['bk'], 'L0_xattn_Wv': _L0_xattn_in['Wv'], 'L0_xattn_bv': _L0_xattn_in['bv'], 'L0_xattn_Wo': _L0_xattn_in['Wo'], 'L0_xattn_bo': _L0_xattn_in['bo'], 'L0_ffn_wqkv': _L0_ffn_in['wqkv'], 'L0_ffn_q_scale': _L0_ffn_in['q_scale'], 'L0_ffn_k_scale': _L0_ffn_in['k_scale'], 'L0_ffn_wo': _L0_ffn_in['wo'], 'L0_ffn_ln_g': _L0_ffn_in['ln_g'], 'L0_ffn_ln_b': _L0_ffn_in['ln_b'], 'L0_ffn_w1': _L0_ffn_in['w1'], 'L0_ffn_b1': _L0_ffn_in['b1'], 'L0_ffn_w2': _L0_ffn_in['w2'], 'L0_ffn_b2': _L0_ffn_in['b2']}

def reference(x, ctx_768, g_xattn, g_ffn, L0_xattn_ln1_g, L0_xattn_ln1_b, L0_xattn_ln2_g, L0_xattn_ln2_b, L0_xattn_Wq, L0_xattn_bq, L0_xattn_Wk, L0_xattn_bk, L0_xattn_Wv, L0_xattn_bv, L0_xattn_Wo, L0_xattn_bo, L0_ffn_wqkv, L0_ffn_q_scale, L0_ffn_k_scale, L0_ffn_wo, L0_ffn_ln_g, L0_ffn_ln_b, L0_ffn_w1, L0_ffn_b1, L0_ffn_w2, L0_ffn_b2):
    import jax
    import jax.numpy as jnp

    def _L0_xattn_ref(modality1, modality2, ln1_g, ln1_b, ln2_g, ln2_b, Wq, bq, Wk, bk, Wv, bv, Wo, bo):
        import jax, jax.numpy as jnp
        import numpy as np
        EPS = 1e-05

        def layernorm(x, g, b):
            mu = jnp.mean(x, axis=-1, keepdims=True)
            var = jnp.mean(jnp.square(x - mu), axis=-1, keepdims=True)
            return (x - mu) * jax.lax.rsqrt(var + EPS) * g + b
        E = Wq.shape[1]
        scaling = E ** (-0.5)
        x1 = layernorm(modality1, ln1_g, ln1_b)
        x2 = layernorm(modality2, ln2_g, ln2_b)
        q = x1 @ Wq + bq
        k = x2 @ Wk + bk
        v = x2 @ Wv + bv
        scores = jnp.einsum('bqe,bke->bqk', q, k) * scaling
        attn = jax.nn.softmax(scores, axis=-1)
        ctx = jnp.einsum('bqk,bke->bqe', attn, v)
        return ctx @ Wo + bo

    def _L0_ffn_ref(x, wqkv, q_scale, k_scale, wo, ln_g, ln_b, w1, b1, w2, b2):
        import jax, jax.numpy as jnp
        import numpy as np
        DIM = 128
        DEPTH = 2
        HEADS = 8
        DIM_HEAD = 64
        WINDOW = 64
        INNER = HEADS * DIM_HEAD
        HID = int(DIM * 4 * 2 / 3)
        B, N = (2, 1024)
        QK_SCALE = 8.0

        def shift_token(t):
            t1, t2 = jnp.split(t, 2, axis=-1)
            t2 = jnp.pad(t2, ((0, 0), (1, 0), (0, 0)))[:, :-1]
            return jnp.concatenate([t1, t2], axis=-1)

        def l2norm(t):
            return t / jnp.clip(jnp.linalg.norm(t, axis=-1, keepdims=True), 1e-12)

        def rotate_half(x):
            x1, x2 = jnp.split(x, 2, axis=-1)
            return jnp.concatenate([-x2, x1], axis=-1)

        def rotary_xpos(q, k):
            n = q.shape[-2]
            half_idx = jnp.arange(0, DIM_HEAD, 2, dtype=jnp.float32)
            inv_freq = 1.0 / 10000.0 ** (half_idx / DIM_HEAD)
            t = jnp.arange(n, dtype=jnp.float32)
            freqs = t[:, None] * inv_freq[None, :]
            freqs = jnp.concatenate([freqs, freqs], axis=-1)
            base = (half_idx + 0.4 * DIM_HEAD) / (1.4 * DIM_HEAD)
            power = (t - n // 2) / float(WINDOW // 2)
            scale = base[None, :] ** power[:, None]
            scale = jnp.concatenate([scale, scale], axis=-1)
            cos, sin = (jnp.cos(freqs), jnp.sin(freqs))
            q = q * cos * scale + rotate_half(q) * sin * scale
            k = k * cos / scale + rotate_half(k) * sin / scale
            return (q, k)

        def local_attention(q, k, v):
            b, h, n, d = q.shape
            w = n // WINDOW
            bq = q.reshape(b, h, w, WINDOW, d) * QK_SCALE
            bk = k.reshape(b, h, w, WINDOW, d)
            bv = v.reshape(b, h, w, WINDOW, d)

            def look_around(t):
                p = jnp.pad(t, ((0, 0), (0, 0), (1, 0), (0, 0), (0, 0)))
                return jnp.concatenate([p[:, :, :w], p[:, :, 1:]], axis=3)
            bk, bv = (look_around(bk), look_around(bv))
            bt = jnp.arange(n).reshape(w, WINDOW)
            btp = jnp.pad(bt, ((1, 0), (0, 0)), constant_values=-1)
            btk = jnp.concatenate([btp[:w], btp[1:]], axis=1)
            sim = jnp.einsum('bhwid,bhwjd->bhwij', bq, bk)
            i = bt[:, :, None]
            j = btk[:, None, :]
            mask = (i < j) | (i > j + WINDOW) | (j == -1)
            sim = jnp.where(mask, -jnp.finfo(sim.dtype).max, sim)
            attn = jax.nn.softmax(sim, axis=-1)
            out = jnp.einsum('bhwij,bhwjd->bhwid', attn, bv)
            return out.reshape(b, h, n, d)

        def _layer(x, wqkv, qs, ksc, wo, lg, lb, w1, b1, w2, b2):
            b, n, _ = x.shape
            h = shift_token(x)
            qkv = h @ wqkv
            q, k, v = jnp.split(qkv, 3, axis=-1)
            to_heads = lambda t: t.reshape(b, n, HEADS, DIM_HEAD).transpose(0, 2, 1, 3)
            q, k, v = (to_heads(q), to_heads(k), to_heads(v))
            q = l2norm(q) * qs
            k = l2norm(k) * ksc
            q, k = rotary_xpos(q, k)
            o = local_attention(q, k, v)
            o = o.transpose(0, 2, 1, 3).reshape(b, n, INNER)
            x = x + o @ wo
            h = shift_token(x)
            mu = h.mean(-1, keepdims=True)
            var = h.var(-1, keepdims=True)
            h = (h - mu) / jnp.sqrt(var + 1e-05) * lg + lb
            h = h @ w1 + b1
            a, g = jnp.split(h, 2, axis=-1)
            h = a * jax.nn.gelu(g, approximate=False)
            x = x + h @ w2 + b2
            return x
        for l in range(DEPTH):
            x = _layer(x, wqkv[l], q_scale[l], k_scale[l], wo[l], ln_g[l], ln_b[l], w1[l], b1[l], w2[l], b2[l])
        return x
    x = x + jnp.tanh(g_xattn[0]) * _L0_xattn_ref(_layernorm(x, axis=-1), ctx_768, L0_xattn_ln1_g, L0_xattn_ln1_b, L0_xattn_ln2_g, L0_xattn_ln2_b, L0_xattn_Wq, L0_xattn_bq, L0_xattn_Wk, L0_xattn_bk, L0_xattn_Wv, L0_xattn_bv, L0_xattn_Wo, L0_xattn_bo)
    x = x + jnp.tanh(g_ffn[0]) * _L0_ffn_ref(_layernorm(x, axis=-1), L0_ffn_wqkv, L0_ffn_q_scale, L0_ffn_k_scale, L0_ffn_wo, L0_ffn_ln_g, L0_ffn_ln_b, L0_ffn_w1, L0_ffn_b1, L0_ffn_w2, L0_ffn_b2)
    return x

_drawn_inputs = setup_inputs


def setup_inputs(seed=0):
    import zlib

    import numpy as np

    out = dict(_drawn_inputs(seed))
    spreads = {'L0_xattn_ln1_g': (1.0, 0.2),
     'L0_xattn_ln1_b': (0.0, 0.505),
     'L0_xattn_ln2_g': (1.0, 0.2),
     'L0_xattn_ln2_b': (0.0, 0.1),
     'L0_ffn_q_scale': (1.0, 0.6),
     'L0_ffn_k_scale': (1.0, 0.6),
     'L0_ffn_ln_g': (1.0, 0.6),
     'L0_ffn_ln_b': (0.0, 0.8),
     'L0_ffn_b1': (0.0, 0.1),
     'L0_ffn_b2': (0.0, 0.1)}
    factors = {'L0_xattn_bq': 36.395, 'L0_xattn_bk': 64.0, 'L0_xattn_bv': 7.793, 'L0_xattn_bo': 7.612}
    for name, (base, spread) in spreads.items():
        noise = np.random.default_rng([zlib.crc32(name.encode()), seed]).standard_normal(out[name].shape)
        drawn = base * np.exp(spread * noise) if base else spread * noise
        out[name] = jnp.asarray(drawn.astype(out[name].dtype))
    for name, factor in factors.items():
        out[name] = (out[name] * factor).astype(out[name].dtype)
    return out
```

```python
from contextlib import ExitStack

import numpy as np

import concourse.bass as bass
from concourse import mybir

F32 = mybir.dt.float32
F32R = mybir.dt.float32r
ALU = mybir.AluOpType
ACT = mybir.ActivationFunctionType
AX = mybir.AxisListType

B, N, D = 16, 128, 128
NC, DC = 120, 96
HEADS, DH, W = 8, 64, 64
INNER = HEADS * DH
PAIRS = HEADS // 2
DEPTH = 2
HID = int(D * 4 * 2 / 3)
CH = [(0, 128), (128, 128), (256, HID - 256)]
GB = 4
NG = B // GB
EPS = 1e-5
NEG = -1e30
LN_SCALE = 2.0 ** 16
LN_BACK = 8.0 * float(np.log(2.0))


def tables():
    half = np.arange(0, DH, 2, dtype=np.float32)
    inv = (np.float32(1.0) / np.power(np.float32(10000.0), half / np.float32(DH))).astype(np.float32)
    t = np.arange(N, dtype=np.float32)
    fr = (t[:, None] * inv[None, :]).astype(np.float32)
    fr = np.concatenate([fr, fr], -1)
    base = ((half + np.float32(0.4 * DH)) / np.float32(1.4 * DH)).astype(np.float32)
    power = ((t - N // 2) / np.float32(W // 2)).astype(np.float32)
    sc = np.power(base[None, :].astype(np.float64), power[:, None])
    sc = np.concatenate([sc, sc], -1)
    cos, sin = np.cos(fr.astype(np.float64)), np.sin(fr.astype(np.float64))
    sgn = np.concatenate([-np.ones(DH // 2), np.ones(DH // 2)])[None, :]
    cq, sq = cos * sc * 8.0, sin * sc * 8.0 * sgn
    ck, sk = cos / sc, sin / sc * sgn
    rot = np.stack([cq, ck, sq, sk], 1).astype(np.float32)
    i = np.arange(128)[:, None] % W
    j = np.arange(N)[None, :]
    m1 = np.where((j >= i) & (j <= i + W), 0.0, NEG)
    m0 = np.where(j[:, :W] <= i, 0.0, NEG)
    mask = np.concatenate([m1, m0], 1).astype(np.float32)
    return rot, mask, np.eye(128, dtype=np.float32)


def build(nc, x, ctx_768, g_xattn, g_ffn, ln1_g, ln1_b, ln2_g, ln2_b, Wq, bq, Wk, bk, Wv, bv, Wo, bo,
          wqkv, q_scale, k_scale, wo, ln_g, ln_b, w1, b1, w2, b2, rot, mask, ident, out):
    ctx = ExitStack()
    with ctx:
        def sb(name, shape, dt=F32):
            return ctx.enter_context(nc.sbuf_tensor(name, shape, dt))

        def sem(name):
            return ctx.enter_context(nc.semaphore(name))

        def sem2(name):
            return [sem(name + "0"), sem(name + "1")]

        def sb2(name, shape, dt=F32):
            return [sb(name + "0", shape, dt), sb(name + "1", shape, dt)]

        shared = sb("shared", [128, 6 * 2 * INNER])

        class Carve:
            def __init__(self):
                self.at = 0

            def __call__(self, parts, *shape):
                size = int(np.prod(shape))
                v = shared[0:parts, self.at:self.at + size]
                self.at += size
                assert self.at <= 6 * 2 * INNER
                return v.rearrange("p (a b) -> p a b", a=shape[0]) if len(shape) == 2 else v

        idn = sb("idn", [128, 128])
        msk = sb("msk", [128, 192])
        rott = sb("rott", [128, 4, DH])
        ones = sb("ones", [128, 128])
        epst = sb("epst", [128, 1])
        mark_v, mark_g = sb("mark_v", [128, 8]), sb("mark_g", [128, 1])
        backt = sb("backt", [128, 1])
        wq_s, wo_s = sb("wq_s", [D, D]), sb("wo_s", [D, D])
        wk_s, wv_s = sb("wk_s", [DC, D]), sb("wv_s", [DC, D])
        cols = sb("cols", [128, 8])
        bvb, bob = sb("bvb", [128, D]), sb("bob", [128, D])
        gates = sb("gates", [128, 2])
        tg = sb("tg", [128, 2])
        wqkv_raw = sb("wqkv_raw", [D, DEPTH, 3 * INNER])
        wqkv_hi = sb("wqkv_hi", [D, DEPTH * 3 * INNER], F32R)
        wqkv_lo = sb("wqkv_lo", [D, DEPTH * 3 * INNER], F32R)
        wo_raw = sb("wo_raw", [128, DEPTH, PAIRS, D])
        w1_raw = sb("w1_raw", [D, DEPTH, 2 * HID])
        w2_raw = sb("w2_raw", [128, DEPTH, 3, D])
        lgb = sb("lgb", [128, 3, DEPTH])
        b1_raw = sb("b1_raw", [128, DEPTH, 6])
        b1_all = sb("b1_all", [128, DEPTH, 6])
        qks = sb("qks", [128, DEPTH, 2, DH])
        ctab = sb("ctab", [128, DEPTH, 2, DH])
        stab = sb("stab", [128, DEPTH, 2, DH])
        wo_l = sb("wo_l", [128, PAIRS, D])
        w1g = sb("w1g", [D, 2 * HID])
        w1_hi, w1_lo = sb("w1_hi", [D, 2 * HID], F32R), sb("w1_lo", [D, 2 * HID], F32R)
        w2_hi, w2_lo = sb("w2_hi", [128, 3, D], F32R), sb("w2_lo", [128, 3, D], F32R)
        b1_l, b2_l = sb("b1_l", [128, 6]), sb("b2_l", [128, 1])

        xt = sb("xt", [N, B, D])
        ct = sb("ct", [NC, B, DC])
        xs = sb("xs", [D, B, N + 1])
        hn_hi = sb("hn_hi", [D, B, N], F32R)
        hn_lo = sb("hn_lo", [D, B, N], F32R)

        bst = sb("bst", [128, GB, 6])
        cst = sb("cst", [128, GB, 6])
        mv, cmv = sb("mv", [128, GB, 2]), sb("cmv", [128, GB, 2])
        r1, r2, rc, tmp4 = (sb(n, [128, GB]) for n in ("r1", "r2", "rc", "tmp4"))
        lnv, lnc = sb("lnv", [128, GB]), sb("lnc", [128, GB])
        cut = Carve()
        zx, zc = cut(N, GB, D), cut(NC, GB, DC)
        x1T, c1T = cut(D, GB * N), cut(DC, GB, NC)
        xqT, xkT, xv = cut(D, GB, N), cut(D, GB, NC), cut(NC, GB, D)
        xp, xpT, xcT = cut(N, GB, NC), cut(NC, GB, N), cut(D, GB, N)
        nmx = sb("nmx", [128, GB])
        nmb = sb("nmb", [128, GB])
        xsum = sb("xsum", [128, GB])
        xri = sb("xri", [128, GB])
        xrt = sb("xrt", [128, GB])

        h_hi, h_lo = sb2("h_hi", [D, N], F32R), sb2("h_lo", [D, N], F32R)
        sqr = sb2("sqr", [N, 2 * INNER])
        ss, ssc, lns, rr = (sb2(n, [N, 2 * HEADS]) for n in ("ss", "ssc", "lns", "rr"))
        cut = Carve()
        qn, rc1, rs1 = ([cut(N, 2 * INNER) for _ in range(2)] for _ in range(3))
        qr = rs1
        qT, kT = sb2("qT", [128, PAIRS, N]), sb2("kT", [128, PAIRS, N])
        vv = sb2("vv", [N, INNER])
        sm1, sm0 = sb2("sm1", [128, PAIRS, 128]), sb2("sm0", [128, PAIRS, W])
        nm = sb2("nm", [128, 8])
        p1, p0 = sb2("p1", [128, PAIRS, 128]), sb2("p0", [128, PAIRS, W])
        psum_ = sb2("psum_", [128, 8])
        pri = sb2("pri", [128, 8])
        pT1, pT0 = sb2("pT1", [128, PAIRS, 128]), sb2("pT0", [W, 2, 2, 128])
        oT = sb2("oT", [128, PAIRS, N])
        dd, dsq, lnl, rstd, hnf = (sb2(n, [D, N]) for n in ("dd", "dsq", "lnl", "rstd", "hnf"))

        cut = Carve()
        gl, uu = cut(128, 3, 512), cut(128, 3, 512)
        u_hi, u_lo = sb("u_hi", [128, 3, 512], F32R), sb("u_lo", [128, 3, 512], F32R)
        cut = Carve()
        stg = [cut(D, GB, N) for _ in range(2)]
        ot = [cut(N, GB, D) for _ in range(2)]

        ps = ctx.enter_context(nc.psum_tensor("ps", [128, 8, 512], F32))
        QB, KB, VB, TQ, TK, S1, S0, OB = range(8)

        block = ctx.enter_context(nc.Block())

        ld_x, ld_c, ld_w, ld_small, ld_st, ld_stg, ld_b, ld_bg = (
            sem(n) for n in ("ld_x", "ld_c", "ld_w", "ld_small", "ld_st", "ld_stg", "ld_b", "ld_bg"))
        cst_v = sem("cst_v")
        cst_g = sem("cst_g")
        tanh_done = sem("tanh_done")
        tab_done = sem("tab_done")
        wsplit = sem("wsplit")
        b1_ps, b1_done = sem("b1_ps"), sem("b1_done")
        xbias = sem("xbias")
        xchain = sem("xchain")
        xln, xlnr = sem("xln"), sem("xlnr")
        x_z, x_zT, x_1T = sem("x_z"), sem("x_zT"), sem("x_1T")
        x_qk_ps, x_v_ps, x_q, x_k, x_v = (sem(n) for n in ("x_qk_ps", "x_v_ps", "x_q", "x_k", "x_v"))
        x_s, x_nm, x_p, x_pT_ps, x_pT, x_c_ps, x_c, x_y_ps, x_a = (
            sem(n) for n in ("x_s", "x_nm", "x_p", "x_pT_ps", "x_pT", "x_c_ps", "x_c", "x_y_ps", "x_a"))
        x_v2, x_l2, x_z2, x_T2, x_out = (sem(n) for n in ("x_v2", "x_l2", "x_z2", "x_T2", "x_out"))
        layer_w = sem("layer_w")
        h_ready, q_ps, k_ps, v_ps = (sem2(n) for n in ("h_ready", "q_ps", "k_ps", "v_ps"))
        h_hi_ok = sem2("h_hi_ok")
        sq_done, ss_sum, ss_ready, ln_done, r_ready = (sem2(n) for n in ("sq_done", "ss_sum", "ss_ready", "ln_done", "r_ready"))
        qn_ready, v_ready, c_ready, s_ready, rot_ready = (sem2(n) for n in ("qn_ready", "v_ready", "c_ready", "s_ready", "rot_ready"))
        tq_ps, tk_ps, qT_ready, kT_ready = (sem2(n) for n in ("tq_ps", "tk_ps", "qT_ready", "kT_ready"))
        s1_ps, s0_ps, sm_ready, p1_done, p0_done = (sem2(n) for n in ("s1_ps", "s0_ps", "sm_ready", "p1_done", "p0_done"))
        ri_ready, pn_ready, pt1_ps, pt0_ps, pt_ready = (sem2(n) for n in ("ri_ready", "pn_ready", "pt1_ps", "pt0_ps", "pt_ready"))
        o_ps, oT_ready, y_ps, x_upd = (sem2(n) for n in ("o_ps", "oT_ready", "y_ps", "x_upd"))
        m_ps, d_ready, d2_ready, var_ps, lnl_done, rstd_ready, hnf_ready, hh_ready, hn_ready = (
            sem2(n) for n in ("m_ps", "d_ready", "d2_ready", "var_ps", "lnl_done", "rstd_ready", "hnf_ready", "hh_ready", "hn_ready"))
        g_ps, gl_ready, u_ready, uh_ready, ul_ready, f_acc = (
            [sem(f"{n}{c}") for c in range(3)] for n in ("g_ps", "gl_ready", "u_ready", "uh_ready", "ul_ready", "f_acc"))
        f_ps, f_upd = sem("f_ps"), sem("f_upd")
        st_ready, st_T, ot_ready, stored = (sem2(n) for n in ("st_ready", "st_T", "ot_ready", "stored"))

        class Batch:

            def __init__(self, layer, pair, n):
                self.layer = layer
                self.j = n % 2
                self.g = layer * (B // 2) + pair + n // 2
                self.b = (pair + n // 2) * 2 + self.j

        def pipeline(eng, layer, step):
            def alone(n):
                step(lambda d: Batch(layer, 0, n + d), lambda d: 0 <= n + d < B)

            for n in range(-3, 1):
                alone(n)
            with eng.Fori(0, (B - 4) // 2) as pair:
                for n in (1, 2):
                    step(lambda d, n=n: Batch(layer, pair, n + d), lambda d: True)
            for n in range(B - 3, B + 1):
                alone(n)

        def apart(carrier, s, value, k):
            if carrier is nc.gpsimd:
                carrier.wait_ge(s, value)
                carrier.tensor_tensor(mark_g[:], ones[:, 0:1], ones[:, 1:2], ALU.mult)
            else:
                carrier.wait_ge(s, value)
                carrier.memset(mark_v[:, k:k + 1], 0.0)

        def h_of(b):
            return xs[:, bass.ds(b, 1), 0:N].rearrange("p o n -> p (o n)")

        def halves(t, b, nb):
            return t[0:64, bass.ds(b, nb), 0:N], t[64:128, bass.ds(b, nb), 1:N + 1]

        @block.sync
        def _(sp):
            for g in range(NG):
                sp.dma_start(xt[:, g * GB:(g + 1) * GB, :],
                             x[g * GB:(g + 1) * GB].rearrange("b n d -> n b d")).then_inc(ld_x, 16)
            sp.dma_start(idn[:], ident).then_inc(ld_st, 16)
            sp.dma_start(wq_s[:], Wq).then_inc(ld_st, 16)
            sp.dma_start(wo_s[:], Wo).then_inc(ld_st, 16)
            sp.dma_start(wqkv_raw[:], wqkv.rearrange("l d n -> d l n")).then_inc(ld_w, 16)
            sp.dma_start(wo_raw[:], wo.rearrange("l (c p) n -> p l c n", p=128)).then_inc(ld_w, 16)
            sp.dma_start(w1_raw[:], w1.rearrange("l d n -> d l n")).then_inc(ld_w, 16)
            for c, (o, m) in enumerate(CH):
                sp.dma_start(w2_raw[0:m, :, c, :], w2[:, o:o + m, :].rearrange("l p n -> p l n")).then_inc(ld_w, 16)
            for g in range(NG):
                j = g % 2
                sp.wait_ge(ot_ready[j], g // 2 + 1)
                sp.dma_start(out[g * GB:(g + 1) * GB].rearrange("b n d -> n b d"), ot[j][:]).then_inc(stored[j], 16)
            sp.wait_ge(stored[0], 16 * (NG // 2))
            sp.wait_ge(stored[1], 16 * (NG // 2))

        @block.gpsimd
        def _(pool):
            pool.dma_start(ct[:], ctx_768.rearrange("b n d -> n b d")).then_inc(ld_c, 16)
            pool.dma_start(wk_s[:], Wk).then_inc(ld_stg, 16)
            pool.dma_start(wv_s[:], Wv).then_inc(ld_stg, 16)
            pool.dma_start(bvb[:], bv.rearrange("(o d) -> o d", o=1).partition_broadcast(128)).then_inc(ld_bg, 16)
            pool.dma_start(bob[:], bo.rearrange("(o d) -> o d", o=1).partition_broadcast(128)).then_inc(ld_bg, 16)
            pool.dma_start(rott[:], rot).then_inc(ld_small, 16)
            pool.dma_start(msk[:], mask).then_inc(ld_small, 16)
            pool.dma_start(qks[:, :, 0, :], q_scale.partition_broadcast(128)).then_inc(ld_small, 16)
            pool.dma_start(qks[:, :, 1, :], k_scale.partition_broadcast(128)).then_inc(ld_small, 16)
            for l in range(DEPTH):
                for s in range(2):
                    for c, (o, m) in enumerate(CH):
                        pool.dma_start(b1_raw[0:m, l, s * 3 + c:s * 3 + c + 1],
                                       b1[l:l + 1, s * HID + o:s * HID + o + m].rearrange("o p -> p o")).then_inc(ld_small, 16)
            pool.wait_ge(cst_v, 4)

            pool.wait_ge(xbias, 1)
            for g in range(NG):
                pool.wait_ge(x_z, 2 * GB * g + GB)
                xg = xt[:, g * GB:(g + 1) * GB, :]
                nc.gpsimd.tensor_tensor(xg, xg, bob[:].unsqueeze(1).to_broadcast([128, GB, D]), ALU.add).then_inc(cst_g, 1)

            def step(at, on):
                if on(1):
                    m = at(1)
                    j = m.j
                    pool.wait_ge(ri_ready[j], m.g + 1)
                    nc.gpsimd.tensor_tensor(p1[j][:], p1[j][:], pri[j][:, 0:4].unsqueeze(2).to_broadcast([128, PAIRS, 128]),
                                            ALU.mult).then_inc(pn_ready[j], 1)
                    nc.gpsimd.tensor_tensor(p0[j][:], p0[j][:], pri[j][:, 4:8].unsqueeze(2).to_broadcast([128, PAIRS, W]),
                                            ALU.mult).then_inc(pn_ready[j], 1)
                if on(3):
                    m = at(3)
                    j, q4 = m.j, qn[m.j][:].rearrange("p (s h u d) -> p s h u d", s=2, h=HEADS, u=2)
                    s4 = rs1[j][:].rearrange("p (s h u d) -> p s h u d", s=2, h=HEADS, u=2)
                    apart(nc.gpsimd, qn_ready[j], m.g + 1, 0)
                    for s in range(2):
                        for u in range(2):
                            tb = stab[:, bass.ds(m.layer, 1), s, u * 32:u * 32 + 32].to_broadcast([128, HEADS, 32])
                            nc.gpsimd.tensor_tensor(s4[:, s, :, u, :], q4[:, s, :, 1 - u, :], tb, ALU.mult).then_inc(s_ready[j], 1)
                    pool.wait_ge(c_ready[j], 2 * m.g + 2)
                    pool.wait_ge(s_ready[j], 4 * m.g + 4)
                    nc.gpsimd.tensor_tensor(qr[j][:], rc1[j][:], rs1[j][:], ALU.add).then_inc(rot_ready[j], 1)

            with pool.Fori(0, DEPTH) as layer:
                pipeline(pool, layer, step)

        @block.tensor
        def _(pe):
            mm, tr = nc.tensor.matmul, nc.tensor.transpose

            pe.wait_ge(ld_stg, 16 * 2)
            pe.wait_ge(ld_st, 16 * 3)
            with pe.Fori(0, NG) as g:
                pe.wait_ge(x_z, 2 * GB * g + 2 * GB)
                if True:
                    for i in range(GB):
                        last = tr(ps[:, 0, i * 128:i * 128 + 128], zx[:, i, :], idn[:])
                    last.then_inc(x_zT, 1)
                    for i in range(GB):
                        last = tr(ps[0:DC, 1, i * NC:(i + 1) * NC], zc[:, i, :], idn[0:NC, 0:NC])
                    last.then_inc(x_zT, 1)
                pe.wait_ge(x_1T, 2 * g + 1)
                mm(ps[:, 2, :], wq_s[:], x1T[:], start=True, stop=True).then_inc(x_qk_ps, 1)
                pe.wait_ge(x_1T, 2 * g + 2)
                mm(ps[:, 3, 0:GB * NC], wk_s[:], c1T[:].rearrange("p b n -> p (b n)"), start=True, stop=True).then_inc(x_qk_ps, 1)
                for i in range(GB):
                    last = mm(ps[0:NC, 4, i * D:(i + 1) * D], c1T[:, i, :], wv_s[:], start=True, stop=True)
                last.then_inc(x_v_ps, 1)
                pe.wait_ge(x_q, g + 1)
                pe.wait_ge(x_k, g + 1)
                for i in range(GB):
                    last = mm(ps[:, 5, i * NC:(i + 1) * NC], xqT[:, i, :], xkT[:, i, :], start=True, stop=True)
                last.then_inc(x_s, 1)
                pe.wait_ge(x_p, GB * g + GB)
                for i in range(GB):
                    last = tr(ps[0:NC, 6, i * N:(i + 1) * N], xp[:, i, :], idn[:])
                last.then_inc(x_pT_ps, 1)
                pe.wait_ge(x_pT, g + 1)
                pe.wait_ge(x_v, g + 1)
                for i in range(GB):
                    last = mm(ps[:, 7, i * N:(i + 1) * N], xv[:, i, :], xpT[:, i, :], start=True, stop=True)
                last.then_inc(x_c_ps, 1)
                pe.wait_ge(x_c, g + 1)
                for i in range(GB):
                    last = mm(ps[:, 2, i * D:(i + 1) * D], xcT[:, i, :], wo_s[:], start=True, stop=True)
                last.then_inc(x_y_ps, 1)
                pe.wait_ge(x_z2, GB * g + GB)
                for i in range(GB):
                    last = tr(ps[:, 0, i * N:(i + 1) * N], zx[:, i, :], idn[:])
                last.then_inc(x_T2, 1)

            def qkv(m, part):
                done = (q_ps, k_ps, v_ps)[part]
                whi = wqkv_hi[:, bass.ds(m.layer * 3 * INNER + part * INNER, INNER)]
                wlo = wqkv_lo[:, bass.ds(m.layer * 3 * INNER + part * INNER, INNER)]
                j = m.j
                mm(ps[:, part, :], h_hi[j][:], whi, start=True, stop=False)
                mm(ps[:, part, :], h_hi[j][:], wlo, start=False, stop=False)
                mm(ps[:, part, :], h_lo[j][:], whi, start=False, stop=True).then_inc(done[j], 1)

            def step(at, on):
                if on(1):
                    m = at(1)
                    j = m.j
                    if on(0):
                        prev = at(0)
                        pe.wait_ge(sm_ready[prev.j], 8 * prev.g + 8)
                    pe.wait_ge(qT_ready[j], m.g + 1)
                    pe.wait_ge(kT_ready[j], m.g + 1)
                    mm(ps[:, TQ, 0:2], idn[:], idn[:, 0:2], start=True, stop=True)
                    for c in range(PAIRS):
                        for a in (0, 64):
                            last = mm(ps[a:a + 64, S1, c * 128:(c + 1) * 128], qT[j][a:a + 64, c, W:N], kT[j][a:a + 64, c, :],
                                      start=True, stop=True)
                    last.then_inc(s1_ps[j], 1)
                    for c in range(PAIRS):
                        for a in (0, 64):
                            last = mm(ps[a:a + 64, S0, c * W:(c + 1) * W], qT[j][a:a + 64, c, 0:W], kT[j][a:a + 64, c, 0:W],
                                      start=True, stop=True)
                    last.then_inc(s0_ps[j], 1)
                if on(-1):
                    m = at(-1)
                    j = m.j
                    pe.wait_ge(x_upd[j], 2 * m.g + 2)
                    mm(ps[:, OB, 0:N], ones[:], h_of(m.b), start=True, stop=True).then_inc(m_ps[j], 1)
                if on(3):
                    m = at(3)
                    pe.wait_ge(h_ready[m.j], m.g + 1)
                    if on(2):
                        pe.wait_ge(qn_ready[at(2).j], at(2).g + 1)
                    qkv(m, 0)
                if on(0):
                    m = at(0)
                    j = m.j
                    pe.wait_ge(pn_ready[j], 2 * m.g + 2)
                    for c in range(PAIRS):
                        last = tr(ps[:, TQ, c * 128:(c + 1) * 128], p1[j][:, c, :], idn[:])
                    last.then_inc(pt1_ps[j], 1)
                    for c in range(2):
                        last = tr(ps[:, TK, c * 128:(c + 1) * 128],
                                  p0[j][:, 2 * c:2 * c + 2, :].rearrange("p a k -> p (a k)"), idn[:])
                    last.then_inc(pt0_ps[j], 1)
                if on(3):
                    qkv(at(3), 1)
                if on(-1):
                    m = at(-1)
                    j = m.j
                    pe.wait_ge(d2_ready[j], m.g + 1)
                    mm(ps[:, OB, 0:N], ones[:], dsq[j][:], start=True, stop=True).then_inc(var_ps[j], 1)
                if on(2):
                    if on(1):
                        pe.wait_ge(v_ready[at(1).j], at(1).g + 1)
                    qkv(at(2), 2)
                if on(0):
                    m = at(0)
                    j = m.j
                    pe.wait_ge(pt_ready[j], 3 * m.g + 3)
                    pe.wait_ge(v_ready[j], m.g + 1)
                    if on(-1):
                        pm = at(-1)
                        pe.wait_ge(lnl_done[pm.j], pm.g + 1)

                    def first_window(c):
                        for a in (0, 64):
                            v_h = (2 * c + a // 64) * DH
                            last = mm(ps[a:a + 64, OB, c * 128:c * 128 + W], vv[j][0:W, v_h:v_h + DH],
                                      pT0[j][:, c % 2, c // 2, a:a + 64], start=True, stop=True)
                        return last

                    def second_window(c):
                        for a in (0, 64):
                            v_h = (2 * c + a // 64) * DH
                            mm(ps[a:a + 64, OB, c * 128 + W:(c + 1) * 128], vv[j][:, v_h:v_h + DH], pT1[j][:, c, a:a + 64],
                               start=True, stop=True)

                    for c in range(PAIRS):
                        second_window(c)
                    for c in range(PAIRS):
                        last = first_window(c)
                    last.then_inc(o_ps[j], 1)
                if on(2):
                    m = at(2)
                    j = m.j
                    pe.wait_ge(rot_ready[j], m.g + 1)
                    for c in range(PAIRS):
                        last = tr(ps[:, TQ, c * 128:(c + 1) * 128], qr[j][:, c * 128:(c + 1) * 128], idn[:])
                    last.then_inc(tq_ps[j], 1)
                    for c in range(PAIRS):
                        last = tr(ps[:, TK, c * 128:(c + 1) * 128], qr[j][:, INNER + c * 128:INNER + (c + 1) * 128], idn[:])
                    last.then_inc(tk_ps[j], 1)
                if on(0):
                    m = at(0)
                    j = m.j
                    pe.wait_ge(oT_ready[j], m.g + 1)
                    for c in range(PAIRS):
                        last = mm(ps[:, OB, 0:N], wo_l[:, c, :], oT[j][:, c, :], start=(c == 0), stop=(c == PAIRS - 1))
                    last.then_inc(y_ps[j], 1)

            def hidden(g, gl_, c):
                o, m = CH[c]
                hh = hn_hi[:, bass.ds(g * GB, GB), :].rearrange("p b n -> p (b n)")
                hl = hn_lo[:, bass.ds(g * GB, GB), :].rearrange("p b n -> p (b n)")
                for s in range(2):
                    o2 = s * HID + o
                    mm(ps[0:m, 2 * c + s, :], w1_hi[:, o2:o2 + m], hh, start=True, stop=False)
                    mm(ps[0:m, 2 * c + s, :], w1_hi[:, o2:o2 + m], hl, start=False, stop=False)
                    last = mm(ps[0:m, 2 * c + s, :], w1_lo[:, o2:o2 + m], hh, start=False, stop=True)
                last.then_inc(g_ps[c], 1)

            def back(gl_, c):
                o, m = CH[c]
                pe.wait_ge(ul_ready[c], gl_ + 1)
                if c == 0:
                    pe.wait_ge(f_upd, 2 * gl_ + 2)
                mm(ps[:, 6, :], w2_hi[0:m, c, :], u_hi[0:m, c, :], start=(c == 0), stop=False)
                mm(ps[:, 6, :], w2_hi[0:m, c, :], u_lo[0:m, c, :], start=False, stop=False)
                last = mm(ps[:, 6, :], w2_lo[0:m, c, :], u_hi[0:m, c, :], start=False, stop=(c == 2))
                last.then_inc(f_acc[c], 1)
                if c == 2:
                    pass

            pe.wait_ge(x_out, 2 * NG)
            pe.wait_ge(ld_w, 16 * 6)
            pe.wait_ge(ld_b, 16 * 14)
            for l in range(DEPTH):
                for s in range(2):
                    for c, (o, m) in enumerate(CH):
                        k = l * 6 + s * 3 + c
                        last = mm(ps[0:m, OB, k:k + 1], w1_raw[:, l, s * HID + o:s * HID + o + m], lgb[:, 1, l:l + 1],
                                  start=True, stop=True)
            last.then_inc(b1_ps, 1)

            pe.wait_ge(wsplit, 2)
            with pe.Fori(0, DEPTH) as layer:
                pe.wait_ge(layer_w, 9 * layer + 9)
                pipeline(pe, layer, step)
                for j in (0, 1):
                    pe.wait_ge(hn_ready[j], (B // 2) * layer + B // 2)
                hidden(0, layer * NG, 0)

                def group(g, last_one):
                    gl_ = layer * NG + g
                    if True:
                        hidden(g, gl_, 1)
                        back(gl_, 0)
                        hidden(g, gl_, 2)
                        back(gl_, 1)
                    if not last_one:
                        pe.wait_ge(u_ready[0], gl_ + 1)
                        hidden(g + 1, gl_ + 1, 0)
                    back(gl_, 2)
                    if not last_one:
                        pe.wait_ge(u_ready[1], gl_ + 1)
                        pe.wait_ge(u_ready[2], gl_ + 1)

                with pe.Fori(0, NG - 1) as g:
                    group(g, False)
                group(NG - 1, True)

            for g in range(NG):
                j = g % 2
                pe.wait_ge(st_ready[j], 2 * (g // 2) + 2)
                if g >= 2:
                    pe.wait_ge(ot_ready[j], g // 2)
                for i in range(GB):
                    last = tr(ps[:, j, i * 128:(i + 1) * 128], stg[j][:, i, :], idn[:])
                last.then_inc(st_T[j], 1)

        @block.scalar
        def _(act):
            A = nc.scalar.activation
            act.dma_start(gates[:, 0:1], g_xattn.rearrange("(o d) -> o d", o=1).partition_broadcast(128)).then_inc(ld_b, 16)
            act.dma_start(gates[:, 1:2], g_ffn.rearrange("(o d) -> o d", o=1).partition_broadcast(128)).then_inc(ld_b, 16)
            for k, (v, n) in enumerate(((ln1_g, D), (ln1_b, D), (ln2_g, DC), (ln2_b, DC), (bq, D), (bk, D))):
                act.dma_start(cols[0:n, k:k + 1], v.rearrange("(p o) -> p o", o=1)).then_inc(ld_b, 16)
            for k, v in enumerate((ln_g, ln_b, b2)):
                for l in range(DEPTH):
                    act.dma_start(lgb[:, k, l:l + 1], v[l:l + 1, :].rearrange("o p -> p o")).then_inc(ld_b, 16)
            act.wait_ge(ld_b, 16 * 14)
            A(tg[:], gates[:], ACT.Tanh).then_inc(tanh_done, 1)
            act.wait_ge(cst_v, 4)
            nc.scalar.preload_act_table_set("natural_log_exp_and_others")

            with act.Fori(0, NG) as g:
                act.wait_ge(xln, 2 * g + 1)
                A(lnv[:], mv[:, :, 1], ACT.Ln, bias=epst[:]).then_inc(xlnr, 1)
                A(lnc[0:NC, :], cmv[0:NC, :, 1], ACT.Ln, bias=epst[0:NC, :]).then_inc(xlnr, 1)
                act.wait_ge(xlnr, 10 * g + 2)
                A(r1[:], lnv[:], ACT.Exp, scale=-0.5).then_inc(xlnr, 1)
                A(rc[0:NC, :], lnc[0:NC, :], ACT.Exp, scale=-0.5).then_inc(xlnr, 1)
                act.wait_ge(xln, 2 * g + 2)
                A(lnv[:], tmp4[:], ACT.Ln, bias=epst[:]).then_inc(xlnr, 1)
                act.wait_ge(xlnr, 10 * g + 5)
                A(r2[:], lnv[:], ACT.Exp, scale=-0.5).then_inc(xlnr, 1)
                act.wait_ge(x_qk_ps, 2 * g + 1)
                A(xqT[:].rearrange("p b n -> p (b n)"), ps[:, 2, :], ACT.Identity, bias=cols[:, 4:5]).then_inc(x_q, 1)
                for i in range(GB):
                    act.wait_ge(x_nm, 2 * g + 2)
                    A(xp[:, i, :], ps[:, 5, i * NC:(i + 1) * NC], ACT.Exp, bias=nmb[:, i:i + 1], scale=float(D) ** -0.5,
                      accum_out=xsum[:, i:i + 1]).then_inc(x_p, 1)
                act.wait_ge(x_pT_ps, g + 1)
                A(xpT[:].rearrange("p b n -> p (b n)"), ps[0:NC, 6, :], ACT.Copy).then_inc(x_pT, 1)
                act.wait_ge(x_c_ps, g + 1)
                A(xcT[:].rearrange("p b n -> p (b n)"), ps[:, 7, :], ACT.Copy).then_inc(x_c, 1)
                act.wait_ge(x_v2, g + 1)
                A(lnv[:], mv[:, :, 1], ACT.Ln, bias=epst[:]).then_inc(xlnr, 1)
                act.wait_ge(xlnr, 10 * g + 7)
                A(r1[:], lnv[:], ACT.Exp, scale=-0.5).then_inc(xlnr, 3)
                act.wait_ge(x_T2, g + 1)
                lo, hi = halves(xs, g * GB, GB)
                A(lo, ps[0:64, 0, :].rearrange("p (b n) -> p b n", b=GB), ACT.Copy).then_inc(x_out, 1)
                A(hi, ps[64:128, 0, :].rearrange("p (b n) -> p b n", b=GB), ACT.Copy).then_inc(x_out, 1)

            def step(at, on):
                if on(1):
                    m = at(1)
                    j = m.j
                    for c in range(PAIRS):
                        act.wait_ge(sm_ready[j], 8 * m.g + c + 1)
                        A(p1[j][:, c, :], sm1[j][:, c, :], ACT.Exp, bias=nm[j][:, c:c + 1], scale=-1.0,
                          accum_out=psum_[j][:, c:c + 1]).then_inc(p1_done[j], 1)
                if on(3):
                    m = at(3)
                    act.wait_ge(q_ps[m.j], m.g + 1)
                    A(sqr[m.j][:, 0:INNER], ps[:, QB, :], ACT.Square).then_inc(sq_done[m.j], 1)
                if on(0):
                    m = at(0)
                    j = m.j
                    act.wait_ge(pt1_ps[j], m.g + 1)
                    A(pT1[j][:].rearrange("p c n -> p (c n)"), ps[:, TQ, :], ACT.Copy).then_inc(pt_ready[j], 1)
                    act.wait_ge(pt0_ps[j], m.g + 1)
                    for u in range(2):
                        A(pT0[j][:, u, :, :].rearrange("p c n -> p (c n)"), ps[u * W:(u + 1) * W, TK, 0:256],
                          ACT.Copy).then_inc(pt_ready[j], 1)
                if on(3):
                    m = at(3)
                    act.wait_ge(k_ps[m.j], m.g + 1)
                    A(sqr[m.j][:, INNER:], ps[:, KB, :], ACT.Square).then_inc(sq_done[m.j], 1)
                if on(-1):
                    m = at(-1)
                    j = m.j
                    act.wait_ge(var_ps[j], m.g + 1)
                    A(lnl[j][:], ps[:, OB, 0:N], ACT.Ln, bias=epst[:]).then_inc(lnl_done[j], 1)
                if on(1):
                    m = at(1)
                    j = m.j
                    for c in range(PAIRS):
                        act.wait_ge(sm_ready[j], 8 * m.g + 4 + c + 1)
                        A(p0[j][:, c, :], sm0[j][:, c, :], ACT.Exp, bias=nm[j][:, 4 + c:5 + c], scale=-1.0,
                          accum_out=psum_[j][:, 4 + c:5 + c]).then_inc(p0_done[j], 1)
                if on(3):
                    m = at(3)
                    j = m.j
                    act.wait_ge(ss_ready[j], m.g + 1)
                    A(lns[j][:], ssc[j][:], ACT.Ln, scale=LN_SCALE).then_inc(ln_done[j], 1)
                if on(-1):
                    m = at(-1)
                    j = m.j
                    act.wait_ge(lnl_done[j], m.g + 1)
                    A(rstd[j][:], lnl[j][:], ACT.Exp, scale=-0.5).then_inc(rstd_ready[j], 1)
                if on(3):
                    m = at(3)
                    j = m.j
                    act.wait_ge(ln_done[j], m.g + 1)
                    A(rr[j][:], lns[j][:], ACT.Exp, scale=-0.5, bias=backt[:]).then_inc(r_ready[j], 1)
                if on(0):
                    m = at(0)
                    j = m.j
                    act.wait_ge(o_ps[j], m.g + 1)
                    A(oT[j][:].rearrange("p c n -> p (c n)"), ps[:, OB, :], ACT.Copy).then_inc(oT_ready[j], 1)
                if on(2):
                    m = at(2)
                    j = m.j
                    act.wait_ge(v_ps[j], m.g + 1)
                    A(vv[j][:], ps[:, VB, :], ACT.Copy).then_inc(v_ready[j], 1)
                    act.wait_ge(tq_ps[j], m.g + 1)
                    A(qT[j][:].rearrange("p c n -> p (c n)"), ps[:, TQ, :], ACT.Copy).then_inc(qT_ready[j], 1)
                    act.wait_ge(tk_ps[j], m.g + 1)
                    A(kT[j][:].rearrange("p c n -> p (c n)"), ps[:, TK, :], ACT.Copy).then_inc(kT_ready[j], 1)

            with act.Fori(0, DEPTH) as layer:
                pipeline(act, layer, step)

                nc.scalar.preload_act_table_set("gelu_and_others")

                def chunk(gl_, c):
                    o, m = CH[c]
                    act.wait_ge(g_ps[c], gl_ + 1)
                    A(gl[0:m, c, :], ps[0:m, 2 * c + 1, :], ACT.Gelu, bias=b1_l[0:m, 3 + c:4 + c]).then_inc(gl_ready[c], 1)

                def split(gl_, c):
                    o, m = CH[c]
                    act.wait_ge(u_ready[c], gl_ + 1)
                    A(u_hi[0:m, c, :], uu[0:m, c, :], ACT.Copy).then_inc(uh_ready[c], 1)

                with act.Fori(0, NG) as g:
                    gl_ = layer * NG + g
                    chunk(gl_, 0)
                    split(gl_, 0)
                    chunk(gl_, 1)
                    split(gl_, 1)
                    chunk(gl_, 2)
                    split(gl_, 2)
                nc.scalar.preload_act_table_set("natural_log_exp_and_others")

            for g in range(NG):
                j = g % 2
                lo, hi = halves(xs, g * GB, GB)
                act.wait_ge(f_upd, 2 * NG * (DEPTH - 1) + 2 * g + 4)
                if g >= 2:
                    act.wait_ge(st_T[j], g // 2)
                A(stg[j][0:64, :, :], lo, ACT.Copy).then_inc(st_ready[j], 1)
                A(stg[j][64:128, :, :], hi, ACT.Copy).then_inc(st_ready[j], 1)

        @block.vector
        def _(dve):
            V = nc.vector
            V.memset(ones[:], 1.0 / D).then_inc(cst_v, 1)
            V.memset(epst[:], EPS).then_inc(cst_v, 1)
            V.memset(mark_v[:, 7:8], 0.0).then_inc(f_upd, 2)
            V.memset(backt[:], LN_BACK).then_inc(cst_v, 1)
            V.memset(xs[64:128, :, 0:1], 0.0).then_inc(cst_v, 1)
            dve.wait_ge(tanh_done, 1)
            dve.wait_ge(ld_b, 16 * 14)
            dve.wait_ge(ld_bg, 16 * 2)
            V.tensor_scalar(bob[:], bob[:], tg[:, 0:1], None, ALU.mult).then_inc(xbias, 1)
            dve.wait_ge(ld_small, 16 * 16)
            for l in range(DEPTH):
                V.tensor_tensor(ctab[:, l, :, :], rott[:, 0:2, :], qks[:, l, :, :], ALU.mult).then_inc(tab_done, 1)
                for u in range(2):
                    V.tensor_tensor(stab[:, l, :, u * 32:u * 32 + 32], rott[:, 2:4, u * 32:u * 32 + 32],
                                    qks[:, l, :, (1 - u) * 32:(1 - u) * 32 + 32], ALU.mult).then_inc(tab_done, 1)

            with dve.Fori(0, NG) as g:
                c0 = 0
                xg, cg = xt[:, bass.ds(g * GB, GB), :], ct[:, bass.ds(g * GB, GB), :]
                K = 46
                dve.wait_ge(ld_x, 16 * NG)
                dve.wait_ge(ld_c, 16)
                for i in range(GB):
                    V.bn_stats(bst[:, i, :], xt[:, bass.ds(g * GB + i, 1), :].rearrange("p o d -> p (o d)")).then_inc(xchain, 1)
                    V.bn_stats(cst[0:NC, i, :], ct[:, bass.ds(g * GB + i, 1), :].rearrange("p o d -> p (o d)")).then_inc(xchain, 1)
                apart(V, xchain, K * g + 8, 2)
                for i in range(GB):
                    V.bn_aggr(mv[:, i, :], bst[:, i, :]).then_inc(xchain, 1)
                    V.bn_aggr(cmv[0:NC, i, :], cst[0:NC, i, :]).then_inc(xchain, 1)
                dve.wait_ge(xchain, K * g + 16)
                V.memset(tmp4[:], 0.0).then_inc(xln, 1)
                dve.wait_ge(xlnr, 10 * g + 4)
                dve.wait_ge(xln, 2 * g + 1)
                V.tensor_tensor(tmp4[:], r1[:], r1[:], ALU.mult).then_inc(xchain, 1)
                dve.wait_ge(xchain, K * g + 17)
                V.tensor_tensor(tmp4[:], tmp4[:], mv[:, :, 1], ALU.mult).then_inc(xln, 1)
                for i in range(GB):
                    V.tensor_scalar(zc[:, i, :], ct[:, bass.ds(g * GB + i, 1), :].rearrange("p o d -> p (o d)"),
                                    cmv[0:NC, i, 0:1], rc[0:NC, i:i + 1], ALU.subtract, ALU.mult).then_inc(xchain, 1)
                dve.wait_ge(xlnr, 10 * g + 6)
                V.tensor_tensor(r1[:], r1[:], r2[:], ALU.mult).then_inc(xchain, 1)
                dve.wait_ge(xchain, K * g + 22)
                for i in range(GB):
                    V.tensor_scalar(zx[:, i, :], xt[:, bass.ds(g * GB + i, 1), :].rearrange("p o d -> p (o d)"),
                                    mv[:, i, 0:1], r1[:, i:i + 1], ALU.subtract, ALU.mult).then_inc(x_z, 1)
                V.tensor_copy(nmx[:], r1[:]).then_inc(x_z, GB)
                dve.wait_ge(x_zT, 2 * g + 1)
                V.tensor_scalar(x1T[:], ps[:, 0, :], cols[:, 0:1], cols[:, 1:2], ALU.mult, ALU.add).then_inc(x_1T, 1)
                dve.wait_ge(x_zT, 2 * g + 2)
                V.tensor_scalar(c1T[:].rearrange("p b n -> p (b n)"), ps[0:DC, 1, 0:GB * NC], cols[0:DC, 2:3], cols[0:DC, 3:4],
                                ALU.mult, ALU.add).then_inc(x_1T, 1)
                dve.wait_ge(x_qk_ps, 2 * g + 2)
                V.tensor_scalar(xkT[:].rearrange("p b n -> p (b n)"), ps[:, 3, 0:GB * NC], cols[:, 5:6], None, ALU.add).then_inc(x_k, 1)
                dve.wait_ge(x_v_ps, g + 1)
                V.tensor_tensor(xv[:], ps[0:NC, 4, :].rearrange("p (b d) -> p b d", b=GB),
                                bvb[0:NC, :].unsqueeze(1).to_broadcast([NC, GB, D]), ALU.add).then_inc(x_v, 1)
                dve.wait_ge(x_s, g + 1)
                V.tensor_reduce(nmx[:], ps[:, 5, 0:GB * NC].rearrange("p (b n) -> p b n", b=GB), AX.X, ALU.max).then_inc(x_nm, 1)
                dve.wait_ge(x_nm, 2 * g + 1)
                V.tensor_scalar(nmb[:], nmx[:], -float(D) ** -0.5, None, ALU.mult).then_inc(x_nm, 1)
                dve.wait_ge(x_p, GB * g + GB)
                V.reciprocal(xri[:], xsum[:]).then_inc(xchain, 1)
                dve.wait_ge(xchain, K * g + 23)
                V.tensor_scalar(xrt[:], xri[:], tg[:, 0:1], None, ALU.mult).then_inc(xchain, 1)
                dve.wait_ge(xchain, K * g + 24)
                dve.wait_ge(x_y_ps, g + 1)
                dve.wait_ge(cst_g, g + 1)
                for i in range(GB):
                    xi = xt[:, bass.ds(g * GB + i, 1), :].rearrange("p o d -> p (o d)")
                    V.scalar_tensor_tensor(out=xi, in0=ps[:, 2, i * D:(i + 1) * D], scalar=xrt[:, i:i + 1], in1=xi,
                                           op0=ALU.mult, op1=ALU.add).then_inc(xchain, 1)
                apart(V, xchain, K * g + 28, 3)
                for i in range(GB):
                    V.bn_stats(bst[:, i, :], xt[:, bass.ds(g * GB + i, 1), :].rearrange("p o d -> p (o d)")).then_inc(xchain, 1)
                apart(V, xchain, K * g + 32, 4)
                for i in range(GB):
                    V.bn_aggr(mv[:, i, :], bst[:, i, :]).then_inc(xchain, 1)
                dve.wait_ge(xchain, K * g + 36)
                V.tensor_copy(nmx[:], mv[:, :, 0]).then_inc(x_v2, 1)
                dve.wait_ge(x_v2, g + 1)
                dve.wait_ge(xlnr, 10 * g + 10)
                for i in range(GB):
                    V.tensor_scalar(zx[:, i, :], xt[:, bass.ds(g * GB + i, 1), :].rearrange("p o d -> p (o d)"),
                                    nmx[:, i:i + 1], r1[:, i:i + 1], ALU.subtract, ALU.mult).then_inc(x_z2, 1)
                V.memset(nmb[:], 0.0).then_inc(xchain, 10)
                dve.wait_ge(xchain, K * g + 46)

            dve.wait_ge(ld_w, 16 * 6)
            wr = wqkv_raw[:].rearrange("p l n -> p (l n)")
            V.tensor_copy(wqkv_hi[:], wr).then_inc(wsplit, 1)
            dve.wait_ge(wsplit, 1)
            V.tensor_tensor(wqkv_lo[:], wr, wqkv_hi[:].bitcast(F32), ALU.subtract).then_inc(wsplit, 1)
            dve.wait_ge(b1_ps, 1)
            for c, (o, m) in enumerate(CH):
                V.tensor_tensor(b1_all[0:m, :, c::3], ps[0:m, OB, 0:12].rearrange("p (l s c) -> p l s c", l=2, s=2)[:, :, :, c],
                                b1_raw[0:m, :, c::3], ALU.add).then_inc(b1_done, 1)

            def head_in(m):
                j = m.j
                V.tensor_copy(h_hi[j][:], h_of(m.b)).then_inc(h_hi_ok[j], 1)
                dve.wait_ge(h_hi_ok[j], m.g + 1)
                V.tensor_tensor(h_lo[j][:], h_of(m.b), h_hi[j][:].bitcast(F32), ALU.subtract).then_inc(h_ready[j], 1)

            def step(at, on):
                if on(-1):
                    m = at(-1)
                    j = m.j
                    dve.wait_ge(y_ps[j], m.g + 1)
                    for t, q in zip(halves(xs, m.b, 1), (0, 64)):
                        t = t.rearrange("p o n -> p (o n)")
                        V.tensor_tensor(t, ps[q:q + 64, OB, 0:N], t, ALU.add).then_inc(x_upd[j], 1)
                if on(3):
                    if on(1):
                        dve.wait_ge(v_ps[at(1).j], at(1).g + 1)
                    head_in(at(3))
                if on(1):
                    m = at(1)
                    j = m.j
                    apart(V, s1_ps[j], m.g + 1, 0)
                    for c in range(PAIRS):
                        V.tensor_tensor_reduce(out=sm1[j][:, c, :], in0=ps[:, S1, c * 128:(c + 1) * 128], in1=msk[:, 0:128],
                                               scale=-1.0, scalar=3e38, op0=ALU.add, op1=ALU.min,
                                               accum_out=nm[j][:, c:c + 1]).then_inc(sm_ready[j], 1)
                    apart(V, s0_ps[j], m.g + 1, 1)
                    for c in range(PAIRS):
                        V.tensor_tensor_reduce(out=sm0[j][:, c, :], in0=ps[:, S0, c * W:(c + 1) * W], in1=msk[:, 128:192],
                                               scale=-1.0, scalar=3e38, op0=ALU.add, op1=ALU.min,
                                               accum_out=nm[j][:, 4 + c:5 + c]).then_inc(sm_ready[j], 1)
                if on(-1):
                    m = at(-1)
                    j = m.j
                    dve.wait_ge(m_ps[j], m.g + 1)
                    V.tensor_tensor(dd[j][:], h_of(m.b), ps[:, OB, 0:N], ALU.subtract).then_inc(d_ready[j], 1)
                    dve.wait_ge(d_ready[j], m.g + 1)
                    V.tensor_tensor(dsq[j][:], dd[j][:], dd[j][:], ALU.mult).then_inc(d2_ready[j], 1)
                if on(3):
                    m = at(3)
                    j = m.j
                    dve.wait_ge(sq_done[j], 2 * m.g + 2)
                    V.tensor_reduce(ss[j][:], sqr[j][:].rearrange("p (h d) -> p h d", d=DH), AX.X, ALU.add).then_inc(ss_sum[j], 1)
                    dve.wait_ge(ss_sum[j], m.g + 1)
                    V.tensor_scalar(ssc[j][:], ss[j][:], 1e-24, None, ALU.max).then_inc(ss_ready[j], 1)
                if on(1):
                    m = at(1)
                    j = m.j
                    dve.wait_ge(p1_done[j], 4 * m.g + 4)
                    dve.wait_ge(p0_done[j], 4 * m.g + 4)
                    V.reciprocal(pri[j][:], psum_[j][:]).then_inc(ri_ready[j], 1)
                if on(-1):
                    m = at(-1)
                    j = m.j
                    dve.wait_ge(rstd_ready[j], m.g + 1)
                    V.tensor_tensor(hnf[j][:], dd[j][:], rstd[j][:], ALU.mult).then_inc(hnf_ready[j], 1)
                    dve.wait_ge(hnf_ready[j], m.g + 1)
                    hh = hn_hi[:, bass.ds(m.b, 1), :].rearrange("p o n -> p (o n)")
                    hl = hn_lo[:, bass.ds(m.b, 1), :].rearrange("p o n -> p (o n)")
                    V.tensor_copy(hh, hnf[j][:]).then_inc(hh_ready[j], 1)
                    dve.wait_ge(hh_ready[j], m.g + 1)
                    V.tensor_tensor(hl, hnf[j][:], hh.bitcast(F32), ALU.subtract).then_inc(hn_ready[j], 1)
                if on(3):
                    m = at(3)
                    j = m.j
                    dve.wait_ge(r_ready[j], m.g + 1)
                    V.tensor_tensor(qn[j].rearrange("p (h d) -> p h d", d=DH), ps[:, QB:KB + 1, :].rearrange("p s (h d) -> p (s h) d", d=DH),
                                    rr[j][:].unsqueeze(2).to_broadcast([128, 2 * HEADS, DH]), ALU.mult).then_inc(qn_ready[j], 1)
                if on(3):
                    m = at(3)
                    j = m.j
                    dve.wait_ge(qn_ready[j], m.g + 1)
                    for s in range(2):
                        V.tensor_tensor(rc1[j][:, s * INNER:(s + 1) * INNER].rearrange("p (h d) -> p h d", h=HEADS),
                                        qn[j][:, s * INNER:(s + 1) * INNER].rearrange("p (h d) -> p h d", h=HEADS),
                                        ctab[:, bass.ds(m.layer, 1), s, :].to_broadcast([128, HEADS, DH]),
                                        ALU.mult).then_inc(c_ready[j], 1)

            dve.wait_ge(x_out, 2 * NG)
            dve.wait_ge(b1_done, 3)
            with dve.Fori(0, DEPTH) as layer:
                def of(t):
                    return t[:, bass.ds(layer, 1)]
                V.tensor_copy(wo_l[:], wo_raw[:, bass.ds(layer, 1)].rearrange("p o c n -> p (o c) n")).then_inc(layer_w, 1)
                V.tensor_scalar(w1g[:], of(w1_raw).rearrange("p o n -> p (o n)"), lgb[:, 0, bass.ds(layer, 1)], None,
                                ALU.mult).then_inc(layer_w, 1)
                dve.wait_ge(layer_w, 9 * layer + 2)
                V.tensor_copy(w1_hi[:], w1g[:]).then_inc(layer_w, 1)
                for c, (o, m) in ((0, (0, 128)), (2, CH[2])):
                    n = 2 if c == 0 else 1
                    V.tensor_copy(w2_hi[0:m, c:c + n, :], w2_raw[0:m, bass.ds(layer, 1), c:c + n, :].rearrange("p o c n -> p (o c) n")
                                  ).then_inc(layer_w, 1)
                dve.wait_ge(layer_w, 9 * layer + 5)
                V.tensor_tensor(w1_lo[:], w1g[:], w1_hi[:].bitcast(F32), ALU.subtract).then_inc(layer_w, 1)
                for c, (o, m) in ((0, (0, 128)), (2, CH[2])):
                    n = 2 if c == 0 else 1
                    V.tensor_tensor(w2_lo[0:m, c:c + n, :], w2_raw[0:m, bass.ds(layer, 1), c:c + n, :].rearrange("p o c n -> p (o c) n"),
                                    w2_hi[0:m, c:c + n, :].bitcast(F32), ALU.subtract).then_inc(layer_w, 1)
                for c, (o, m) in enumerate(CH):
                    V.tensor_copy(b1_l[0:m, c::3], b1_all[0:m, bass.ds(layer, 1), c::3].rearrange("p o n -> p (o n)")
                                  ).then_inc(b1_done, 1)
                V.tensor_copy(b2_l[:], lgb[:, 2, bass.ds(layer, 1)]).then_inc(layer_w, 1)
                dve.wait_ge(b1_done, 3 * layer + 6)
                dve.wait_ge(layer_w, 9 * layer + 9)

                pipeline(dve, layer, step)

                def gate(gl_, c):
                    o, m = CH[c]
                    dve.wait_ge(gl_ready[c], gl_ + 1)
                    V.scalar_tensor_tensor(out=uu[0:m, c, :], in0=ps[0:m, 2 * c, :], scalar=b1_l[0:m, c:c + 1], in1=gl[0:m, c, :],
                                           op0=ALU.add, op1=ALU.mult).then_inc(u_ready[c], 1)

                def low(gl_, c):
                    o, m = CH[c]
                    dve.wait_ge(uh_ready[c], gl_ + 1)
                    V.tensor_tensor(u_lo[0:m, c, :], uu[0:m, c, :], u_hi[0:m, c, :].bitcast(F32), ALU.subtract).then_inc(ul_ready[c], 1)

                with dve.Fori(0, NG) as g:
                    gl_ = layer * NG + g
                    gate(gl_, 0)
                    low(gl_, 0)
                    gate(gl_, 1)
                    low(gl_, 1)
                    gate(gl_, 2)
                    low(gl_, 2)
                    dve.wait_ge(f_acc[2], gl_ + 1)
                    for t, q in zip(halves(xs, g * GB, GB), (0, 64)):
                        V.scalar_tensor_tensor(out=t, in0=ps[q:q + 64, 6, :].rearrange("p (b n) -> p b n", b=GB),
                                               scalar=b2_l[q:q + 64, :], in1=t, op0=ALU.add, op1=ALU.add).then_inc(f_upd, 1)
                dve.wait_ge(f_upd, 2 * NG * layer + 2 * NG + 2)

            for g in range(NG):
                j = g % 2
                dve.wait_ge(st_T[j], g // 2 + 1)
                if g >= 2:
                    dve.wait_ge(stored[j], 16 * (g // 2))
                V.scalar_tensor_tensor(out=ot[j][:].rearrange("p b n -> p (b n)"), in0=ps[:, j, :], scalar=tg[:, 1:2],
                                       in1=xt[:, g * GB:(g + 1) * GB, :].rearrange("p b n -> p (b n)"),
                                       op0=ALU.mult, op1=ALU.add).then_inc(ot_ready[j], 1)


_INS = ["x", "ctx_768", "g_xattn", "g_ffn"] + ["L0_xattn_" + n for n in (
    "ln1_g", "ln1_b", "ln2_g", "ln2_b", "Wq", "bq", "Wk", "bk", "Wv", "bv", "Wo", "bo")] + ["L0_ffn_" + n for n in (
    "wqkv", "q_scale", "k_scale", "wo", "ln_g", "ln_b", "w1", "b1", "w2", "b2")]


def kernel(**inputs):
    import concourse.bacc as _bacc
    from concourse.bass_utils import run_bass_kernel_spmd as _run

    nc = _bacc.Bacc("TRN2", target_bir_lowering=False, num_devices=1)
    given = {n: np.ascontiguousarray(inputs[n]) for n in _INS}
    given |= dict(zip(("rot_table", "window_masks", "identity"), tables()))
    arrays, args = {}, []
    for name, a in given.items():
        arrays[f"in_{name}_dram"] = a
        args.append(nc.dram_tensor(f"in_{name}_dram", a.shape, mybir.dt.from_np(a.dtype), kind="ExternalInput").ap())
    args.append(nc.dram_tensor("out_0_dram", (B, N, D), F32, kind="ExternalOutput").ap())
    build(nc, *args)
    r = _run(nc, [arrays], core_ids=[0])
    return r.results[0]["out_0_dram"]
```

```python
from contextlib import ExitStack

import numpy as np

import concourse.bass as bass
from concourse import mybir

F32 = mybir.dt.float32
F32R = mybir.dt.float32r
ALU = mybir.AluOpType
ACT = mybir.ActivationFunctionType
AX = mybir.AxisListType

B, N, D = 16, 128, 128
NC, DC = 120, 96
HEADS, DH, W = 8, 64, 64
INNER = HEADS * DH
PAIRS = HEADS // 2
DEPTH = 2
HID = int(D * 4 * 2 / 3)
CH = [(0, 128), (128, 128), (256, HID - 256)]
GB = 4
NG = B // GB
EPS = 1e-5
NEG = -1e30
LN_SCALE = 2.0 ** 16
LN_BACK = 8.0 * float(np.log(2.0))


def tables():
    half = np.arange(0, DH, 2, dtype=np.float32)
    inv = (np.float32(1.0) / np.power(np.float32(10000.0), half / np.float32(DH))).astype(np.float32)
    t = np.arange(N, dtype=np.float32)
    fr = (t[:, None] * inv[None, :]).astype(np.float32)
    fr = np.concatenate([fr, fr], -1)
    base = ((half + np.float32(0.4 * DH)) / np.float32(1.4 * DH)).astype(np.float32)
    power = ((t - N // 2) / np.float32(W // 2)).astype(np.float32)
    sc = np.power(base[None, :].astype(np.float64), power[:, None])
    sc = np.concatenate([sc, sc], -1)
    cos, sin = np.cos(fr.astype(np.float64)), np.sin(fr.astype(np.float64))
    sgn = np.concatenate([-np.ones(DH // 2), np.ones(DH // 2)])[None, :]
    cq, sq = cos * sc * 8.0, sin * sc * 8.0 * sgn
    ck, sk = cos / sc, sin / sc * sgn
    rot = np.stack([cq, ck, sq, sk], 1).astype(np.float32)
    i = np.arange(128)[:, None] % W
    j = np.arange(N)[None, :]
    m1 = np.where((j >= i) & (j <= i + W), 0.0, NEG)
    m0 = np.where(j[:, :W] <= i, 0.0, NEG)
    mask = np.concatenate([m1, m0], 1).astype(np.float32)
    return rot, mask, np.eye(128, dtype=np.float32)


def build(nc, x, ctx_768, g_xattn, g_ffn, ln1_g, ln1_b, ln2_g, ln2_b, Wq, bq, Wk, bk, Wv, bv, Wo, bo,
          wqkv, q_scale, k_scale, wo, ln_g, ln_b, w1, b1, w2, b2, rot, mask, ident, out):
    ctx = ExitStack()
    with ctx:
        def sb(name, shape, dt=F32):
            return ctx.enter_context(nc.sbuf_tensor(name, shape, dt))

        def sem(name):
            return ctx.enter_context(nc.semaphore(name))

        def sem2(name):
            return [sem(name + "0"), sem(name + "1")]

        def sb2(name, shape, dt=F32):
            return [sb(name + "0", shape, dt), sb(name + "1", shape, dt)]

        shared = sb("shared", [128, 6 * 2 * INNER])

        class Carve:
            def __init__(self):
                self.at = 0

            def __call__(self, parts, *shape):
                size = int(np.prod(shape))
                v = shared[0:parts, self.at:self.at + size]
                self.at += size
                assert self.at <= shared.shape[1]
                return v.rearrange("p (a b) -> p a b", a=shape[0]) if len(shape) == 2 else v

        idn = sb("idn", [128, 128])
        msk = sb("msk", [128, 192])
        rott = sb("rott", [128, 4, DH])
        ones = sb("ones", [128, 128])
        epst = sb("epst", [128, 1])
        mark_v, mark_g = sb("mark_v", [128, 8]), sb("mark_g", [128, 1])
        backt = sb("backt", [128, 1])
        eps2t = sb("eps2t", [128, 1])
        wq_s, wo_s = sb("wq_s", [D, D]), sb("wo_s", [D, D])
        wk_s, wv_s = sb("wk_s", [DC, D]), sb("wv_s", [DC, D])
        cols = sb("cols", [128, 8])
        bvb, bob = sb("bvb", [128, D]), sb("bob", [128, D])
        gates = sb("gates", [128, 2])
        tg = sb("tg", [128, 2])
        wqkv_raw = sb("wqkv_raw", [D, DEPTH, 3 * INNER])
        wqkv_hi = sb("wqkv_hi", [D, DEPTH * 3 * INNER], F32R)
        wqkv_lo = sb("wqkv_lo", [D, DEPTH * 3 * INNER], F32R)
        wo_raw = sb("wo_raw", [128, DEPTH, PAIRS, D])
        w1_raw = sb("w1_raw", [D, DEPTH, 2 * HID])
        w2_raw = sb("w2_raw", [128, DEPTH, 3, D])
        lgb = sb("lgb", [128, 3, DEPTH])
        b1_raw = sb("b1_raw", [128, DEPTH, 6])
        b1_all = sb("b1_all", [128, DEPTH, 6])
        qks = sb("qks", [128, DEPTH, 2, DH])
        ctab = sb("ctab", [128, DEPTH, 2, DH])
        stab = sb("stab", [128, DEPTH, 2, DH])
        wo_l = sb("wo_l", [128, PAIRS, D])
        w1g = sb("w1g", [D, 2 * HID])
        w1_hi, w1_lo = sb("w1_hi", [D, 2 * HID], F32R), sb("w1_lo", [D, 2 * HID], F32R)
        w2_hi, w2_lo = sb("w2_hi", [128, 3, D], F32R), sb("w2_lo", [128, 3, D], F32R)
        b1_l, b2_l = sb("b1_l", [128, 6]), sb("b2_l", [128, 1])

        xt = sb("xt", [N, B, D])
        ct = sb("ct", [NC, B, DC])
        xs = sb("xs", [D, B, N + 1])
        hn_hi = sb("hn_hi", [D, B, N], F32R)
        hn_lo = sb("hn_lo", [D, B, N], F32R)

        bst = sb("bst", [128, GB, 6])
        cst = sb("cst", [128, GB, 6])
        mv, cmv = sb("mv", [128, GB, 2]), sb("cmv", [128, GB, 2])
        lnv, lnc, r1, rc = (sb(n, [128, GB]) for n in ("lnv", "lnc", "r1", "rc"))
        bst2, mv2 = sb("bst2", [128, GB, 6]), sb("mv2", [128, GB, 2])
        lnv2, r2 = sb("lnv2", [128, GB]), sb("r2", [128, GB])
        cut = Carve()
        zx, zc = cut(N, GB, D), cut(NC, GB, DC)
        x1T, c1T = cut(D, GB * N), cut(DC, GB, NC)
        xqT, xkT, xv = cut(D, GB, N), cut(D, GB, NC), cut(NC, GB, D)
        zo = cut(N, GB, D)
        xp, xpT, xcT = cut(N, GB, NC), cut(NC, GB, N), cut(D, GB, N)
        nmx = sb("nmx", [128, GB])
        nmb = sb("nmb", [128, GB])
        xsum = sb("xsum", [128, GB])
        xri = sb("xri", [128, GB])
        xrt = sb("xrt", [128, GB])

        h_hi, h_lo = sb2("h_hi", [D, N], F32R), sb2("h_lo", [D, N], F32R)
        sqr = sb2("sqr", [N, 2 * INNER])
        ss, ssc, lns, rr = (sb2(n, [N, 2 * HEADS]) for n in ("ss", "ssc", "lns", "rr"))
        cut = Carve()
        (qn0, rs0, rc0), (qn1, rs1_, rc1_) = ([cut(N, 2 * INNER) for _ in range(3)] for _ in range(2))
        qn, rs1, rc1 = (qn0, qn1), (rs0, rs1_), (rc0, rc1_)
        qr = rs1
        qT, kT = sb2("qT", [128, PAIRS, N]), sb2("kT", [128, PAIRS, N])
        vv = sb2("vv", [N, INNER])
        sm1, sm0 = sb2("sm1", [128, PAIRS, 128]), sb2("sm0", [128, PAIRS, W])
        nm = sb2("nm", [128, 8])
        p1, p0 = sb2("p1", [128, PAIRS, 128]), sb2("p0", [128, PAIRS, W])
        psum_ = sb2("psum_", [128, 8])
        pri = sb2("pri", [128, 8])
        pT1, pT0 = sb2("pT1", [128, PAIRS, 128]), sb2("pT0", [W, 2, 2, 128])
        oT = sb2("oT", [128, PAIRS, N])
        dd, dsq, lnl, rstd, hnf = (sb2(n, [D, N]) for n in ("dd", "dsq", "lnl", "rstd", "hnf"))

        cut = Carve()
        gl, uu = cut(128, 3, 512), cut(128, 3, 512)
        u_hi, u_lo = sb("u_hi", [128, 3, 512], F32R), sb("u_lo", [128, 3, 512], F32R)
        cut = Carve()
        stg = [cut(D, GB, N) for _ in range(2)]
        ot = [cut(N, GB, D) for _ in range(2)]

        ps = ctx.enter_context(nc.psum_tensor("ps", [128, 8, 512], F32))
        QB, KB, VB, TQ, TK, S1, S0, OB = range(8)

        block = ctx.enter_context(nc.Block())

        ld_x0, ld_c0, ld_x, ld_c, ld_w, ld_small, ld_b1, ld_st, ld_gate, ld_cols, ld_b, ld_bg, ld_wqkv = (
            sem(n) for n in ("ld_x0", "ld_c0", "ld_x", "ld_c", "ld_w", "ld_small", "ld_b1", "ld_st", "ld_gate",
                             "ld_cols", "ld_b", "ld_bg", "ld_wqkv"))
        cst_v = sem("cst_v")
        cst_g = sem("cst_g")
        tanh_done = sem("tanh_done")
        tab_done = sem("tab_done")
        wsplit = sem("wsplit")
        b1_ps, b1_done = sem("b1_ps"), sem("b1_done")
        xbias = sem("xbias")
        x_st, x_rs, x_z, x_zT, x_1T, x_c1T = (sem(n) for n in ("x_st", "x_rs", "x_z", "x_zT", "x_1T", "x_c1T"))
        x_q_ps, x_k_ps, x_v_ps, x_q, x_k, x_v = (sem(n) for n in ("x_q_ps", "x_k_ps", "x_v_ps", "x_q", "x_k", "x_v"))
        x_s, x_nm, x_p, x_ri, x_pT_ps, x_pT, x_c_ps, x_c, x_y_ps = (
            sem(n) for n in ("x_s", "x_nm", "x_p", "x_ri", "x_pT_ps", "x_pT", "x_c_ps", "x_c", "x_y_ps"))
        x_res, x_st2, x_rs2, x_z2, x_T2, x_out = (sem(n) for n in ("x_res", "x_st2", "x_rs2", "x_z2", "x_T2", "x_out"))
        layer_w = sem("layer_w")
        h_ready, qk_ps, v_ps = (sem2(n) for n in ("h_ready", "qk_ps", "v_ps"))
        h_hi_ok = sem2("h_hi_ok")
        sq_done, ss_sum, ss_ready, ln_done, r_ready = (sem2(n) for n in ("sq_done", "ss_sum", "ss_ready", "ln_done", "r_ready"))
        qn_ready, v_ready, c_ready, s_ready, rot_ready = (sem2(n) for n in ("qn_ready", "v_ready", "c_ready", "s_ready", "rot_ready"))
        rT_ps, qT_ready, kT_ready = (sem2(n) for n in ("rT_ps", "qT_ready", "kT_ready"))
        s_ps, sm_ready, p_done = (sem2(n) for n in ("s_ps", "sm_ready", "p_done"))
        ri_ready, pn_ready, pt_ps, pt_ready = (sem2(n) for n in ("ri_ready", "pn_ready", "pt_ps", "pt_ready"))
        o_ps, oT_ready, y_ps, x_upd = (sem2(n) for n in ("o_ps", "oT_ready", "y_ps", "x_upd"))
        m_ps, d_ready, d2_ready, var_ps, lnl_done, rstd_ready, hnf_ready, hh_ready, hn_ready = (
            sem2(n) for n in ("m_ps", "d_ready", "d2_ready", "var_ps", "lnl_done", "rstd_ready", "hnf_ready", "hh_ready", "hn_ready"))
        g_ps, gl_ready, u_ready, uh_ready, ul_ready, f_acc = (
            [sem(f"{n}{c}") for c in range(3)] for n in ("g_ps", "gl_ready", "u_ready", "uh_ready", "ul_ready", "f_acc"))
        f_ps, f_upd = sem("f_ps"), sem("f_upd")
        st_ready, st_T, ot_ready, stored = (sem2(n) for n in ("st_ready", "st_T", "ot_ready", "stored"))

        class Batch:

            def __init__(self, layer, pair, n):
                self.layer = layer
                self.j = n % 2
                self.g = layer * (B // 2) + pair + n // 2
                self.b = (pair + n // 2) * 2 + self.j

        def pipeline(eng, layer, step, first=-2, between=None):
            def alone(n):
                step(lambda d: Batch(layer, 0, n + d), lambda d: 0 <= n + d < B)

            for n in range(first, 1):
                alone(n)
            with eng.Fori(0, (B - 4) // 2) as pair:
                for n in (1, 2):
                    step(lambda d, n=n: Batch(layer, pair, n + d), lambda d: True)
            for n in range(B - 3, B + 1):
                if n == B - 2 and between:
                    between()
                alone(n)

        def groups(eng, first, both, last):
            first(0)
            with eng.Fori(0, NG - 2) as g:
                both(g, True)
            both(NG - 2, False)
            last(NG - 1)

        def apart(carrier, s, value, k):
            if carrier is nc.gpsimd:
                carrier.wait_ge(s, value)
                carrier.tensor_tensor(mark_g[:], ones[:, 0:1], ones[:, 1:2], ALU.mult)
            else:
                carrier.wait_ge(s, value)
                carrier.memset(mark_v[:, k:k + 1], 0.0)

        def h_of(b):
            return xs[:, bass.ds(b, 1), 0:N].rearrange("p o n -> p (o n)")

        def halves(t, b, nb):
            return t[0:64, bass.ds(b, nb), 0:N], t[64:128, bass.ds(b, nb), 1:N + 1]

        @block.sync
        def _(sp):
            sp.dma_start(xt[:, 0:GB, :], x[0:GB].rearrange("b n d -> n b d")).then_inc(ld_x0, 16)
            sp.dma_start(gates[:, 0:1], g_xattn.rearrange("(o d) -> o d", o=1).partition_broadcast(128)).then_inc(ld_gate, 16)
            sp.dma_start(gates[:, 1:2], g_ffn.rearrange("(o d) -> o d", o=1).partition_broadcast(128)).then_inc(ld_gate, 16)
            sp.dma_start(idn[:], ident).then_inc(ld_st, 16)
            sp.dma_start(wq_s[:], Wq).then_inc(ld_st, 16)
            sp.dma_start(wo_s[:], Wo).then_inc(ld_st, 16)
            sp.dma_start(xt[:, GB:, :], x[GB:].rearrange("b n d -> n b d")).then_inc(ld_x, 16)
            sp.dma_start(wqkv_raw[:], wqkv.rearrange("l d n -> d l n")).then_inc(ld_wqkv, 16)
            sp.dma_start(wo_raw[:], wo.rearrange("l (c p) n -> p l c n", p=128)).then_inc(ld_w, 16)
            sp.dma_start(w1_raw[:], w1.rearrange("l d n -> d l n")).then_inc(ld_w, 16)
            for c, (o, m) in enumerate(CH):
                sp.dma_start(w2_raw[0:m, :, c, :], w2[:, o:o + m, :].rearrange("l p n -> p l n")).then_inc(ld_w, 16)
            for k, v in enumerate((ln_g, ln_b, b2)):
                for l in range(DEPTH):
                    sp.dma_start(lgb[:, k, l:l + 1], v[l:l + 1, :].rearrange("o p -> p o")).then_inc(ld_b, 16)
            for g in range(NG):
                j = g % 2
                sp.wait_ge(ot_ready[j], g // 2 + 1)
                sp.dma_start(out[g * GB:(g + 1) * GB].rearrange("b n d -> n b d"), ot[j][:]).then_inc(stored[j], 16)
            sp.wait_ge(stored[0], 16 * (NG // 2))
            sp.wait_ge(stored[1], 16 * (NG // 2))

        @block.gpsimd
        def _(pool):
            pool.dma_start(ct[:, 0:GB, :], ctx_768[0:GB].rearrange("b n d -> n b d")).then_inc(ld_c0, 16)
            pool.dma_start(wk_s[:], Wk).then_inc(ld_c0, 16)
            pool.dma_start(wv_s[:], Wv).then_inc(ld_c0, 16)
            pool.dma_start(bvb[:], bv.rearrange("(o d) -> o d", o=1).partition_broadcast(128)).then_inc(ld_bg, 16)
            pool.dma_start(bob[:], bo.rearrange("(o d) -> o d", o=1).partition_broadcast(128)).then_inc(ld_bg, 16)
            pool.dma_start(ct[:, GB:, :], ctx_768[GB:].rearrange("b n d -> n b d")).then_inc(ld_c, 16)
            pool.dma_start(rott[:], rot).then_inc(ld_small, 16)
            pool.dma_start(msk[:], mask).then_inc(ld_small, 16)
            pool.dma_start(qks[:, :, 0, :], q_scale.partition_broadcast(128)).then_inc(ld_small, 16)
            pool.dma_start(qks[:, :, 1, :], k_scale.partition_broadcast(128)).then_inc(ld_small, 16)
            T, C = nc.gpsimd.tensor_tensor, nc.gpsimd.tensor_copy
            pool.wait_ge(tanh_done, 1)
            pool.wait_ge(ld_bg, 16 * 2)
            T(bob[:], bob[:], tg[:, 0:1].to_broadcast([128, D]), ALU.mult).then_inc(xbias, 1)
            pool.wait_ge(xbias, 1)

            def add_bias(g):
                pool.wait_ge(x_z, 2 * GB * g + GB)
                xg = xt[:, g * GB:(g + 1) * GB, :]
                T(xg, xg, bob[:].unsqueeze(1).to_broadcast([128, GB, D]), ALU.add).then_inc(cst_g, 1)

            add_bias(0)
            pool.wait_ge(ld_small, 16 * 4)
            for l in range(DEPTH):
                T(ctab[:, l, :, :], rott[:, 0:2, :], qks[:, l, :, :], ALU.mult).then_inc(tab_done, 1)
                for u in range(2):
                    T(stab[:, l, :, u * 32:u * 32 + 32], rott[:, 2:4, u * 32:u * 32 + 32],
                      qks[:, l, :, (1 - u) * 32:(1 - u) * 32 + 32], ALU.mult).then_inc(tab_done, 1)
            pool.wait_ge(wsplit, 1)
            T(wqkv_lo[:], wqkv_raw[:].rearrange("p l n -> p (l n)"), wqkv_hi[:].bitcast(F32), ALU.subtract).then_inc(wsplit, 1)
            add_bias(1)
            for l in range(DEPTH):
                for s in range(2):
                    for c, (o, m) in enumerate(CH):
                        pool.dma_start(b1_raw[0:m, l, s * 3 + c:s * 3 + c + 1],
                                       b1[l:l + 1, s * HID + o:s * HID + o + m].rearrange("o p -> p o")).then_inc(ld_b1, 16)
            for g in range(2, NG):
                add_bias(g)
            pool.wait_ge(tab_done, 6)
            pool.wait_ge(ld_w, 16 * 5)
            pool.wait_ge(ld_b, 16 * 6)
            pool.wait_ge(b1_done, 3)

            def step(at, on):
                if on(2):
                    m = at(2)
                    j = m.j
                    pool.wait_ge(s_ready[j], 4 * m.g + 4)
                    for s in range(2):
                        part = slice(s * INNER, (s + 1) * INNER)
                        pool.wait_ge(c_ready[j], 2 * m.g + s + 1)
                        T(qr[j][:, part], rc1[j][:, part], rs1[j][:, part], ALU.add).then_inc(rot_ready[j], 1)
                if on(1):
                    m = at(1)
                    j = m.j
                    pool.wait_ge(ri_ready[j], m.g + 1)
                    nc.gpsimd.tensor_tensor(p1[j][:], p1[j][:], pri[j][:, 0:4].unsqueeze(2).to_broadcast([128, PAIRS, 128]),
                                            ALU.mult).then_inc(pn_ready[j], 1)
                    nc.gpsimd.tensor_tensor(p0[j][:], p0[j][:], pri[j][:, 4:8].unsqueeze(2).to_broadcast([128, PAIRS, W]),
                                            ALU.mult).then_inc(pn_ready[j], 1)
                if on(3):
                    m = at(3)
                    j, q4 = m.j, qn[m.j][:].rearrange("p (s h u d) -> p s h u d", s=2, h=HEADS, u=2)
                    s4 = rs1[j][:].rearrange("p (s h u d) -> p s h u d", s=2, h=HEADS, u=2)
                    apart(nc.gpsimd, qn_ready[j], m.g + 1, 0)
                    for s in range(2):
                        for u in range(2):
                            tb = stab[:, bass.ds(m.layer, 1), s, u * 32:u * 32 + 32].to_broadcast([128, HEADS, 32])
                            nc.gpsimd.tensor_tensor(s4[:, s, :, u, :], q4[:, s, :, 1 - u, :], tb, ALU.mult).then_inc(s_ready[j], 1)
                if on(1) and not on(0):
                    C(wo_l[:], wo_raw[:, bass.ds(at(1).layer, 1)].rearrange("p o c n -> p (o c) n")).then_inc(layer_w, 1)

            for layer in range(DEPTH):
                def of(t):
                    return t[:, bass.ds(layer, 1)]
                def w1_in():
                    T(w1g[:], of(w1_raw).rearrange("p o n -> p (o n)"), lgb[:, 0, bass.ds(layer, 1)].to_broadcast([128, 2 * HID]),
                      ALU.mult).then_inc(layer_w, 1)
                    apart(nc.gpsimd, layer_w, 12 * layer + 2, 0)
                    C(w1_hi[:], w1g[:]).then_inc(layer_w, 1)

                pipeline(pool, layer, step, -3, w1_in)

                w2_parts = [(o, n, m, w2_raw[0:m, bass.ds(layer, 1), o:o + n, :].rearrange("p o c n -> p (o c) n"))
                            for o, n, m in ((0, 2, 128), (2, 1, CH[2][1]))]
                for o, n, m, raw in w2_parts:
                    C(w2_hi[0:m, o:o + n, :], raw).then_inc(layer_w, 1)
                for c, (o, m) in enumerate(CH):
                    C(b1_l[0:m, c::3], b1_all[0:m, bass.ds(layer, 1), c::3].rearrange("p o n -> p (o n)")).then_inc(layer_w, 1)
                C(b2_l[:], lgb[:, 2, bass.ds(layer, 1)]).then_inc(layer_w, 1)
                pool.wait_ge(layer_w, 12 * layer + 9)
                T(w1_lo[:], w1g[:], w1_hi[:].bitcast(F32), ALU.subtract).then_inc(layer_w, 1)
                for o, n, m, raw in w2_parts:
                    T(w2_lo[0:m, o:o + n, :], raw, w2_hi[0:m, o:o + n, :].bitcast(F32), ALU.subtract).then_inc(layer_w, 1)

                with pool.Fori(0, NG) as g:
                    pool.wait_ge(uh_ready[0], layer * NG + g + 1)
                    T(u_lo[:, 0, :], uu[:, 0, :], u_hi[:, 0, :].bitcast(F32), ALU.subtract).then_inc(ul_ready[0], 1)

        @block.tensor
        def _(pe):
            mm, tr = nc.tensor.matmul, nc.tensor.transpose

            pe.wait_ge(ld_c0, 16 * 3)
            pe.wait_ge(ld_st, 16 * 3)

            def qkv(m, part):
                done = (qk_ps, qk_ps, v_ps)[part]
                whi = wqkv_hi[:, bass.ds(m.layer * 3 * INNER + part * INNER, INNER)]
                wlo = wqkv_lo[:, bass.ds(m.layer * 3 * INNER + part * INNER, INNER)]
                j = m.j
                mm(ps[:, part, :], h_hi[j][:], whi, start=True, stop=False)
                mm(ps[:, part, :], h_hi[j][:], wlo, start=False, stop=False)
                mm(ps[:, part, :], h_lo[j][:], whi, start=False, stop=True).then_inc(done[j], 1)

            def first_qk(layer):
                m = Batch(layer, 0, 0)
                pe.wait_ge(h_ready[m.j], m.g + 1)
                qkv(m, 0)
                qkv(m, 1)

            def tokens_T(g):
                pe.wait_ge(x_z, 2 * GB * g + GB)
                for i in range(GB):
                    last = tr(ps[:, 0, i * 128:i * 128 + 128], zx[:, i, :], idn[:])
                last.then_inc(x_zT, 1)

            def context_T(g):
                pe.wait_ge(x_z, 2 * GB * g + 2 * GB)
                for i in range(GB):
                    last = tr(ps[0:DC, 1, i * NC:(i + 1) * NC], zc[:, i, :], idn[0:NC, 0:NC])
                last.then_inc(x_zT, 1)

            def q_in(g):
                pe.wait_ge(x_1T, g + 1)
                mm(ps[:, 2, :], wq_s[:], x1T[:], start=True, stop=True).then_inc(x_q_ps, 1)

            def k_in(g):
                pe.wait_ge(x_c1T, g + 1)
                mm(ps[:, 3, 0:GB * NC], wk_s[:], c1T[:].rearrange("p b n -> p (b n)"), start=True, stop=True).then_inc(x_k_ps, 1)

            def v_in(g):
                for i in range(GB):
                    last = mm(ps[0:NC, 4, i * D:(i + 1) * D], c1T[:, i, :], wv_s[:], start=True, stop=True)
                last.then_inc(x_v_ps, 1)

            def scores(g):
                pe.wait_ge(x_q, g + 1)
                pe.wait_ge(x_k, g + 1)
                for i in range(GB):
                    last = mm(ps[:, 5, i * NC:(i + 1) * NC], xqT[:, i, :], xkT[:, i, :], start=True, stop=True)
                last.then_inc(x_s, 1)

            def probs_T(g):
                pe.wait_ge(x_p, GB * g + GB)
                for i in range(GB):
                    last = tr(ps[0:NC, 6, i * N:(i + 1) * N], xp[:, i, :], idn[:])
                last.then_inc(x_pT_ps, 1)

            def mix(g):
                pe.wait_ge(x_pT, g + 1)
                pe.wait_ge(x_v, g + 1)
                for i in range(GB):
                    last = mm(ps[:, 7, i * N:(i + 1) * N], xv[:, i, :], xpT[:, i, :], start=True, stop=True)
                last.then_inc(x_c_ps, 1)

            def project(g):
                pe.wait_ge(x_c, g + 1)
                for i in range(GB):
                    last = mm(ps[:, 7, i * D:(i + 1) * D], xcT[:, i, :], wo_s[:], start=True, stop=True)
                last.then_inc(x_y_ps, 1)

            def out_T(g):
                pe.wait_ge(x_z2, GB * g + GB)
                for i in range(GB):
                    last = tr(ps[:, 2, i * N:(i + 1) * N], zo[:, i, :], idn[:])
                last.then_inc(x_T2, 1)

            def first(g):
                tokens_T(g)
                context_T(g)
                q_in(g)
                k_in(g)
                v_in(g)
                scores(g)

            def both(g, _):
                tokens_T(g + 1)
                probs_T(g)
                context_T(g + 1)
                mix(g)
                q_in(g + 1)
                project(g)
                k_in(g + 1)
                v_in(g + 1)
                scores(g + 1)
                out_T(g)

            def last_group(g):
                probs_T(g)
                pe.wait_ge(wsplit, 2)
                first_qk(0)
                mix(g)
                project(g)
                pe.wait_ge(ld_w, 16 * 5)
                pe.wait_ge(ld_b, 16 * 6)
                for l in range(DEPTH):
                    for s in range(2):
                        for c, (o, m) in enumerate(CH):
                            k = l * 6 + s * 3 + c
                            last = mm(ps[0:m, 3, k:k + 1], w1_raw[:, l, s * HID + o:s * HID + o + m], lgb[:, 1, l:l + 1],
                                      start=True, stop=True)
                last.then_inc(b1_ps, 1)
                out_T(g)

            groups(pe, first, both, last_group)

            def hidden(g, c):
                o, m = CH[c]
                hh = hn_hi[:, bass.ds(g * GB, GB), :].rearrange("p b n -> p (b n)")
                hl = hn_lo[:, bass.ds(g * GB, GB), :].rearrange("p b n -> p (b n)")
                for s in range(2):
                    o2 = s * HID + o
                    mm(ps[0:m, 2 * c + s, :], w1_hi[:, o2:o2 + m], hh, start=True, stop=False)
                    mm(ps[0:m, 2 * c + s, :], w1_hi[:, o2:o2 + m], hl, start=False, stop=False)
                    last = mm(ps[0:m, 2 * c + s, :], w1_lo[:, o2:o2 + m], hh, start=False, stop=True)
                last.then_inc(g_ps[c], 1)

            def step(at, on):
                if on(0):
                    m = at(0)
                    j = m.j
                    if on(1):
                        pe.wait_ge(qT_ready[at(1).j], at(1).g + 1)
                        pe.wait_ge(kT_ready[at(1).j], at(1).g + 1)
                    pe.wait_ge(pn_ready[j], 2 * m.g + 2)
                    for c in range(PAIRS):
                        last = tr(ps[:, TQ, c * 128:(c + 1) * 128], p1[j][:, c, :], idn[:])
                    last.then_inc(pt_ps[j], 1)
                    for c in range(2):
                        last = tr(ps[:, TK, c * 128:(c + 1) * 128],
                                  p0[j][:, 2 * c:2 * c + 2, :].rearrange("p a k -> p (a k)"), idn[:])
                    last.then_inc(pt_ps[j], 1)
                if on(1):
                    m = at(1)
                    j = m.j
                    if not on(0):
                        pe.wait_ge(qT_ready[j], m.g + 1)
                        pe.wait_ge(kT_ready[j], m.g + 1)
                        mm(ps[:, TQ, 0:2], idn[:], idn[:, 0:2], start=True, stop=True)
                    for c in range(PAIRS):
                        for a in (0, 64):
                            last = mm(ps[a:a + 64, S1, c * 128:(c + 1) * 128], qT[j][a:a + 64, c, W:N], kT[j][a:a + 64, c, :],
                                      start=True, stop=True)
                    last.then_inc(s_ps[j], 1)
                    for c in range(PAIRS):
                        for a in (0, 64):
                            last = mm(ps[a:a + 64, S0, c * W:(c + 1) * W], qT[j][a:a + 64, c, 0:W], kT[j][a:a + 64, c, 0:W],
                                      start=True, stop=True)
                    last.then_inc(s_ps[j], 1)
                if on(-1):
                    m = at(-1)
                    j = m.j
                    if not on(0):
                        pe.wait_ge(layer_w, 12 * m.layer + 12)
                        hidden(0, 0)
                    pe.wait_ge(x_upd[j], 2 * m.g + 2)
                    mm(ps[:, OB, 0:N], ones[:], h_of(m.b), start=True, stop=True).then_inc(m_ps[j], 1)
                if on(3):
                    m = at(3)
                    pe.wait_ge(h_ready[m.j], m.g + 1)
                    pe.wait_ge(qn_ready[at(2).j], at(2).g + 1)
                    qkv(m, 0)
                if on(3):
                    qkv(at(3), 1)
                if on(-1):
                    m = at(-1)
                    j = m.j
                    if not on(0):
                        hidden(0, 1)
                    pe.wait_ge(d2_ready[j], m.g + 1)
                    mm(ps[:, OB, 0:N], ones[:], dsq[j][:], start=True, stop=True).then_inc(var_ps[j], 1)
                if on(2):
                    if on(1):
                        pe.wait_ge(v_ready[at(1).j], at(1).g + 1)
                    qkv(at(2), 2)
                if on(0):
                    m = at(0)
                    j = m.j
                    pe.wait_ge(pt_ready[j], 3 * m.g + 3)
                    pe.wait_ge(v_ready[j], m.g + 1)
                    if on(-1):
                        pm = at(-1)
                        pe.wait_ge(lnl_done[pm.j], pm.g + 1)

                    def first_window(c):
                        for a in (0, 64):
                            v_h = (2 * c + a // 64) * DH
                            last = mm(ps[a:a + 64, OB, c * 128:c * 128 + W], vv[j][0:W, v_h:v_h + DH],
                                      pT0[j][:, c % 2, c // 2, a:a + 64], start=True, stop=True)
                        return last

                    def second_window(c):
                        for a in (0, 64):
                            v_h = (2 * c + a // 64) * DH
                            mm(ps[a:a + 64, OB, c * 128 + W:(c + 1) * 128], vv[j][:, v_h:v_h + DH], pT1[j][:, c, a:a + 64],
                               start=True, stop=True)

                    for c in range(PAIRS):
                        second_window(c)
                    for c in range(PAIRS):
                        last = first_window(c)
                    last.then_inc(o_ps[j], 1)
                if on(2):
                    m = at(2)
                    j = m.j
                    pe.wait_ge(rot_ready[j], 2 * m.g + 1)
                    for c in range(PAIRS):
                        last = tr(ps[:, TQ, c * 128:(c + 1) * 128], qr[j][:, c * 128:(c + 1) * 128], idn[:])
                    last.then_inc(rT_ps[j], 1)
                    pe.wait_ge(rot_ready[j], 2 * m.g + 2)
                    for c in range(PAIRS):
                        last = tr(ps[:, TK, c * 128:(c + 1) * 128], qr[j][:, INNER + c * 128:INNER + (c + 1) * 128], idn[:])
                    last.then_inc(rT_ps[j], 1)
                if on(0):
                    m = at(0)
                    j = m.j
                    if not on(-1):
                        pe.wait_ge(layer_w, 12 * m.layer + 1)
                    pe.wait_ge(oT_ready[j], m.g + 1)
                    for c in range(PAIRS):
                        last = mm(ps[:, OB, 0:N], wo_l[:, c, :], oT[j][:, c, :], start=(c == 0), stop=(c == PAIRS - 1))
                    last.then_inc(y_ps[j], 1)

            def back(gl_, c):
                o, m = CH[c]
                pe.wait_ge(ul_ready[c], gl_ + 1)
                if c == 0:
                    pe.wait_ge(f_upd, 2 * gl_ + 2)
                mm(ps[:, 6, :], w2_hi[0:m, c, :], u_hi[0:m, c, :], start=(c == 0), stop=False)
                mm(ps[:, 6, :], w2_hi[0:m, c, :], u_lo[0:m, c, :], start=False, stop=False)
                last = mm(ps[:, 6, :], w2_lo[0:m, c, :], u_hi[0:m, c, :], start=False, stop=(c == 2))
                last.then_inc(f_acc[c], 1)

            for layer in range(DEPTH):
                pipeline(pe, layer, step)
                with pe.Fori(0, NG - 1) as g:
                    gl_ = layer * NG + g
                    hidden(g, 2)
                    back(gl_, 0)
                    pe.wait_ge(hn_ready[1], (B // 2) * (layer + 1))
                    pe.wait_ge(u_ready[0], gl_ + 1)
                    hidden(g + 1, 0)
                    back(gl_, 1)
                    pe.wait_ge(u_ready[1], gl_ + 1)
                    hidden(g + 1, 1)
                    back(gl_, 2)
                    pe.wait_ge(u_ready[2], gl_ + 1)
                gl_ = layer * NG + NG - 1
                hidden(NG - 1, 2)
                back(gl_, 0)
                back(gl_, 1)
                if layer + 1 < DEPTH:
                    first_qk(layer + 1)
                back(gl_, 2)

            for g in range(NG):
                j = g % 2
                pe.wait_ge(st_ready[j], 2 * (g // 2) + 2)
                if g >= 2:
                    pe.wait_ge(ot_ready[j], g // 2)
                for i in range(GB):
                    last = tr(ps[:, j, i * 128:(i + 1) * 128], stg[j][:, i, :], idn[:])
                last.then_inc(st_T[j], 1)

        @block.scalar
        def _(act):
            A = nc.scalar.activation
            for k, (v, n) in enumerate(((ln1_g, D), (ln1_b, D), (ln2_g, DC), (ln2_b, DC), (bq, D), (bk, D))):
                act.dma_start(cols[0:n, k:k + 1], v.rearrange("(p o) -> p o", o=1)).then_inc(ld_cols, 16)
            act.wait_ge(ld_gate, 16 * 2)
            A(tg[:], gates[:], ACT.Tanh).then_inc(tanh_done, 1)
            nc.scalar.preload_act_table_set("natural_log_exp_and_others")
            act.wait_ge(cst_v, 5)

            def squares(m, s):
                act.wait_ge(qk_ps[m.j], 2 * m.g + s + 1)
                A(sqr[m.j][:, s * INNER:(s + 1) * INNER], ps[:, s, :], ACT.Square).then_inc(sq_done[m.j], 1)

            def norms_ln(m):
                act.wait_ge(ss_ready[m.j], m.g + 1)
                A(lns[m.j][:], ssc[m.j][:], ACT.Ln, scale=LN_SCALE).then_inc(ln_done[m.j], 1)

            def norms_exp(m):
                act.wait_ge(ln_done[m.j], m.g + 1)
                A(rr[m.j][:], lns[m.j][:], ACT.Exp, scale=-0.5, bias=backt[:]).then_inc(r_ready[m.j], 1)

            def norms(g):
                act.wait_ge(x_st, 16 * g + 16)
                A(lnv[:], mv[:, :, 1], ACT.Ln, bias=eps2t[:], scale=1.0 + EPS).then_inc(x_rs, 1)
                A(lnc[0:NC, :], cmv[0:NC, :, 1], ACT.Ln, bias=epst[0:NC, :]).then_inc(x_rs, 1)
                act.wait_ge(x_rs, 4 * g + 2)
                A(r1[:], lnv[:], ACT.Exp, scale=-0.5).then_inc(x_rs, 1)
                A(rc[0:NC, :], lnc[0:NC, :], ACT.Exp, scale=-0.5).then_inc(x_rs, 1)

            def q_out(g):
                act.wait_ge(x_q_ps, g + 1)
                A(xqT[:].rearrange("p b n -> p (b n)"), ps[:, 2, :], ACT.Identity, bias=cols[:, 4:5]).then_inc(x_q, 1)

            def exps(g):
                act.wait_ge(x_nm, 2 * g + 2)
                for i in range(GB):
                    A(xp[:, i, :], ps[:, 5, i * NC:(i + 1) * NC], ACT.Exp, bias=nmb[:, i:i + 1], scale=float(D) ** -0.5,
                      accum_out=xsum[:, i:i + 1]).then_inc(x_p, 1)

            def mixed(g):
                act.wait_ge(x_c_ps, g + 1)
                A(xcT[:].rearrange("p b n -> p (b n)"), ps[:, 7, :], ACT.Copy).then_inc(x_c, 1)

            def norm_out(g):
                act.wait_ge(x_st2, 2 * GB * g + 2 * GB)
                A(lnv2[:], mv2[:, :, 1], ACT.Ln, bias=epst[:]).then_inc(x_rs2, 1)
                act.wait_ge(x_rs2, 2 * g + 1)
                A(r2[:], lnv2[:], ACT.Exp, scale=-0.5).then_inc(x_rs2, 1)

            def results(g):
                act.wait_ge(x_T2, g + 1)
                lo, hi = halves(xs, g * GB, GB)
                A(lo, ps[0:64, 2, :].rearrange("p (b n) -> p b n", b=GB), ACT.Copy).then_inc(x_out, 1)
                A(hi, ps[64:128, 2, :].rearrange("p (b n) -> p b n", b=GB), ACT.Copy).then_inc(x_out, 1)

            def probs_T(g):
                act.wait_ge(x_pT_ps, g + 1)
                A(xpT[:].rearrange("p b n -> p (b n)"), ps[0:NC, 6, :], ACT.Copy).then_inc(x_pT, 1)

            def context_affine(g):
                act.wait_ge(x_zT, 2 * g + 2)
                A(c1T[:].rearrange("p b n -> p (b n)"), ps[0:DC, 1, 0:GB * NC], ACT.Identity, scale=cols[0:DC, 2:3],
                  bias=cols[0:DC, 3:4]).then_inc(x_c1T, 1)

            def k_out(g):
                act.wait_ge(x_k_ps, g + 1)
                A(xkT[:].rearrange("p b n -> p (b n)"), ps[:, 3, 0:GB * NC], ACT.Identity, bias=cols[:, 5:6]).then_inc(x_k, 1)

            def first(g):
                norms(g)
                act.wait_ge(ld_cols, 16 * 6)
                context_affine(g)
                q_out(g)
                k_out(g)
                exps(g)
                norms(g + 1)
                act.wait_ge(ld_wqkv, 16)
                A(wqkv_hi[:], wqkv_raw[:].rearrange("p l n -> p (l n)"), ACT.Copy).then_inc(wsplit, 1)

            def both(g, more):
                probs_T(g)
                context_affine(g + 1)
                mixed(g)
                q_out(g + 1)
                k_out(g + 1)
                if more:
                    norms(g + 2)
                norm_out(g)
                exps(g + 1)
                results(g)

            def last_group(g):
                probs_T(g)
                squares(Batch(0, 0, 0), 0)
                squares(Batch(0, 0, 0), 1)
                mixed(g)
                norms_ln(Batch(0, 0, 0))
                norms_exp(Batch(0, 0, 0))
                norm_out(g)
                results(g)

            groups(act, first, both, last_group)

            def step(at, on):
                if on(0):
                    m = at(0)
                    j = m.j
                    act.wait_ge(pt_ps[j], 2 * m.g + 1)
                    A(pT1[j][:].rearrange("p c n -> p (c n)"), ps[:, TQ, :], ACT.Copy).then_inc(pt_ready[j], 1)
                    act.wait_ge(pt_ps[j], 2 * m.g + 2)
                    for u in range(2):
                        A(pT0[j][:, u, :, :].rearrange("p c n -> p (c n)"), ps[u * W:(u + 1) * W, TK, 0:256],
                          ACT.Copy).then_inc(pt_ready[j], 1)
                if on(1):
                    m = at(1)
                    j = m.j
                    for c in range(PAIRS):
                        act.wait_ge(sm_ready[j], 8 * m.g + c + 1)
                        A(p1[j][:, c, :], sm1[j][:, c, :], ACT.Exp, bias=nm[j][:, c:c + 1], scale=-1.0,
                          accum_out=psum_[j][:, c:c + 1]).then_inc(p_done[j], 1)
                if on(3):
                    squares(at(3), 0)
                if on(3):
                    squares(at(3), 1)
                if on(-1):
                    m = at(-1)
                    j = m.j
                    act.wait_ge(var_ps[j], m.g + 1)
                    A(lnl[j][:], ps[:, OB, 0:N], ACT.Ln, bias=epst[:]).then_inc(lnl_done[j], 1)
                if on(1):
                    m = at(1)
                    j = m.j
                    for c in range(PAIRS):
                        act.wait_ge(sm_ready[j], 8 * m.g + 4 + c + 1)
                        A(p0[j][:, c, :], sm0[j][:, c, :], ACT.Exp, bias=nm[j][:, 4 + c:5 + c], scale=-1.0,
                          accum_out=psum_[j][:, 4 + c:5 + c]).then_inc(p_done[j], 1)
                if on(3):
                    norms_ln(at(3))
                if on(-1):
                    m = at(-1)
                    j = m.j
                    act.wait_ge(lnl_done[j], m.g + 1)
                    A(rstd[j][:], lnl[j][:], ACT.Exp, scale=-0.5).then_inc(rstd_ready[j], 1)
                if on(3):
                    norms_exp(at(3))
                if on(0):
                    m = at(0)
                    j = m.j
                    act.wait_ge(o_ps[j], m.g + 1)
                    A(oT[j][:].rearrange("p c n -> p (c n)"), ps[:, OB, :], ACT.Copy).then_inc(oT_ready[j], 1)
                if on(2):
                    m = at(2)
                    j = m.j
                    act.wait_ge(rT_ps[j], 2 * m.g + 1)
                    A(qT[j][:].rearrange("p c n -> p (c n)"), ps[:, TQ, :], ACT.Copy).then_inc(qT_ready[j], 1)
                    act.wait_ge(rT_ps[j], 2 * m.g + 2)
                    A(kT[j][:].rearrange("p c n -> p (c n)"), ps[:, TK, :], ACT.Copy).then_inc(kT_ready[j], 1)
                    act.wait_ge(v_ps[j], m.g + 1)
                    A(vv[j][:], ps[:, VB, :], ACT.Copy).then_inc(v_ready[j], 1)

            for layer in range(DEPTH):
                pipeline(act, layer, step)

                nc.scalar.preload_act_table_set("gelu_and_others")

                def chunk(gl_, c):
                    o, m = CH[c]
                    act.wait_ge(g_ps[c], gl_ + 1)
                    A(gl[0:m, c, :], ps[0:m, 2 * c + 1, :], ACT.Gelu, bias=b1_l[0:m, 3 + c:4 + c]).then_inc(gl_ready[c], 1)

                def split(gl_, c):
                    o, m = CH[c]
                    act.wait_ge(u_ready[c], gl_ + 1)
                    A(u_hi[0:m, c, :], uu[0:m, c, :], ACT.Copy).then_inc(uh_ready[c], 1)

                chunk(layer * NG, 0)
                chunk(layer * NG, 1)
                split(layer * NG, 0)
                with act.Fori(0, NG - 1) as g:
                    gl_ = layer * NG + g
                    chunk(gl_, 2)
                    split(gl_, 1)
                    chunk(gl_ + 1, 0)
                    split(gl_, 2)
                    chunk(gl_ + 1, 1)
                    split(gl_ + 1, 0)
                gl_ = layer * NG + NG - 1
                chunk(gl_, 2)
                split(gl_, 1)
                split(gl_, 2)
                nc.scalar.preload_act_table_set("natural_log_exp_and_others")
                if layer + 1 < DEPTH:
                    m = Batch(layer + 1, 0, 0)
                    squares(m, 0)
                    squares(m, 1)
                    norms_ln(m)
                    norms_exp(m)

            for g in range(NG):
                j = g % 2
                lo, hi = halves(xs, g * GB, GB)
                act.wait_ge(f_upd, 2 * NG * (DEPTH - 1) + 2 * g + 4)
                if g >= 2:
                    act.wait_ge(st_T[j], g // 2)
                A(stg[j][0:64, :, :], lo, ACT.Copy).then_inc(st_ready[j], 1)
                A(stg[j][64:128, :, :], hi, ACT.Copy).then_inc(st_ready[j], 1)

        @block.vector
        def _(dve):
            V = nc.vector
            V.memset(ones[:], 1.0 / D).then_inc(cst_v, 1)
            V.memset(epst[:], EPS).then_inc(cst_v, 1)
            V.memset(mark_v[:, 7:8], 0.0).then_inc(f_upd, 2)
            V.memset(backt[:], LN_BACK).then_inc(cst_v, 1)
            V.memset(xs[64:128, :, 0:1], 0.0).then_inc(cst_v, 1)
            V.memset(eps2t[:], EPS * EPS).then_inc(cst_v, 1)

            def row(t, b):
                return t[:, bass.ds(b, 1), :].rearrange("p o d -> p (o d)")

            def head_in(m):
                j = m.j
                V.tensor_copy(h_hi[j][:], h_of(m.b)).then_inc(h_hi_ok[j], 1)
                dve.wait_ge(h_hi_ok[j], m.g + 1)
                V.tensor_tensor(h_lo[j][:], h_of(m.b), h_hi[j][:].bitcast(F32), ALU.subtract).then_inc(h_ready[j], 1)

            def squared_norms(m):
                dve.wait_ge(sq_done[m.j], 2 * m.g + 2)
                V.tensor_reduce(ss[m.j][:], sqr[m.j][:].rearrange("p (h d) -> p h d", d=DH), AX.X, ALU.add).then_inc(ss_sum[m.j], 1)
                dve.wait_ge(ss_sum[m.j], m.g + 1)
                V.tensor_scalar(ssc[m.j][:], ss[m.j][:], 1e-24, None, ALU.max).then_inc(ss_ready[m.j], 1)

            def over_norms(m):
                dve.wait_ge(r_ready[m.j], m.g + 1)
                V.tensor_tensor(qn[m.j].rearrange("p (h d) -> p h d", d=DH), ps[:, QB:KB + 1, :].rearrange("p s (h d) -> p (s h) d", d=DH),
                                rr[m.j][:].unsqueeze(2).to_broadcast([128, 2 * HEADS, DH]), ALU.mult).then_inc(qn_ready[m.j], 1)

            def stats(g):
                for i in range(GB):
                    V.bn_stats(bst[:, i, :], row(xt, g * GB + i)).then_inc(x_st, 1)
                    V.bn_stats(cst[0:NC, i, :], row(ct, g * GB + i)).then_inc(x_st, 1)
                apart(V, x_st, 16 * g + 8, 2)
                for i in range(GB):
                    V.bn_aggr(mv[:, i, :], bst[:, i, :]).then_inc(x_st, 1)
                    V.bn_aggr(cmv[0:NC, i, :], cst[0:NC, i, :]).then_inc(x_st, 1)

            def normed(g):
                dve.wait_ge(x_st, 16 * g + 16)
                dve.wait_ge(x_rs, 4 * g + 4)
                for i in range(GB):
                    V.tensor_scalar(zx[:, i, :], row(xt, g * GB + i), mv[:, i, 0:1], r1[:, i:i + 1],
                                    ALU.subtract, ALU.mult).then_inc(x_z, 1)
                for i in range(GB):
                    V.tensor_scalar(zc[:, i, :], row(ct, g * GB + i), cmv[0:NC, i, 0:1], rc[0:NC, i:i + 1],
                                    ALU.subtract, ALU.mult).then_inc(x_z, 1)

            def affine(g):
                dve.wait_ge(x_zT, 2 * g + 1)
                V.tensor_scalar(x1T[:], ps[:, 0, :], cols[:, 0:1], cols[:, 1:2], ALU.mult, ALU.add).then_inc(x_1T, 1)

            def v_out(g):
                dve.wait_ge(x_v_ps, g + 1)
                V.tensor_tensor(xv[:], ps[0:NC, 4, :].rearrange("p (b d) -> p b d", b=GB),
                                bvb[0:NC, :].unsqueeze(1).to_broadcast([NC, GB, D]), ALU.add).then_inc(x_v, 1)

            def maxima(g):
                dve.wait_ge(x_s, g + 1)
                V.tensor_reduce(nmx[:], ps[:, 5, 0:GB * NC].rearrange("p (b n) -> p b n", b=GB), AX.X, ALU.max).then_inc(x_nm, 1)
                dve.wait_ge(x_nm, 2 * g + 1)
                V.tensor_scalar(nmb[:], nmx[:], -float(D) ** -0.5, None, ALU.mult).then_inc(x_nm, 1)

            def sums(g):
                dve.wait_ge(x_p, GB * g + GB)
                V.reciprocal(xri[:], xsum[:]).then_inc(x_ri, 1)
                dve.wait_ge(x_ri, 2 * g + 1)
                V.tensor_scalar(xrt[:], xri[:], tg[:, 0:1], None, ALU.mult).then_inc(x_ri, 1)

            def residual(g):
                dve.wait_ge(x_ri, 2 * g + 2)
                dve.wait_ge(cst_g, g + 1)
                dve.wait_ge(x_y_ps, g + 1)
                for i in range(GB):
                    V.scalar_tensor_tensor(out=row(xt, g * GB + i), in0=ps[:, 7, i * D:(i + 1) * D], scalar=xrt[:, i:i + 1],
                                           in1=row(xt, g * GB + i), op0=ALU.mult, op1=ALU.add).then_inc(x_res, 1)
                apart(V, x_res, GB * g + GB, 3)
                for i in range(GB):
                    V.bn_stats(bst2[:, i, :], row(xt, g * GB + i)).then_inc(x_st2, 1)
                apart(V, x_st2, 2 * GB * g + GB, 4)
                for i in range(GB):
                    V.bn_aggr(mv2[:, i, :], bst2[:, i, :]).then_inc(x_st2, 1)

            def stack_in(g):
                dve.wait_ge(x_st2, 2 * GB * g + 2 * GB)
                dve.wait_ge(x_rs2, 2 * g + 2)
                for i in range(GB):
                    V.tensor_scalar(zo[:, i, :], row(xt, g * GB + i), mv2[:, i, 0:1], r2[:, i:i + 1],
                                    ALU.subtract, ALU.mult).then_inc(x_z2, 1)

            def first(g):
                dve.wait_ge(ld_x0, 16)
                dve.wait_ge(ld_c0, 16 * 3)
                stats(g)
                normed(g)
                dve.wait_ge(ld_cols, 16 * 6)
                affine(g)
                dve.wait_ge(ld_bg, 16 * 2)
                v_out(g)
                maxima(g)
                dve.wait_ge(ld_x, 16)
                dve.wait_ge(ld_c, 16)
                stats(g + 1)

            def both(g, more):
                normed(g + 1)
                affine(g + 1)
                sums(g)
                if more:
                    stats(g + 2)
                residual(g)
                v_out(g + 1)
                maxima(g + 1)
                stack_in(g)

            def last_group(g):
                m = Batch(0, 0, 0)
                dve.wait_ge(x_out, 2)
                head_in(m)
                sums(g)
                squared_norms(m)
                residual(g)
                over_norms(m)
                stack_in(g)

            groups(dve, first, both, last_group)

            dve.wait_ge(ld_b1, 16 * 12)
            dve.wait_ge(b1_ps, 1)
            for c, (o, m) in enumerate(CH):
                V.tensor_tensor(b1_all[0:m, :, c::3], ps[0:m, 3, 0:12].rearrange("p (l s c) -> p l s c", l=2, s=2)[:, :, :, c],
                                b1_raw[0:m, :, c::3], ALU.add).then_inc(b1_done, 1)

            def cosine(m, s):
                part = slice(s * INNER, (s + 1) * INNER)
                V.tensor_tensor(rc1[m.j][:, part].rearrange("p (h d) -> p h d", h=HEADS),
                                qn[m.j][:, part].rearrange("p (h d) -> p h d", h=HEADS),
                                ctab[:, bass.ds(m.layer, 1), s, :].to_broadcast([128, HEADS, DH]), ALU.mult).then_inc(c_ready[m.j], 1)

            def step(at, on):
                if on(-1):
                    m = at(-1)
                    j = m.j
                    dve.wait_ge(y_ps[j], m.g + 1)
                    for t, q in zip(halves(xs, m.b, 1), (0, 64)):
                        t = t.rearrange("p o n -> p (o n)")
                        V.tensor_tensor(t, ps[q:q + 64, OB, 0:N], t, ALU.add).then_inc(x_upd[j], 1)
                if on(3):
                    if on(1):
                        dve.wait_ge(v_ps[at(1).j], at(1).g + 1)
                    head_in(at(3))
                if on(2):
                    m = at(2)
                    dve.wait_ge(qn_ready[m.j], m.g + 1)
                    cosine(m, 0)
                if on(1):
                    m = at(1)
                    j = m.j
                    apart(V, s_ps[j], 2 * m.g + 1, 0)
                    for c in range(PAIRS):
                        V.tensor_tensor_reduce(out=sm1[j][:, c, :], in0=ps[:, S1, c * 128:(c + 1) * 128], in1=msk[:, 0:128],
                                               scale=-1.0, scalar=3e38, op0=ALU.add, op1=ALU.min,
                                               accum_out=nm[j][:, c:c + 1]).then_inc(sm_ready[j], 1)
                    apart(V, s_ps[j], 2 * m.g + 2, 1)
                    for c in range(PAIRS):
                        V.tensor_tensor_reduce(out=sm0[j][:, c, :], in0=ps[:, S0, c * W:(c + 1) * W], in1=msk[:, 128:192],
                                               scale=-1.0, scalar=3e38, op0=ALU.add, op1=ALU.min,
                                               accum_out=nm[j][:, 4 + c:5 + c]).then_inc(sm_ready[j], 1)
                if on(-1):
                    m = at(-1)
                    j = m.j
                    dve.wait_ge(m_ps[j], m.g + 1)
                    V.tensor_tensor(dd[j][:], h_of(m.b), ps[:, OB, 0:N], ALU.subtract).then_inc(d_ready[j], 1)
                    dve.wait_ge(d_ready[j], m.g + 1)
                    V.tensor_tensor(dsq[j][:], dd[j][:], dd[j][:], ALU.mult).then_inc(d2_ready[j], 1)
                if on(2):
                    m = at(2)
                    cosine(m, 1)
                if on(3):
                    squared_norms(at(3))
                if on(1):
                    m = at(1)
                    j = m.j
                    dve.wait_ge(p_done[j], 8 * m.g + 8)
                    V.reciprocal(pri[j][:], psum_[j][:]).then_inc(ri_ready[j], 1)
                if on(-1):
                    m = at(-1)
                    j = m.j
                    dve.wait_ge(rstd_ready[j], m.g + 1)
                    V.tensor_tensor(hnf[j][:], dd[j][:], rstd[j][:], ALU.mult).then_inc(hnf_ready[j], 1)
                if on(3):
                    over_norms(at(3))
                if on(-1):
                    m = at(-1)
                    j = m.j
                    hh = hn_hi[:, bass.ds(m.b, 1), :].rearrange("p o n -> p (o n)")
                    hl = hn_lo[:, bass.ds(m.b, 1), :].rearrange("p o n -> p (o n)")
                    dve.wait_ge(hnf_ready[j], m.g + 1)
                    V.tensor_copy(hh, hnf[j][:]).then_inc(hh_ready[j], 1)
                    dve.wait_ge(hh_ready[j], m.g + 1)
                    V.tensor_tensor(hl, hnf[j][:], hh.bitcast(F32), ALU.subtract).then_inc(hn_ready[j], 1)

            dve.wait_ge(x_out, 2 * NG)
            dve.wait_ge(ld_small, 16 * 4)
            dve.wait_ge(tab_done, 6)
            for layer in range(DEPTH):
                pipeline(dve, layer, step)

                def gate(gl_, c):
                    o, m = CH[c]
                    dve.wait_ge(gl_ready[c], gl_ + 1)
                    V.scalar_tensor_tensor(out=uu[0:m, c, :], in0=ps[0:m, 2 * c, :], scalar=b1_l[0:m, c:c + 1], in1=gl[0:m, c, :],
                                           op0=ALU.add, op1=ALU.mult).then_inc(u_ready[c], 1)

                def low(gl_, c):
                    o, m = CH[c]
                    dve.wait_ge(uh_ready[c], gl_ + 1)
                    V.tensor_tensor(u_lo[0:m, c, :], uu[0:m, c, :], u_hi[0:m, c, :].bitcast(F32), ALU.subtract).then_inc(ul_ready[c], 1)

                def update(g, gl_):
                    dve.wait_ge(f_acc[2], gl_ + 1)
                    for t, q in zip(halves(xs, g * GB, GB), (0, 64)):
                        V.scalar_tensor_tensor(out=t, in0=ps[q:q + 64, 6, :].rearrange("p (b n) -> p b n", b=GB),
                                               scalar=b2_l[q:q + 64, :], in1=t, op0=ALU.add, op1=ALU.add).then_inc(f_upd, 1)

                gate(layer * NG, 0)
                gate(layer * NG, 1)
                with dve.Fori(0, NG - 1) as g:
                    gl_ = layer * NG + g
                    gate(gl_, 2)
                    low(gl_, 1)
                    gate(gl_ + 1, 0)
                    low(gl_, 2)
                    gate(gl_ + 1, 1)
                    update(g, gl_)
                gl_ = layer * NG + NG - 1
                gate(gl_, 2)
                low(gl_, 1)
                if layer + 1 < DEPTH:
                    dve.wait_ge(f_upd, 2 * NG * layer + 4)
                    head_in(Batch(layer + 1, 0, 0))
                low(gl_, 2)
                update(NG - 1, gl_)
                dve.wait_ge(f_upd, 2 * NG * layer + 2 * NG + 2)
                if layer + 1 < DEPTH:
                    squared_norms(Batch(layer + 1, 0, 0))
                    over_norms(Batch(layer + 1, 0, 0))

            for g in range(NG):
                j = g % 2
                dve.wait_ge(st_T[j], g // 2 + 1)
                if g >= 2:
                    dve.wait_ge(stored[j], 16 * (g // 2))
                V.scalar_tensor_tensor(out=ot[j][:].rearrange("p b n -> p (b n)"), in0=ps[:, j, :], scalar=tg[:, 1:2],
                                       in1=xt[:, g * GB:(g + 1) * GB, :].rearrange("p b n -> p (b n)"),
                                       op0=ALU.mult, op1=ALU.add).then_inc(ot_ready[j], 1)


_INS = ["x", "ctx_768", "g_xattn", "g_ffn"] + ["L0_xattn_" + n for n in (
    "ln1_g", "ln1_b", "ln2_g", "ln2_b", "Wq", "bq", "Wk", "bk", "Wv", "bv", "Wo", "bo")] + ["L0_ffn_" + n for n in (
    "wqkv", "q_scale", "k_scale", "wo", "ln_g", "ln_b", "w1", "b1", "w2", "b2")]


def kernel(**inputs):
    import concourse.bacc as _bacc
    from concourse.bass_utils import run_bass_kernel_spmd as _run

    nc = _bacc.Bacc("TRN2", target_bir_lowering=False, num_devices=1)
    given = {n: np.ascontiguousarray(inputs[n]) for n in _INS}
    given |= dict(zip(("rot_table", "window_masks", "identity"), tables()))
    arrays, args = {}, []
    for name, a in given.items():
        arrays[f"in_{name}_dram"] = a
        args.append(nc.dram_tensor(f"in_{name}_dram", a.shape, mybir.dt.from_np(a.dtype), kind="ExternalInput").ap())
    args.append(nc.dram_tensor("out_0_dram", (B, N, D), F32, kind="ExternalOutput").ap())
    build(nc, *args)
    r = _run(nc, [arrays], core_ids=[0])
    return r.results[0]["out_0_dram"]
```

```python
from contextlib import ExitStack

import numpy as np

import concourse.bass as bass
from concourse import mybir

F32 = mybir.dt.float32
F32R = mybir.dt.float32r
ALU = mybir.AluOpType
ACT = mybir.ActivationFunctionType
AX = mybir.AxisListType

B, N, D = 16, 128, 128
NC, DC = 120, 96
HEADS, DH, W = 8, 64, 64
INNER = HEADS * DH
PAIRS = HEADS // 2
DEPTH = 2
HID = int(D * 4 * 2 / 3)
CH = [(0, 128), (128, 128), (256, HID - 256)]
GB = 4
NG = B // GB
EPS = 1e-5
NEG = -1e30
LN_SCALE = 2.0 ** 16
LN_BACK = 8.0 * float(np.log(2.0))


def tables():
    half = np.arange(0, DH, 2, dtype=np.float32)
    inv = (np.float32(1.0) / np.power(np.float32(10000.0), half / np.float32(DH))).astype(np.float32)
    t = np.arange(N, dtype=np.float32)
    fr = (t[:, None] * inv[None, :]).astype(np.float32)
    fr = np.concatenate([fr, fr], -1)
    base = ((half + np.float32(0.4 * DH)) / np.float32(1.4 * DH)).astype(np.float32)
    power = ((t - N // 2) / np.float32(W // 2)).astype(np.float32)
    sc = np.power(base[None, :].astype(np.float64), power[:, None])
    sc = np.concatenate([sc, sc], -1)
    cos, sin = np.cos(fr.astype(np.float64)), np.sin(fr.astype(np.float64))
    sgn = np.concatenate([-np.ones(DH // 2), np.ones(DH // 2)])[None, :]
    cq, sq = cos * sc * 8.0, sin * sc * 8.0 * sgn
    ck, sk = cos / sc, sin / sc * sgn
    rot = np.stack([cq, ck, sq, sk], 1).astype(np.float32)
    i = np.arange(128)[:, None] % W
    j = np.arange(N)[None, :]
    m1 = np.where((j >= i) & (j <= i + W), 0.0, NEG)
    m0 = np.where(j[:, :W] <= i, 0.0, NEG)
    mask = np.concatenate([m1, m0], 1).astype(np.float32)
    return rot, mask, np.eye(128, dtype=np.float32)


def build(nc, x, ctx_768, g_xattn, g_ffn, ln1_g, ln1_b, ln2_g, ln2_b, Wq, bq, Wk, bk, Wv, bv, Wo, bo,
          wqkv, q_scale, k_scale, wo, ln_g, ln_b, w1, b1, w2, b2, rot, mask, ident, out):
    ctx = ExitStack()
    with ctx:
        def sb(name, shape, dt=F32):
            return ctx.enter_context(nc.sbuf_tensor(name, shape, dt))

        def sem(name):
            return ctx.enter_context(nc.semaphore(name))

        def sem2(name):
            return [sem(name + "0"), sem(name + "1")]

        def sb2(name, shape, dt=F32):
            return [sb(name + "0", shape, dt), sb(name + "1", shape, dt)]

        shared = sb("shared", [128, 6 * 2 * INNER])

        class Carve:
            def __init__(self):
                self.at = 0

            def __call__(self, parts, *shape):
                size = int(np.prod(shape))
                v = shared[0:parts, self.at:self.at + size]
                self.at += size
                assert self.at <= shared.shape[1]
                return v.rearrange("p (a b) -> p a b", a=shape[0]) if len(shape) == 2 else v

        idn = sb("idn", [128, 128])
        msk = sb("msk", [128, 192])
        rott = sb("rott", [128, 4, DH])
        ones = sb("ones", [128, 128])
        epst = sb("epst", [128, 1])
        mark_v, mark_g = sb("mark_v", [128, 8]), sb("mark_g", [128, 1])
        backt = sb("backt", [128, 1])
        eps2t = sb("eps2t", [128, 1])
        wq_s, wo_s = sb("wq_s", [D, D]), sb("wo_s", [D, D])
        wk_s, wv_s = sb("wk_s", [DC, D]), sb("wv_s", [DC, D])
        cols = sb("cols", [128, 8])
        bvb, bob = sb("bvb", [128, D]), sb("bob", [128, D])
        gates = sb("gates", [128, 2])
        tg = sb("tg", [128, 2])
        wqkv_raw = sb("wqkv_raw", [D, DEPTH, 3 * INNER])
        wqkv_hi = sb("wqkv_hi", [D, DEPTH * 3 * INNER], F32R)
        wqkv_lo = sb("wqkv_lo", [D, DEPTH * 3 * INNER], F32R)
        wo_raw = sb("wo_raw", [128, DEPTH, PAIRS, D])
        w1_raw = sb("w1_raw", [D, DEPTH, 2 * HID])
        w2_raw = sb("w2_raw", [128, DEPTH, 3, D])
        lgb = sb("lgb", [128, 3, DEPTH])
        b1_raw = sb("b1_raw", [128, DEPTH, 6])
        b1_all = sb("b1_all", [128, DEPTH, 6])
        qks = sb("qks", [128, DEPTH, 2, DH])
        ctab = sb("ctab", [128, DEPTH, 2, DH])
        stab = sb("stab", [128, DEPTH, 2, DH])
        wo_l = sb("wo_l", [128, PAIRS, D])
        w1g = sb("w1g", [D, 2 * HID])
        w1_hi, w1_lo = sb("w1_hi", [D, 2 * HID], F32R), sb("w1_lo", [D, 2 * HID], F32R)
        w2_hi, w2_lo = sb("w2_hi", [128, 3, D], F32R), sb("w2_lo", [128, 3, D], F32R)
        b1_l, b2_l = sb("b1_l", [128, 6]), sb("b2_l", [128, 1])

        xt = sb("xt", [N, B, D])
        ct = sb("ct", [NC, B, DC])
        xs = sb("xs", [D, B, N + 1])
        hn_hi = sb("hn_hi", [D, B, N], F32R)
        hn_lo = sb("hn_lo", [D, B, N], F32R)

        bst = sb("bst", [128, GB, 6])
        cst = sb("cst", [128, GB, 6])
        mv, cmv = sb("mv", [128, GB, 2]), sb("cmv", [128, GB, 2])
        lnv, lnc, r1, rc = (sb(n, [128, GB]) for n in ("lnv", "lnc", "r1", "rc"))
        bst2, mv2 = sb("bst2", [128, GB, 6]), sb("mv2", [128, GB, 2])
        lnv2, r2 = sb("lnv2", [128, GB]), sb("r2", [128, GB])
        cut = Carve()
        zx, zc = cut(N, GB, D), cut(NC, GB, DC)
        x1T, c1T = cut(D, GB * N), cut(DC, GB, NC)
        xqT, xkT, xv = cut(D, GB, N), cut(D, GB, NC), cut(NC, GB, D)
        xp, xpT, xcT = cut(N, GB, NC), cut(NC, GB, N), cut(D, GB, N)
        nmx = sb("nmx", [128, GB])
        nmb = sb("nmb", [128, GB])
        xsum = sb("xsum", [128, GB])
        xri = sb("xri", [128, GB])
        xrt = sb("xrt", [128, GB])

        h_hi, h_lo = sb2("h_hi", [D, N], F32R), sb2("h_lo", [D, N], F32R)
        sqr = sb2("sqr", [N, 2 * INNER])
        ss, ssc, lns, rr = (sb2(n, [N, 2 * HEADS]) for n in ("ss", "ssc", "lns", "rr"))
        cut = Carve()
        (qn0, rs0, rc0), (qn1, rs1_, rc1_) = ([cut(N, 2 * INNER) for _ in range(3)] for _ in range(2))
        qn, rs1, rc1 = (qn0, qn1), (rs0, rs1_), (rc0, rc1_)
        qr = rs1
        qT, kT = sb2("qT", [128, PAIRS, N]), sb2("kT", [128, PAIRS, N])
        vv = sb2("vv", [N, INNER])
        sm1, sm0 = sb2("sm1", [128, PAIRS, 128]), sb2("sm0", [128, PAIRS, W])
        zo = sm1[1]
        nm = sb2("nm", [128, 8])
        p1, p0 = sb2("p1", [128, PAIRS, 128]), sb2("p0", [128, PAIRS, W])
        psum_ = sb2("psum_", [128, 8])
        pri = sb2("pri", [128, 8])
        pT1, pT0 = sb2("pT1", [128, PAIRS, 128]), sb2("pT0", [W, 2, 2, 128])
        oT = sb2("oT", [128, PAIRS, N])
        dd, dsq, lnl, rstd, hnf = (sb2(n, [D, N]) for n in ("dd", "dsq", "lnl", "rstd", "hnf"))

        cut = Carve()
        gl, uu = cut(128, 3, 512), cut(128, 3, 512)
        u_hi, u_lo = sb("u_hi", [128, 3, 512], F32R), sb("u_lo", [128, 3, 512], F32R)
        stg = [cut(D, GB, N) for _ in range(2)]
        ot = [cut(N, GB, D) for _ in range(NG)]

        ps = ctx.enter_context(nc.psum_tensor("ps", [128, 8, 512], F32))
        QB, KB, VB, TQ, TK, S1, S0, OB = range(8)
        FB, FB_LAST = 6, 7
        MEAN, VAR = slice(PAIRS * W, PAIRS * W + N), slice(PAIRS * W + N, PAIRS * W + 2 * N)

        block = ctx.enter_context(nc.Block())

        ld_x0, ld_c0, ld_x1, ld_x, ld_c, ld_w, ld_small, ld_b1, ld_st, ld_gate, ld_cols, ld_b, ld_bg, ld_wqkv = (
            sem(n) for n in ("ld_x0", "ld_c0", "ld_x1", "ld_x", "ld_c", "ld_w", "ld_small", "ld_b1", "ld_st", "ld_gate",
                             "ld_cols", "ld_b", "ld_bg", "ld_wqkv"))
        cst_v = sem("cst_v")
        cst_g = sem("cst_g")
        tanh_done = sem("tanh_done")
        tab_done = sem("tab_done")
        wsplit = sem("wsplit")
        b1_ps, b1_done = sem("b1_ps"), sem("b1_done")
        xbias = sem("xbias")
        x_st, x_rs, x_z, x_zT, x_1T, x_c1T = (sem(n) for n in ("x_st", "x_rs", "x_z", "x_zT", "x_1T", "x_c1T"))
        x_q_ps, x_k_ps, x_v_ps, x_q, x_k, x_v = (sem(n) for n in ("x_q_ps", "x_k_ps", "x_v_ps", "x_q", "x_k", "x_v"))
        x_s, x_nm, x_p, x_ri, x_pT_ps, x_pT, x_c_ps, x_c, x_y_ps = (
            sem(n) for n in ("x_s", "x_nm", "x_p", "x_ri", "x_pT_ps", "x_pT", "x_c_ps", "x_c", "x_y_ps"))
        x_res, x_st2, x_rs2, x_z2, x_T2, x_out = (sem(n) for n in ("x_res", "x_st2", "x_rs2", "x_z2", "x_T2", "x_out"))
        layer_w = sem("layer_w")
        layer_w1 = sem("layer_w1")
        h_ready, qk_ps, v_ps = (sem2(n) for n in ("h_ready", "qk_ps", "v_ps"))
        h_hi_ok = sem2("h_hi_ok")
        sq_done, ss_sum, ss_ready, ln_done, r_ready = (sem2(n) for n in ("sq_done", "ss_sum", "ss_ready", "ln_done", "r_ready"))
        qn_ready, v_ready, c_ready, s_ready, rot_ready = (sem2(n) for n in ("qn_ready", "v_ready", "c_ready", "s_ready", "rot_ready"))
        rT_ps, qT_ready, kT_ready = (sem2(n) for n in ("rT_ps", "qT_ready", "kT_ready"))
        s_ps, sm_ready, p_done = (sem2(n) for n in ("s_ps", "sm_ready", "p_done"))
        ri_ready, pn_ready, pt_ps, pt_ready = (sem2(n) for n in ("ri_ready", "pn_ready", "pt_ps", "pt_ready"))
        o_ps, oT_ready, y_ps, x_upd = (sem2(n) for n in ("o_ps", "oT_ready", "y_ps", "x_upd"))
        m_ps, d_ready, d2_ready, var_ps, lnl_done, rstd_ready, hnf_ready, hh_ready, hn_ready = (
            sem2(n) for n in ("m_ps", "d_ready", "d2_ready", "var_ps", "lnl_done", "rstd_ready", "hnf_ready", "hh_ready", "hn_ready"))
        g_ps, gl_ready, u_ready, uh_ready, ul_ready, f_acc = (
            [sem(f"{n}{c}") for c in range(3)] for n in ("g_ps", "gl_ready", "u_ready", "uh_ready", "ul_ready", "f_acc"))
        f_ps, f_upd = sem("f_ps"), sem("f_upd")
        st_ready, st_T, ot_ready = (sem2(n) for n in ("st_ready", "st_T", "ot_ready"))
        stored = sem("stored")

        class Batch:

            def __init__(self, layer, pair, n):
                self.layer = layer
                self.j = n % 2
                self.g = layer * (B // 2) + pair + n // 2
                self.b = (pair + n // 2) * 2 + self.j

        def pipeline(eng, layer, step, first=-2, before={}):
            def alone(n):
                step(lambda d: Batch(layer, 0, n + d), lambda d: 0 <= n + d < B)

            for n in range(first, 2):
                before.get(n, lambda: None)()
                alone(n)
            with eng.Fori(0, (B - 6) // 2) as pair:
                for n in (2, 3):
                    step(lambda d, n=n: Batch(layer, pair, n + d), lambda d: True)
            for n in range(B - 4, B + 2):
                before.get(n, lambda: None)()
                alone(n)

        def groups(eng, first, both, last):
            first(0)
            with eng.Fori(0, NG - 2) as g:
                both(g, True)
            both(NG - 2, False)
            last(NG - 1)

        def apart(carrier, s, value, k):
            if carrier is nc.gpsimd:
                carrier.wait_ge(s, value)
                carrier.tensor_tensor(mark_g[:], ones[:, 0:1], ones[:, 1:2], ALU.mult)
            else:
                carrier.wait_ge(s, value)
                carrier.memset(mark_v[:, k:k + 1], 0.0)

        def h_of(b):
            return xs[:, bass.ds(b, 1), 0:N].rearrange("p o n -> p (o n)")

        def halves(t, b, nb):
            return t[0:64, bass.ds(b, nb), 0:N], t[64:128, bass.ds(b, nb), 1:N + 1]

        @block.sync
        def _(sp):
            sp.dma_start(xt[:, 0:GB, :], x[0:GB].rearrange("b n d -> n b d")).then_inc(ld_x0, 16)
            sp.dma_start(gates[:, 0:1], g_xattn.rearrange("(o d) -> o d", o=1).partition_broadcast(128)).then_inc(ld_gate, 16)
            sp.dma_start(gates[:, 1:2], g_ffn.rearrange("(o d) -> o d", o=1).partition_broadcast(128)).then_inc(ld_gate, 16)
            sp.dma_start(idn[:], ident).then_inc(ld_st, 16)
            sp.dma_start(wq_s[:], Wq).then_inc(ld_st, 16)
            sp.dma_start(wo_s[:], Wo).then_inc(ld_st, 16)
            sp.dma_start(xt[:, GB:2 * GB, :], x[GB:2 * GB].rearrange("b n d -> n b d")).then_inc(ld_x1, 16)
            sp.dma_start(ct[:, GB:2 * GB, :], ctx_768[GB:2 * GB].rearrange("b n d -> n b d")).then_inc(ld_x1, 16)
            sp.dma_start(xt[:, 2 * GB:, :], x[2 * GB:].rearrange("b n d -> n b d")).then_inc(ld_x, 16)
            sp.dma_start(wqkv_raw[:], wqkv.rearrange("l d n -> d l n")).then_inc(ld_wqkv, 16)
            sp.dma_start(wo_raw[:], wo.rearrange("l (c p) n -> p l c n", p=128)).then_inc(ld_w, 16)
            sp.dma_start(w1_raw[:], w1.rearrange("l d n -> d l n")).then_inc(ld_w, 16)
            for c, (o, m) in enumerate(CH):
                sp.dma_start(w2_raw[0:m, :, c, :], w2[:, o:o + m, :].rearrange("l p n -> p l n")).then_inc(ld_w, 16)
            for k, v in enumerate((ln_g, ln_b, b2)):
                for l in range(DEPTH):
                    sp.dma_start(lgb[:, k, l:l + 1], v[l:l + 1, :].rearrange("o p -> p o")).then_inc(ld_b, 16)
            for g in range(NG):
                j = g % 2
                sp.wait_ge(ot_ready[j], g // 2 + 1)
                sp.dma_start(out[g * GB:(g + 1) * GB].rearrange("b n d -> n b d"), ot[g][:]).then_inc(stored, 16)
            sp.wait_ge(stored, 16 * NG)

        @block.gpsimd
        def _(pool):
            pool.dma_start(ct[:, 0:GB, :], ctx_768[0:GB].rearrange("b n d -> n b d")).then_inc(ld_c0, 16)
            pool.dma_start(wk_s[:], Wk).then_inc(ld_c0, 16)
            pool.dma_start(wv_s[:], Wv).then_inc(ld_c0, 16)
            pool.dma_start(bvb[:], bv.rearrange("(o d) -> o d", o=1).partition_broadcast(128)).then_inc(ld_bg, 16)
            pool.dma_start(bob[:], bo.rearrange("(o d) -> o d", o=1).partition_broadcast(128)).then_inc(ld_bg, 16)
            pool.dma_start(ct[:, 2 * GB:, :], ctx_768[2 * GB:].rearrange("b n d -> n b d")).then_inc(ld_c, 16)
            pool.dma_start(rott[:], rot).then_inc(ld_small, 16)
            pool.dma_start(msk[:], mask).then_inc(ld_small, 16)
            pool.dma_start(qks[:, :, 0, :], q_scale.partition_broadcast(128)).then_inc(ld_small, 16)
            pool.dma_start(qks[:, :, 1, :], k_scale.partition_broadcast(128)).then_inc(ld_small, 16)
            T, C = nc.gpsimd.tensor_tensor, nc.gpsimd.tensor_copy
            pool.wait_ge(tanh_done, 1)
            pool.wait_ge(ld_bg, 16 * 2)
            T(bob[:], bob[:], tg[:, 0:1].to_broadcast([128, D]), ALU.mult).then_inc(xbias, 1)
            pool.wait_ge(xbias, 1)

            def add_bias(g):
                pool.wait_ge(x_z, 2 * GB * g + GB)
                xg = xt[:, g * GB:(g + 1) * GB, :]
                T(xg, xg, bob[:].unsqueeze(1).to_broadcast([128, GB, D]), ALU.add).then_inc(cst_g, 1)

            add_bias(0)
            pool.wait_ge(ld_small, 16 * 4)
            for l in range(DEPTH):
                T(ctab[:, l, :, :], rott[:, 0:2, :], qks[:, l, :, :], ALU.mult).then_inc(tab_done, 1)
                for u in range(2):
                    T(stab[:, l, :, u * 32:u * 32 + 32], rott[:, 2:4, u * 32:u * 32 + 32],
                      qks[:, l, :, (1 - u) * 32:(1 - u) * 32 + 32], ALU.mult).then_inc(tab_done, 1)
            pool.wait_ge(wsplit, 1)
            T(wqkv_lo[:], wqkv_raw[:].rearrange("p l n -> p (l n)"), wqkv_hi[:].bitcast(F32), ALU.subtract).then_inc(wsplit, 1)
            add_bias(1)
            for l in range(DEPTH):
                for s in range(2):
                    for c, (o, m) in enumerate(CH):
                        pool.dma_start(b1_raw[0:m, l, s * 3 + c:s * 3 + c + 1],
                                       b1[l:l + 1, s * HID + o:s * HID + o + m].rearrange("o p -> p o")).then_inc(ld_b1, 16)
            for g in range(2, NG):
                add_bias(g)
            pool.wait_ge(tab_done, 6)
            pool.wait_ge(ld_w, 16 * 5)
            pool.wait_ge(ld_b, 16 * 6)

            def step(at, on):
                if on(2):
                    m = at(2)
                    j = m.j
                    pool.wait_ge(s_ready[j], 4 * m.g + 4)
                    for s in range(2):
                        part = slice(s * INNER, (s + 1) * INNER)
                        pool.wait_ge(c_ready[j], 2 * m.g + s + 1)
                        T(qr[j][:, part], rc1[j][:, part], rs1[j][:, part], ALU.add).then_inc(rot_ready[j], 1)
                if on(1):
                    m = at(1)
                    j = m.j
                    pool.wait_ge(ri_ready[j], m.g + 1)
                    nc.gpsimd.tensor_tensor(p1[j][:], p1[j][:], pri[j][:, 0:4].unsqueeze(2).to_broadcast([128, PAIRS, 128]),
                                            ALU.mult).then_inc(pn_ready[j], 1)
                    nc.gpsimd.tensor_tensor(p0[j][:], p0[j][:], pri[j][:, 4:8].unsqueeze(2).to_broadcast([128, PAIRS, W]),
                                            ALU.mult).then_inc(pn_ready[j], 1)
                if on(3):
                    m = at(3)
                    j, q4 = m.j, qn[m.j][:].rearrange("p (s h u d) -> p s h u d", s=2, h=HEADS, u=2)
                    s4 = rs1[j][:].rearrange("p (s h u d) -> p s h u d", s=2, h=HEADS, u=2)
                    apart(nc.gpsimd, qn_ready[j], m.g + 1, 0)
                    for s in range(2):
                        for u in range(2):
                            tb = stab[:, bass.ds(m.layer, 1), s, u * 32:u * 32 + 32].to_broadcast([128, HEADS, 32])
                            nc.gpsimd.tensor_tensor(s4[:, s, :, u, :], q4[:, s, :, 1 - u, :], tb, ALU.mult).then_inc(s_ready[j], 1)

            for layer in range(DEPTH):
                def of(t):
                    return t[:, bass.ds(layer, 1)]
                C(wo_l[:], wo_raw[:, layer]).then_inc(layer_w, 1)

                pipeline(pool, layer, step, -3)

                pool.wait_ge(b1_done, 3)
                w2_parts = [(o, n, m, w2_raw[0:m, bass.ds(layer, 1), o:o + n, :].rearrange("p o c n -> p (o c) n"))
                            for o, n, m in ((0, 2, 128), (2, 1, CH[2][1]))]
                for o, n, m, raw in w2_parts:
                    C(w2_hi[0:m, o:o + n, :], raw).then_inc(layer_w, 1)
                for c, (o, m) in enumerate(CH):
                    C(b1_l[0:m, c::3], b1_all[0:m, bass.ds(layer, 1), c::3].rearrange("p o n -> p (o n)")).then_inc(layer_w, 1)
                C(b2_l[:], lgb[:, 2, bass.ds(layer, 1)]).then_inc(layer_w, 1)
                pool.wait_ge(layer_w, 9 * layer + 7)
                for o, n, m, raw in w2_parts:
                    T(w2_lo[0:m, o:o + n, :], raw, w2_hi[0:m, o:o + n, :].bitcast(F32), ALU.subtract).then_inc(layer_w, 1)

                with pool.Fori(1, NG) as g:
                    pool.wait_ge(uh_ready[0], layer * NG + g + 1)
                    T(u_lo[:, 0, :], uu[:, 0, :], u_hi[:, 0, :].bitcast(F32), ALU.subtract).then_inc(ul_ready[0], 1)

        @block.tensor
        def _(pe):
            mm, tr = nc.tensor.matmul, nc.tensor.transpose

            pe.wait_ge(ld_c0, 16 * 3)
            pe.wait_ge(ld_st, 16 * 3)

            def qkv(m, part):
                done = (qk_ps, qk_ps, v_ps)[part]
                whi = wqkv_hi[:, bass.ds(m.layer * 3 * INNER + part * INNER, INNER)]
                wlo = wqkv_lo[:, bass.ds(m.layer * 3 * INNER + part * INNER, INNER)]
                j = m.j
                mm(ps[:, part, :], h_hi[j][:], whi, start=True, stop=False)
                mm(ps[:, part, :], h_hi[j][:], wlo, start=False, stop=False)
                mm(ps[:, part, :], h_lo[j][:], whi, start=False, stop=True).then_inc(done[j], 1)

            def first_qk(layer):
                m = Batch(layer, 0, 0)
                pe.wait_ge(h_ready[m.j], m.g + 1)
                qkv(m, 0)
                qkv(m, 1)

            def tokens_T(g):
                pe.wait_ge(x_z, 2 * GB * g + GB)
                for i in range(GB):
                    last = tr(ps[:, 0, i * 128:i * 128 + 128], zx[:, i, :], idn[:])
                last.then_inc(x_zT, 1)

            def context_T(g):
                pe.wait_ge(x_z, 2 * GB * g + 2 * GB)
                for i in range(GB):
                    last = tr(ps[0:DC, 1, i * NC:(i + 1) * NC], zc[:, i, :], idn[0:NC, 0:NC])
                last.then_inc(x_zT, 1)

            def q_in(g):
                pe.wait_ge(x_1T, g + 1)
                mm(ps[:, 2, :], wq_s[:], x1T[:], start=True, stop=True).then_inc(x_q_ps, 1)

            def k_in(g):
                pe.wait_ge(x_c1T, g + 1)
                mm(ps[:, 3, 0:GB * NC], wk_s[:], c1T[:].rearrange("p b n -> p (b n)"), start=True, stop=True).then_inc(x_k_ps, 1)

            def v_in(g):
                for i in range(GB):
                    last = mm(ps[0:NC, 4, i * D:(i + 1) * D], c1T[:, i, :], wv_s[:], start=True, stop=True)
                last.then_inc(x_v_ps, 1)

            def scores(g):
                pe.wait_ge(x_q, g + 1)
                pe.wait_ge(x_k, g + 1)
                for i in range(GB):
                    last = mm(ps[:, 5, i * NC:(i + 1) * NC], xqT[:, i, :], xkT[:, i, :], start=True, stop=True)
                last.then_inc(x_s, 1)

            def probs_T(g):
                pe.wait_ge(x_p, GB * g + GB)
                for i in range(GB):
                    last = tr(ps[0:NC, 6, i * N:(i + 1) * N], xp[:, i, :], idn[:])
                last.then_inc(x_pT_ps, 1)

            def mix(g):
                pe.wait_ge(x_pT, g + 1)
                pe.wait_ge(x_v, g + 1)
                for i in range(GB):
                    last = mm(ps[:, 7, i * N:(i + 1) * N], xv[:, i, :], xpT[:, i, :], start=True, stop=True)
                last.then_inc(x_c_ps, 1)

            def project(g):
                pe.wait_ge(x_c, g + 1)
                for i in range(GB):
                    last = mm(ps[:, 7, i * D:(i + 1) * D], xcT[:, i, :], wo_s[:], start=True, stop=True)
                last.then_inc(x_y_ps, 1)

            def out_T(g):
                pe.wait_ge(x_z2, GB * g + GB)
                for i in range(GB):
                    last = tr(ps[:, 7, i * N:(i + 1) * N], zo[:, i, :], idn[:])
                last.then_inc(x_T2, 1)

            def first(g):
                tokens_T(g)
                context_T(g)
                q_in(g)
                k_in(g)
                v_in(g)
                scores(g)

            def both(g, _):
                tokens_T(g + 1)
                probs_T(g)
                context_T(g + 1)
                mix(g)
                q_in(g + 1)
                project(g)
                k_in(g + 1)
                v_in(g + 1)
                scores(g + 1)
                out_T(g)

            def last_group(g):
                probs_T(g)
                pe.wait_ge(wsplit, 2)
                first_qk(0)
                mix(g)
                project(g)
                pe.wait_ge(ld_w, 16 * 5)
                pe.wait_ge(ld_b, 16 * 6)
                for l in range(DEPTH):
                    for s in range(2):
                        for c, (o, m) in enumerate(CH):
                            k = l * 6 + s * 3 + c
                            last = mm(ps[0:m, 3, k:k + 1], w1_raw[:, l, s * HID + o:s * HID + o + m], lgb[:, 1, l:l + 1],
                                      start=True, stop=True)
                last.then_inc(b1_ps, 1)

            groups(pe, first, both, last_group)

            def hidden(g, c, halves_=(0, 1)):
                o, m = CH[c]
                hh = hn_hi[:, bass.ds(g * GB, GB), :].rearrange("p b n -> p (b n)")
                hl = hn_lo[:, bass.ds(g * GB, GB), :].rearrange("p b n -> p (b n)")
                for s in halves_:
                    o2 = s * HID + o
                    mm(ps[0:m, 2 * c + s, :], w1_hi[:, o2:o2 + m], hh, start=True, stop=False)
                    mm(ps[0:m, 2 * c + s, :], w1_hi[:, o2:o2 + m], hl, start=False, stop=False)
                    last = mm(ps[0:m, 2 * c + s, :], w1_lo[:, o2:o2 + m], hh, start=False, stop=True)
                if 1 in halves_:
                    last.then_inc(g_ps[c], 1)

            def step(at, on):
                if on(0):
                    m = at(0)
                    j = m.j
                    if on(1):
                        pe.wait_ge(qT_ready[at(1).j], at(1).g + 1)
                        pe.wait_ge(kT_ready[at(1).j], at(1).g + 1)
                    pe.wait_ge(pn_ready[j], 2 * m.g + 2)
                    for c in range(PAIRS):
                        last = tr(ps[:, TQ, c * 128:(c + 1) * 128], p1[j][:, c, :], idn[:])
                    last.then_inc(pt_ps[j], 1)
                    if on(-2):
                        pe.wait_ge(lnl_done[at(-2).j], at(-2).g + 1)
                    for c in range(2):
                        last = tr(ps[:, TK, c * 128:(c + 1) * 128],
                                  p0[j][:, 2 * c:2 * c + 2, :].rearrange("p a k -> p (a k)"), idn[:])
                    last.then_inc(pt_ps[j], 1)
                if on(1):
                    m = at(1)
                    j = m.j
                    if not on(0):
                        pe.wait_ge(qT_ready[j], m.g + 1)
                        pe.wait_ge(kT_ready[j], m.g + 1)
                        mm(ps[:, TQ, 0:2], idn[:], idn[:, 0:2], start=True, stop=True)
                    for c in range(PAIRS):
                        for a in (0, 64):
                            last = mm(ps[a:a + 64, S1, c * 128:(c + 1) * 128], qT[j][a:a + 64, c, W:N], kT[j][a:a + 64, c, :],
                                      start=True, stop=True)
                    last.then_inc(s_ps[j], 1)
                    for c in range(PAIRS):
                        for a in (0, 64):
                            last = mm(ps[a:a + 64, S0, c * W:(c + 1) * W], qT[j][a:a + 64, c, 0:W], kT[j][a:a + 64, c, 0:W],
                                      start=True, stop=True)
                    last.then_inc(s_ps[j], 1)
                if on(3):
                    m = at(3)
                    pe.wait_ge(h_ready[m.j], m.g + 1)
                    pe.wait_ge(qn_ready[at(2).j], at(2).g + 1)
                    qkv(m, 0)
                if on(3):
                    qkv(at(3), 1)
                if on(-1):
                    m = at(-1)
                    j = m.j
                    pe.wait_ge(x_upd[j], 2 * m.g + 2)
                    if on(-2) and not on(0):
                        pm = at(-2)
                        pe.wait_ge(lnl_done[pm.j], pm.g + 1)
                    if on(1):
                        pe.wait_ge(sm_ready[at(1).j], 8 * at(1).g + 8)
                    mm(ps[:, S0, MEAN], ones[:], h_of(m.b), start=True, stop=True).then_inc(m_ps[j], 1)
                if on(1) and not on(2):
                    pe.wait_ge(layer_w1, 3 * at(1).layer + 3)
                    hidden(0, 0)
                if on(0) and not on(1):
                    hidden(0, 1, [0])
                if on(-1) and not on(0):
                    hidden(0, 2, [0])
                if on(2):
                    if on(1):
                        pe.wait_ge(v_ready[at(1).j], at(1).g + 1)
                    qkv(at(2), 2)
                if on(0):
                    m = at(0)
                    j = m.j
                    pe.wait_ge(pt_ready[j], 3 * m.g + 3)
                    pe.wait_ge(v_ready[j], m.g + 1)

                    def first_window(c):
                        for a in (0, 64):
                            v_h = (2 * c + a // 64) * DH
                            last = mm(ps[a:a + 64, OB, c * 128:c * 128 + W], vv[j][0:W, v_h:v_h + DH],
                                      pT0[j][:, c % 2, c // 2, a:a + 64], start=True, stop=True)
                        return last

                    def second_window(c):
                        for a in (0, 64):
                            v_h = (2 * c + a // 64) * DH
                            mm(ps[a:a + 64, OB, c * 128 + W:(c + 1) * 128], vv[j][:, v_h:v_h + DH], pT1[j][:, c, a:a + 64],
                               start=True, stop=True)

                    for c in range(PAIRS):
                        second_window(c)
                    for c in range(PAIRS):
                        last = first_window(c)
                    last.then_inc(o_ps[j], 1)
                if on(-1):
                    m = at(-1)
                    j = m.j
                    pe.wait_ge(d2_ready[j], m.g + 1)
                    mm(ps[:, S0, VAR], ones[:], dsq[j][:], start=True, stop=True).then_inc(var_ps[j], 1)
                if on(2):
                    m = at(2)
                    j = m.j
                    pe.wait_ge(rot_ready[j], 2 * m.g + 1)
                    for c in range(PAIRS):
                        last = tr(ps[:, TQ, c * 128:(c + 1) * 128], qr[j][:, c * 128:(c + 1) * 128], idn[:])
                    last.then_inc(rT_ps[j], 1)
                    pe.wait_ge(rot_ready[j], 2 * m.g + 2)
                    for c in range(PAIRS):
                        last = tr(ps[:, TK, c * 128:(c + 1) * 128], qr[j][:, INNER + c * 128:INNER + (c + 1) * 128], idn[:])
                    last.then_inc(rT_ps[j], 1)
                if on(0) and not on(1):
                    hidden(0, 1, [1])
                if on(0):
                    m = at(0)
                    j = m.j
                    if not on(-1):
                        pe.wait_ge(layer_w, 9 * m.layer + 1)
                    pe.wait_ge(oT_ready[j], m.g + 1)
                    for c in range(PAIRS):
                        last = mm(ps[:, OB, 0:N], wo_l[:, c, :], oT[j][:, c, :], start=(c == 0), stop=(c == PAIRS - 1))
                    last.then_inc(y_ps[j], 1)

            def back(gl_, c, bank):
                o, m = CH[c]
                pe.wait_ge(ul_ready[c], gl_ + 1)
                if c == 0 and bank == FB:
                    pe.wait_ge(f_upd, 2 * gl_ + 2)
                mm(ps[:, bank, :], w2_hi[0:m, c, :], u_hi[0:m, c, :], start=(c == 0), stop=False)
                mm(ps[:, bank, :], w2_hi[0:m, c, :], u_lo[0:m, c, :], start=False, stop=False)
                last = mm(ps[:, bank, :], w2_lo[0:m, c, :], u_hi[0:m, c, :], start=False, stop=(c == 2))
                last.then_inc(f_acc[c], 1)

            def final_T(g):
                j = g % 2
                pe.wait_ge(st_ready[j], 2 * (g // 2) + 2)
                if g >= 2:
                    pe.wait_ge(ot_ready[j], g // 2)
                for i in range(GB):
                    last = tr(ps[:, j, i * 128:(i + 1) * 128], stg[j][:, i, :], idn[:])
                last.then_inc(st_T[j], 1)

            for layer in range(DEPTH):
                pipeline(pe, layer, step, before={-1: lambda: out_T(NG - 1)} if layer == 0 else {})
                hidden(0, 2, [1])
                pe.wait_ge(layer_w, 9 * layer + 9)
                with pe.Fori(0, NG - 1) as g:
                    gl_ = layer * NG + g
                    pe.wait_ge(hn_ready[1], (B // 2) * (layer + 1))
                    pe.wait_ge(u_ready[0], gl_ + 1)
                    hidden(g + 1, 0)
                    back(gl_, 0, FB)
                    back(gl_, 1, FB)
                    pe.wait_ge(u_ready[1], gl_ + 1)
                    hidden(g + 1, 1)
                    back(gl_, 2, FB)
                    pe.wait_ge(u_ready[2], gl_ + 1)
                    hidden(g + 1, 2)
                gl_ = layer * NG + NG - 1
                back(gl_, 0, FB_LAST)
                back(gl_, 1, FB_LAST)
                if layer + 1 < DEPTH:
                    first_qk(layer + 1)
                else:
                    final_T(0)
                back(gl_, 2, FB_LAST)
            for g in range(1, NG):
                final_T(g)

        @block.scalar
        def _(act):
            A = nc.scalar.activation
            for k, (v, n) in enumerate(((ln1_g, D), (ln1_b, D), (ln2_g, DC), (ln2_b, DC), (bq, D), (bk, D))):
                act.dma_start(cols[0:n, k:k + 1], v.rearrange("(p o) -> p o", o=1)).then_inc(ld_cols, 16)
            act.wait_ge(ld_gate, 16 * 2)
            A(tg[:], gates[:], ACT.Tanh).then_inc(tanh_done, 1)
            nc.scalar.preload_act_table_set("natural_log_exp_and_others")
            act.wait_ge(cst_v, 5)

            def squares(m, s):
                act.wait_ge(qk_ps[m.j], 2 * m.g + s + 1)
                A(sqr[m.j][:, s * INNER:(s + 1) * INNER], ps[:, s, :], ACT.Square).then_inc(sq_done[m.j], 1)

            def norms_ln(m):
                act.wait_ge(ss_ready[m.j], m.g + 1)
                A(lns[m.j][:], ssc[m.j][:], ACT.Ln, scale=LN_SCALE).then_inc(ln_done[m.j], 1)

            def norms_exp(m):
                act.wait_ge(ln_done[m.j], m.g + 1)
                A(rr[m.j][:], lns[m.j][:], ACT.Exp, scale=-0.5, bias=backt[:]).then_inc(r_ready[m.j], 1)

            def norms(g):
                act.wait_ge(x_st, 16 * g + 16)
                A(lnv[:], mv[:, :, 1], ACT.Ln, bias=eps2t[:], scale=1.0 + EPS).then_inc(x_rs, 1)
                A(lnc[0:NC, :], cmv[0:NC, :, 1], ACT.Ln, bias=epst[0:NC, :]).then_inc(x_rs, 1)
                act.wait_ge(x_rs, 4 * g + 2)
                A(r1[:], lnv[:], ACT.Exp, scale=-0.5).then_inc(x_rs, 1)
                A(rc[0:NC, :], lnc[0:NC, :], ACT.Exp, scale=-0.5).then_inc(x_rs, 1)

            def q_out(g):
                act.wait_ge(x_q_ps, g + 1)
                A(xqT[:].rearrange("p b n -> p (b n)"), ps[:, 2, :], ACT.Identity, bias=cols[:, 4:5]).then_inc(x_q, 1)

            def exps(g):
                act.wait_ge(x_nm, 2 * g + 2)
                for i in range(GB):
                    A(xp[:, i, :], ps[:, 5, i * NC:(i + 1) * NC], ACT.Exp, bias=nmb[:, i:i + 1], scale=float(D) ** -0.5,
                      accum_out=xsum[:, i:i + 1]).then_inc(x_p, 1)

            def mixed(g):
                act.wait_ge(x_c_ps, g + 1)
                A(xcT[:].rearrange("p b n -> p (b n)"), ps[:, 7, :], ACT.Copy).then_inc(x_c, 1)

            def norm_out(g):
                act.wait_ge(x_st2, 2 * GB * g + 2 * GB)
                A(lnv2[:], mv2[:, :, 1], ACT.Ln, bias=epst[:]).then_inc(x_rs2, 1)
                act.wait_ge(x_rs2, 2 * g + 1)
                A(r2[:], lnv2[:], ACT.Exp, scale=-0.5).then_inc(x_rs2, 1)

            def results(g):
                act.wait_ge(x_T2, g + 1)
                lo, hi = halves(xs, g * GB, GB)
                A(lo, ps[0:64, 7, :].rearrange("p (b n) -> p b n", b=GB), ACT.Copy).then_inc(x_out, 1)
                A(hi, ps[64:128, 7, :].rearrange("p (b n) -> p b n", b=GB), ACT.Copy).then_inc(x_out, 1)

            def probs_T(g):
                act.wait_ge(x_pT_ps, g + 1)
                A(xpT[:].rearrange("p b n -> p (b n)"), ps[0:NC, 6, :], ACT.Copy).then_inc(x_pT, 1)

            def context_affine(g):
                act.wait_ge(x_zT, 2 * g + 2)
                A(c1T[:].rearrange("p b n -> p (b n)"), ps[0:DC, 1, 0:GB * NC], ACT.Identity, scale=cols[0:DC, 2:3],
                  bias=cols[0:DC, 3:4]).then_inc(x_c1T, 1)

            def k_out(g):
                act.wait_ge(x_k_ps, g + 1)
                A(xkT[:].rearrange("p b n -> p (b n)"), ps[:, 3, 0:GB * NC], ACT.Identity, bias=cols[:, 5:6]).then_inc(x_k, 1)

            def first(g):
                norms(g)
                act.wait_ge(ld_cols, 16 * 6)
                context_affine(g)
                q_out(g)
                norms(g + 1)
                k_out(g)
                exps(g)
                act.wait_ge(ld_wqkv, 16)
                A(wqkv_hi[:], wqkv_raw[:].rearrange("p l n -> p (l n)"), ACT.Copy).then_inc(wsplit, 1)

            def both(g, more):
                probs_T(g)
                context_affine(g + 1)
                mixed(g)
                q_out(g + 1)
                k_out(g + 1)
                if more:
                    norms(g + 2)
                norm_out(g)
                exps(g + 1)
                results(g)

            def last_group(g):
                probs_T(g)
                squares(Batch(0, 0, 0), 0)
                squares(Batch(0, 0, 0), 1)
                mixed(g)
                norms_ln(Batch(0, 0, 0))
                norms_exp(Batch(0, 0, 0))
                norm_out(g)

            groups(act, first, both, last_group)

            def step(at, on):
                if on(-2):
                    m = at(-2)
                    j = m.j
                    act.wait_ge(var_ps[j], m.g + 1)
                    A(lnl[j][:], ps[:, S0, VAR], ACT.Ln, bias=epst[:]).then_inc(lnl_done[j], 1)
                if on(1):
                    m = at(1)
                    j = m.j
                    act.wait_ge(v_ps[j], m.g + 1)
                    A(vv[j][:], ps[:, VB, :], ACT.Copy).then_inc(v_ready[j], 1)
                if on(-2):
                    m = at(-2)
                    j = m.j
                    act.wait_ge(lnl_done[j], m.g + 1)
                    A(rstd[j][:], lnl[j][:], ACT.Exp, scale=-0.5).then_inc(rstd_ready[j], 1)
                if on(0):
                    m = at(0)
                    j = m.j
                    act.wait_ge(pt_ps[j], 2 * m.g + 1)
                    A(pT1[j][:].rearrange("p c n -> p (c n)"), ps[:, TQ, :], ACT.Copy).then_inc(pt_ready[j], 1)
                    act.wait_ge(pt_ps[j], 2 * m.g + 2)
                    for u in range(2):
                        A(pT0[j][:, u, :, :].rearrange("p c n -> p (c n)"), ps[u * W:(u + 1) * W, TK, 0:256],
                          ACT.Copy).then_inc(pt_ready[j], 1)
                if on(1):
                    m = at(1)
                    j = m.j
                    for c in range(PAIRS):
                        act.wait_ge(sm_ready[j], 8 * m.g + c + 1)
                        A(p1[j][:, c, :], sm1[j][:, c, :], ACT.Exp, bias=nm[j][:, c:c + 1], scale=-1.0,
                          accum_out=psum_[j][:, c:c + 1]).then_inc(p_done[j], 1)
                if on(3):
                    squares(at(3), 0)
                if on(3):
                    squares(at(3), 1)
                if on(1):
                    m = at(1)
                    j = m.j
                    for c in range(PAIRS):
                        act.wait_ge(sm_ready[j], 8 * m.g + 4 + c + 1)
                        A(p0[j][:, c, :], sm0[j][:, c, :], ACT.Exp, bias=nm[j][:, 4 + c:5 + c], scale=-1.0,
                          accum_out=psum_[j][:, 4 + c:5 + c]).then_inc(p_done[j], 1)
                if on(0):
                    m = at(0)
                    j = m.j
                    act.wait_ge(o_ps[j], m.g + 1)
                    A(oT[j][:].rearrange("p c n -> p (c n)"), ps[:, OB, :], ACT.Copy).then_inc(oT_ready[j], 1)
                if on(3):
                    norms_ln(at(3))
                if on(3):
                    norms_exp(at(3))
                if on(2):
                    m = at(2)
                    j = m.j
                    act.wait_ge(rT_ps[j], 2 * m.g + 1)
                    A(qT[j][:].rearrange("p c n -> p (c n)"), ps[:, TQ, :], ACT.Copy).then_inc(qT_ready[j], 1)
                    act.wait_ge(rT_ps[j], 2 * m.g + 2)
                    A(kT[j][:].rearrange("p c n -> p (c n)"), ps[:, TK, :], ACT.Copy).then_inc(kT_ready[j], 1)

            def unshifted(g):
                j = g % 2
                lo, hi = halves(xs, g * GB, GB)
                if g >= 2:
                    act.wait_ge(st_T[j], g // 2)
                act.wait_ge(f_upd, 2 * NG * (DEPTH - 1) + 2 * g + 3)
                A(stg[j][0:64, :, :], lo, ACT.Copy).then_inc(st_ready[j], 1)
                act.wait_ge(f_upd, 2 * NG * (DEPTH - 1) + 2 * g + 4)
                A(stg[j][64:128, :, :], hi, ACT.Copy).then_inc(st_ready[j], 1)

            for layer in range(DEPTH):
                pipeline(act, layer, step, before={-1: lambda: results(NG - 1)} if layer == 0 else {})

                nc.scalar.preload_act_table_set("gelu_and_others")

                def chunk(gl_, c):
                    o, m = CH[c]
                    act.wait_ge(g_ps[c], gl_ + 1)
                    A(gl[0:m, c, :], ps[0:m, 2 * c + 1, :], ACT.Gelu, bias=b1_l[0:m, 3 + c:4 + c]).then_inc(gl_ready[c], 1)

                def split(gl_, c):
                    o, m = CH[c]
                    act.wait_ge(u_ready[c], gl_ + 1)
                    A(u_hi[0:m, c, :], uu[0:m, c, :], ACT.Copy).then_inc(uh_ready[c], 1)

                act.wait_ge(layer_w, 9 * layer + 9)
                chunk(layer * NG, 0)
                chunk(layer * NG, 1)
                split(layer * NG, 0)
                split(layer * NG, 1)
                with act.Fori(0, NG - 1) as g:
                    gl_ = layer * NG + g
                    chunk(gl_, 2)
                    chunk(gl_ + 1, 0)
                    split(gl_, 2)
                    act.wait_ge(f_acc[0], gl_ + 1)
                    split(gl_ + 1, 0)
                    chunk(gl_ + 1, 1)
                    split(gl_ + 1, 1)
                gl_ = layer * NG + NG - 1
                chunk(gl_, 2)
                if layer + 1 == DEPTH:
                    unshifted(0)
                else:
                    nc.scalar.preload_act_table_set("natural_log_exp_and_others")
                split(gl_, 2)
                if layer + 1 < DEPTH:
                    m = Batch(layer + 1, 0, 0)
                    squares(m, 0)
                    squares(m, 1)
                    norms_ln(m)
                    norms_exp(m)
            for g in range(1, NG):
                unshifted(g)

        @block.vector
        def _(dve):
            V = nc.vector
            V.memset(ones[:], 1.0 / D).then_inc(cst_v, 1)
            V.memset(epst[:], EPS).then_inc(cst_v, 1)
            V.memset(mark_v[:, 7:8], 0.0).then_inc(f_upd, 2)
            V.memset(backt[:], LN_BACK).then_inc(cst_v, 1)
            V.memset(xs[64:128, :, 0:1], 0.0).then_inc(cst_v, 1)
            V.memset(eps2t[:], EPS * EPS).then_inc(cst_v, 1)

            def row(t, b):
                return t[:, bass.ds(b, 1), :].rearrange("p o d -> p (o d)")

            def head_in(m):
                j = m.j
                V.tensor_copy(h_hi[j][:], h_of(m.b)).then_inc(h_hi_ok[j], 1)
                dve.wait_ge(h_hi_ok[j], m.g + 1)
                V.tensor_tensor(h_lo[j][:], h_of(m.b), h_hi[j][:].bitcast(F32), ALU.subtract).then_inc(h_ready[j], 1)

            def squared_norms(m):
                dve.wait_ge(sq_done[m.j], 2 * m.g + 2)
                V.tensor_reduce(ss[m.j][:], sqr[m.j][:].rearrange("p (h d) -> p h d", d=DH), AX.X, ALU.add).then_inc(ss_sum[m.j], 1)
                dve.wait_ge(ss_sum[m.j], m.g + 1)
                V.tensor_scalar(ssc[m.j][:], ss[m.j][:], 1e-24, None, ALU.max).then_inc(ss_ready[m.j], 1)

            def over_norms(m):
                dve.wait_ge(r_ready[m.j], m.g + 1)
                V.tensor_tensor(qn[m.j].rearrange("p (h d) -> p h d", d=DH), ps[:, QB:KB + 1, :].rearrange("p s (h d) -> p (s h) d", d=DH),
                                rr[m.j][:].unsqueeze(2).to_broadcast([128, 2 * HEADS, DH]), ALU.mult).then_inc(qn_ready[m.j], 1)

            def stats(g):
                for i in range(GB):
                    V.bn_stats(bst[:, i, :], row(xt, g * GB + i)).then_inc(x_st, 1)
                    V.bn_stats(cst[0:NC, i, :], row(ct, g * GB + i)).then_inc(x_st, 1)
                apart(V, x_st, 16 * g + 8, 2)
                for i in range(GB):
                    V.bn_aggr(mv[:, i, :], bst[:, i, :]).then_inc(x_st, 1)
                    V.bn_aggr(cmv[0:NC, i, :], cst[0:NC, i, :]).then_inc(x_st, 1)

            def normed(g):
                dve.wait_ge(x_st, 16 * g + 16)
                dve.wait_ge(x_rs, 4 * g + 4)
                for i in range(GB):
                    V.tensor_scalar(zx[:, i, :], row(xt, g * GB + i), mv[:, i, 0:1], r1[:, i:i + 1],
                                    ALU.subtract, ALU.mult).then_inc(x_z, 1)
                for i in range(GB):
                    V.tensor_scalar(zc[:, i, :], row(ct, g * GB + i), cmv[0:NC, i, 0:1], rc[0:NC, i:i + 1],
                                    ALU.subtract, ALU.mult).then_inc(x_z, 1)

            def affine(g):
                dve.wait_ge(x_zT, 2 * g + 1)
                V.tensor_scalar(x1T[:], ps[:, 0, :], cols[:, 0:1], cols[:, 1:2], ALU.mult, ALU.add).then_inc(x_1T, 1)

            def v_out(g):
                dve.wait_ge(x_v_ps, g + 1)
                V.tensor_tensor(xv[:], ps[0:NC, 4, :].rearrange("p (b d) -> p b d", b=GB),
                                bvb[0:NC, :].unsqueeze(1).to_broadcast([NC, GB, D]), ALU.add).then_inc(x_v, 1)

            def maxima(g):
                dve.wait_ge(x_s, g + 1)
                V.tensor_reduce(nmx[:], ps[:, 5, 0:GB * NC].rearrange("p (b n) -> p b n", b=GB), AX.X, ALU.max).then_inc(x_nm, 1)
                dve.wait_ge(x_nm, 2 * g + 1)
                V.tensor_scalar(nmb[:], nmx[:], -float(D) ** -0.5, None, ALU.mult).then_inc(x_nm, 1)

            def sums(g):
                dve.wait_ge(x_p, GB * g + GB)
                V.reciprocal(xri[:], xsum[:]).then_inc(x_ri, 1)
                dve.wait_ge(x_ri, 2 * g + 1)
                V.tensor_scalar(xrt[:], xri[:], tg[:, 0:1], None, ALU.mult).then_inc(x_ri, 1)

            def residual(g):
                dve.wait_ge(x_ri, 2 * g + 2)
                dve.wait_ge(cst_g, g + 1)
                dve.wait_ge(x_y_ps, g + 1)
                for i in range(GB):
                    V.scalar_tensor_tensor(out=row(xt, g * GB + i), in0=ps[:, 7, i * D:(i + 1) * D], scalar=xrt[:, i:i + 1],
                                           in1=row(xt, g * GB + i), op0=ALU.mult, op1=ALU.add).then_inc(x_res, 1)
                apart(V, x_res, GB * g + GB, 3)
                for i in range(GB):
                    V.bn_stats(bst2[:, i, :], row(xt, g * GB + i)).then_inc(x_st2, 1)
                apart(V, x_st2, 2 * GB * g + GB, 4)
                for i in range(GB):
                    V.bn_aggr(mv2[:, i, :], bst2[:, i, :]).then_inc(x_st2, 1)

            def stack_in(g):
                dve.wait_ge(x_st2, 2 * GB * g + 2 * GB)
                dve.wait_ge(x_rs2, 2 * g + 2)
                for i in range(GB):
                    V.tensor_scalar(zo[:, i, :], row(xt, g * GB + i), mv2[:, i, 0:1], r2[:, i:i + 1],
                                    ALU.subtract, ALU.mult).then_inc(x_z2, 1)

            def first(g):
                dve.wait_ge(ld_x0, 16)
                dve.wait_ge(ld_c0, 16 * 3)
                stats(g)
                normed(g)
                dve.wait_ge(ld_cols, 16 * 6)
                affine(g)
                dve.wait_ge(ld_x1, 16 * 2)
                stats(g + 1)
                dve.wait_ge(ld_bg, 16 * 2)
                v_out(g)
                maxima(g)
                dve.wait_ge(ld_x, 16)
                dve.wait_ge(ld_c, 16)

            def both(g, more):
                normed(g + 1)
                affine(g + 1)
                sums(g)
                if more:
                    stats(g + 2)
                residual(g)
                v_out(g + 1)
                maxima(g + 1)
                stack_in(g)

            def last_group(g):
                m = Batch(0, 0, 0)
                dve.wait_ge(x_out, 2)
                head_in(m)
                head_in(Batch(0, 0, 1))
                sums(g)
                squared_norms(m)
                residual(g)
                over_norms(m)
                stack_in(g)

            groups(dve, first, both, last_group)

            dve.wait_ge(ld_b1, 16 * 12)
            dve.wait_ge(b1_ps, 1)
            for c, (o, m) in enumerate(CH):
                V.tensor_tensor(b1_all[0:m, :, c::3], ps[0:m, 3, 0:12].rearrange("p (l s c) -> p l s c", l=2, s=2)[:, :, :, c],
                                b1_raw[0:m, :, c::3], ALU.add).then_inc(b1_done, 1)

            def cosine(m, s):
                part = slice(s * INNER, (s + 1) * INNER)
                V.tensor_tensor(rc1[m.j][:, part].rearrange("p (h d) -> p h d", h=HEADS),
                                qn[m.j][:, part].rearrange("p (h d) -> p h d", h=HEADS),
                                ctab[:, bass.ds(m.layer, 1), s, :].to_broadcast([128, HEADS, DH]), ALU.mult).then_inc(c_ready[m.j], 1)

            def w1_in(layer):
                V.tensor_scalar(w1g[:], w1_raw[:, layer, :], lgb[:, 0, layer:layer + 1], None, ALU.mult).then_inc(layer_w1, 1)
                dve.wait_ge(layer_w1, 3 * layer + 1)
                V.tensor_copy(w1_hi[:], w1g[:]).then_inc(layer_w1, 1)
                dve.wait_ge(layer_w1, 3 * layer + 2)
                V.tensor_tensor(w1_lo[:], w1g[:], w1_hi[:].bitcast(F32), ALU.subtract).then_inc(layer_w1, 1)

            def step(at, on):
                if on(-1):
                    m = at(-1)
                    j = m.j
                    dve.wait_ge(y_ps[j], m.g + 1)
                    for t, q in zip(halves(xs, m.b, 1), (0, 64)):
                        t = t.rearrange("p o n -> p (o n)")
                        V.tensor_tensor(t, ps[q:q + 64, OB, 0:N], t, ALU.add).then_inc(x_upd[j], 1)
                if on(3) and on(1):
                    dve.wait_ge(v_ps[at(1).j], at(1).g + 1)
                    head_in(at(3))
                if on(2):
                    m = at(2)
                    dve.wait_ge(qn_ready[m.j], m.g + 1)
                    cosine(m, 0)
                if on(1):
                    m = at(1)
                    j = m.j
                    apart(V, s_ps[j], 2 * m.g + 1, 0)
                    for c in range(PAIRS):
                        V.tensor_tensor_reduce(out=sm1[j][:, c, :], in0=ps[:, S1, c * 128:(c + 1) * 128], in1=msk[:, 0:128],
                                               scale=-1.0, scalar=3e38, op0=ALU.add, op1=ALU.min,
                                               accum_out=nm[j][:, c:c + 1]).then_inc(sm_ready[j], 1)
                    apart(V, s_ps[j], 2 * m.g + 2, 1)
                    for c in range(PAIRS):
                        V.tensor_tensor_reduce(out=sm0[j][:, c, :], in0=ps[:, S0, c * W:(c + 1) * W], in1=msk[:, 128:192],
                                               scale=-1.0, scalar=3e38, op0=ALU.add, op1=ALU.min,
                                               accum_out=nm[j][:, 4 + c:5 + c]).then_inc(sm_ready[j], 1)
                if on(2):
                    m = at(2)
                    cosine(m, 1)
                if on(-2):
                    m = at(-2)
                    j = m.j
                    dve.wait_ge(rstd_ready[j], m.g + 1)
                    V.tensor_tensor(hnf[j][:], dd[j][:], rstd[j][:], ALU.mult).then_inc(hnf_ready[j], 1)
                if on(-1):
                    m = at(-1)
                    j = m.j
                    dve.wait_ge(m_ps[j], m.g + 1)
                    V.tensor_tensor(dd[j][:], h_of(m.b), ps[:, S0, MEAN], ALU.subtract).then_inc(d_ready[j], 1)
                    dve.wait_ge(d_ready[j], m.g + 1)
                    V.tensor_tensor(dsq[j][:], dd[j][:], dd[j][:], ALU.mult).then_inc(d2_ready[j], 1)
                if on(3):
                    squared_norms(at(3))
                elif on(2):
                    w1_in(at(2).layer)
                if on(1):
                    m = at(1)
                    j = m.j
                    dve.wait_ge(p_done[j], 8 * m.g + 8)
                    V.reciprocal(pri[j][:], psum_[j][:]).then_inc(ri_ready[j], 1)
                if on(-2):
                    m = at(-2)
                    j = m.j
                    hh = hn_hi[:, bass.ds(m.b, 1), :].rearrange("p o n -> p (o n)")
                    hl = hn_lo[:, bass.ds(m.b, 1), :].rearrange("p o n -> p (o n)")
                    dve.wait_ge(hnf_ready[j], m.g + 1)
                    V.tensor_copy(hh, hnf[j][:]).then_inc(hh_ready[j], 1)
                    dve.wait_ge(hh_ready[j], m.g + 1)
                    V.tensor_tensor(hl, hnf[j][:], hh.bitcast(F32), ALU.subtract).then_inc(hn_ready[j], 1)

                if on(3):
                    over_norms(at(3))

            dve.wait_ge(ld_small, 16 * 4)
            dve.wait_ge(tab_done, 6)
            def result(g):
                j = g % 2
                dve.wait_ge(st_T[j], g // 2 + 1)
                V.scalar_tensor_tensor(out=ot[g][:].rearrange("p b n -> p (b n)"), in0=ps[:, j, :], scalar=tg[:, 1:2],
                                       in1=xt[:, g * GB:(g + 1) * GB, :].rearrange("p b n -> p (b n)"),
                                       op0=ALU.mult, op1=ALU.add).then_inc(ot_ready[j], 1)

            for layer in range(DEPTH):
                pipeline(dve, layer, step, before={0: lambda: dve.wait_ge(x_out, 2 * NG)})

                def gate(gl_, c):
                    o, m = CH[c]
                    dve.wait_ge(gl_ready[c], gl_ + 1)
                    V.scalar_tensor_tensor(out=uu[0:m, c, :], in0=ps[0:m, 2 * c, :], scalar=b1_l[0:m, c:c + 1], in1=gl[0:m, c, :],
                                           op0=ALU.add, op1=ALU.mult).then_inc(u_ready[c], 1)

                def low(gl_, c):
                    o, m = CH[c]
                    dve.wait_ge(uh_ready[c], gl_ + 1)
                    V.tensor_tensor(u_lo[0:m, c, :], uu[0:m, c, :], u_hi[0:m, c, :].bitcast(F32), ALU.subtract).then_inc(ul_ready[c], 1)

                def update(g, gl_, bank=FB):
                    dve.wait_ge(f_acc[2], gl_ + 1)
                    for t, q in zip(halves(xs, g * GB, GB), (0, 64)):
                        V.scalar_tensor_tensor(out=t, in0=ps[q:q + 64, bank, :].rearrange("p (b n) -> p b n", b=GB),
                                               scalar=b2_l[q:q + 64, :], in1=t, op0=ALU.add, op1=ALU.add).then_inc(f_upd, 1)

                dve.wait_ge(layer_w, 9 * layer + 9)
                gate(layer * NG, 0)
                gate(layer * NG, 1)
                low(layer * NG, 0)
                low(layer * NG, 1)
                with dve.Fori(0, NG - 1) as g:
                    gl_ = layer * NG + g
                    gate(gl_, 2)
                    dve.wait_ge(ul_ready[0], gl_ + 1)
                    gate(gl_ + 1, 0)
                    low(gl_, 2)
                    gate(gl_ + 1, 1)
                    update(g, gl_)
                    low(gl_ + 1, 1)
                gl_ = layer * NG + NG - 1
                if layer + 1 < DEPTH:
                    dve.wait_ge(f_upd, 2 * NG * layer + 4)
                    head_in(Batch(layer + 1, 0, 0))
                gate(gl_, 2)
                if layer + 1 < DEPTH:
                    head_in(Batch(layer + 1, 0, 1))
                low(gl_, 2)
                if layer + 1 == DEPTH:
                    result(0)
                update(NG - 1, gl_, FB_LAST)
                dve.wait_ge(f_upd, 2 * NG * layer + 2 * NG + 2)
                if layer + 1 < DEPTH:
                    squared_norms(Batch(layer + 1, 0, 0))
                    over_norms(Batch(layer + 1, 0, 0))
            for g in range(1, NG):
                result(g)


_INS = ["x", "ctx_768", "g_xattn", "g_ffn"] + ["L0_xattn_" + n for n in (
    "ln1_g", "ln1_b", "ln2_g", "ln2_b", "Wq", "bq", "Wk", "bk", "Wv", "bv", "Wo", "bo")] + ["L0_ffn_" + n for n in (
    "wqkv", "q_scale", "k_scale", "wo", "ln_g", "ln_b", "w1", "b1", "w2", "b2")]


def kernel(**inputs):
    import concourse.bacc as _bacc
    from concourse.bass_utils import run_bass_kernel_spmd as _run

    nc = _bacc.Bacc("TRN2", target_bir_lowering=False, num_devices=1)
    given = {n: np.ascontiguousarray(inputs[n]) for n in _INS}
    given |= dict(zip(("rot_table", "window_masks", "identity"), tables()))
    arrays, args = {}, []
    for name, a in given.items():
        arrays[f"in_{name}_dram"] = a
        args.append(nc.dram_tensor(f"in_{name}_dram", a.shape, mybir.dt.from_np(a.dtype), kind="ExternalInput").ap())
    args.append(nc.dram_tensor("out_0_dram", (B, N, D), F32, kind="ExternalOutput").ap())
    build(nc, *args)
    r = _run(nc, [arrays], core_ids=[0])
    return r.results[0]["out_0_dram"]
```
